# Optimizing a Trainium2 kernel written in Bass

```python
import numpy as np
import jax
import jax.numpy as jnp

def _softmax(x, axis=-1):
    return jax.nn.softmax(x, axis=axis)

def _gelu(x):
    return jax.nn.gelu(x, approximate=True)

def _silu(x):
    return jax.nn.silu(x)

def _sigmoid(x):
    return jax.nn.sigmoid(x)

def _layernorm(x, axis=-1, eps=1e-05):
    m = jnp.mean(x, axis=axis, keepdims=True)
    v = jnp.var(x, axis=axis, keepdims=True)
    return (x - m) / jnp.sqrt(v + eps)

def _scatter_add(tgt, idx, src, axis=0):
    return tgt.at[idx].add(src)

def _segment_sum(src, seg, n):
    return jax.ops.segment_sum(src, seg, n)
kernel_name = 'mk_hybrid_d1_jaxref_r8_8fcdaa'

def setup_inputs(seed: int=0):
    np.random.seed(seed)
    _w = jnp.asarray

    def _L0_attn_a_setup():
        import jax, jax.numpy as jnp
        import numpy as np
        FP32_EPS = 1.1920929e-07

        def rms_norm(x):
            return x * jax.lax.rsqrt(jnp.mean(x * x, axis=-1, keepdims=True) + FP32_EPS)
        key = jax.random.key(seed)
        k1, k2, k3, k4 = jax.random.split(key, 4)
        n_embd, n_qkv = (128, 128)
        B, T = (4, 1024)

        def casted_init(k, out_f, in_f):
            s = 3.0 ** 0.5 * in_f ** (-0.5)
            return jax.random.uniform(k, (out_f, in_f), jnp.float32, -s, s)
        return {'x': jax.random.normal(k1, (B, T, n_embd), jnp.float32), 'w_qkv': casted_init(k2, 3 * n_qkv, n_embd), 'w_swiglu': casted_init(k3, 2 * n_embd, n_qkv), 'w_out': casted_init(k4, n_embd, n_embd)}
    _L0_attn_a_in = _L0_attn_a_setup()

    def _L0_attn_b_setup():
        import jax, jax.numpy as jnp
        import numpy as np
        import math
        EMBED = 128
        HEADS = 16
        HEAD_DIM = EMBED // HEADS
        B, N = (2, 256)
        key = jax.random.key(seed)
        ks = jax.random.split(key, 8)
        s = 1.0 / math.sqrt(EMBED)
        Wq = jax.random.uniform(ks[0], (EMBED, EMBED), jnp.float32, -s, s)
        bq = jax.random.uniform(ks[1], (EMBED,), jnp.float32, -s, s)
        Wk = jax.random.uniform(ks[2], (EMBED, EMBED), jnp.float32, -s, s)
        bk = jax.random.uniform(ks[3], (EMBED,), jnp.float32, -s, s)
        Wv = jax.random.uniform(ks[4], (EMBED, EMBED), jnp.float32, -s, s)
        bv = jax.random.uniform(ks[5], (EMBED,), jnp.float32, -s, s)
        Wp = jax.random.normal(ks[6], (HEAD_DIM, HEAD_DIM), jnp.float32)
        x = jax.random.normal(ks[7], (B, N, EMBED), jnp.float32)
        return {'x': x, 'Wq': Wq, 'bq': bq, 'Wk': Wk, 'bk': bk, 'Wv': Wv, 'bv': bv, 'Wp': Wp}
    _L0_attn_b_in = _L0_attn_b_setup()

    def _L0_ffn_setup():
        import jax, jax.numpy as jnp
        import numpy as np
        B, S, D, H, L, E, K = (4, 128, 128, 16, 2, 8, 2)
        DFF = 4 * D

        def _ln(x, w, b):
            m = x.mean(-1, keepdims=True)
            v = x.var(-1, keepdims=True)
            return (x - m) / jnp.sqrt(v + 1e-05) * w + b

        def _attn(x, wq, wk, wv, wo, bq, bk, bv, bo):
            Bb, T, C = x.shape
            hd = C // H
            q = (x @ wq + bq).reshape(Bb, T, H, hd).transpose(0, 2, 1, 3)
            k = (x @ wk + bk).reshape(Bb, T, H, hd).transpose(0, 2, 1, 3)
            v = (x @ wv + bv).reshape(Bb, T, H, hd).transpose(0, 2, 1, 3)
            att = jnp.einsum('bhqd,bhkd->bhqk', q, k) * hd ** (-0.5)
            causal = jnp.tril(jnp.ones((T, T), bool))
            att = jnp.where(causal, att, -jnp.inf)
            att = jax.nn.softmax(att, axis=-1)
            y = jnp.einsum('bhqk,bhkd->bhqd', att, v).transpose(0, 2, 1, 3).reshape(Bb, T, C)
            return y @ wo + bo

        def _ffn(h, w1, b1, w2, b2):
            return jax.nn.gelu(h @ w1 + b1, approximate=False) @ w2 + b2

        def _combine_weights(logits):
            vals, idx = jax.lax.top_k(logits, K)
            w = jax.nn.softmax(vals, axis=-1)
            onehot = (idx[..., None] == jnp.arange(E)).astype(w.dtype)
            return jnp.sum(w[..., None] * onehot, axis=-2)

        def _token_moe(h, gw, gb, w1, b1, w2, b2):
            cw = _combine_weights(h @ gw + gb)
            out = jnp.zeros_like(h)
            for e in range(E):
                out = out + _ffn(h, w1[e], b1[e], w2[e], b2[e]) * cw[..., e:e + 1]
            return out

        def _seq_moe(h, gw, gb, w1, b1, w2, b2):
            cw = _combine_weights(h.mean(axis=1) @ gw + gb)
            out = jnp.zeros_like(h)
            for e in range(E):
                out = out + _ffn(h, w1[e], b1[e], w2[e], b2[e]) * cw[:, e, None, None]
            return out
        key = jax.random.key(seed)
        ks = jax.random.split(key, 9)
        n = lambda k, shp: jax.random.normal(k, shp, dtype=jnp.float32) * 0.02
        return {'x': jax.random.normal(ks[0], (B, S, D), dtype=jnp.float32), 'ln1_w': jnp.ones((L, D), jnp.float32), 'ln1_b': jnp.zeros((L, D), jnp.float32), 'ln2_w': jnp.ones((L, D), jnp.float32), 'ln2_b': jnp.zeros((L, D), jnp.float32), 'wq': n(ks[1], (L, D, D)), 'wk': n(ks[2], (L, D, D)), 'wv': n(ks[3], (L, D, D)), 'wo': n(ks[4], (L, D, D)), 'bq': jnp.zeros((L, D), jnp.float32), 'bk': jnp.zeros((L, D), jnp.float32), 'bv': jnp.zeros((L, D), jnp.float32), 'bo': jnp.zeros((L, D), jnp.float32), 'gate_w': n(ks[5], (L, D, E)), 'gate_b': jnp.zeros((L, E), jnp.float32), 'e_w1': n(ks[6], (L, E, D, DFF)), 'e_b1': jnp.zeros((L, E, DFF), jnp.float32), 'e_w2': n(ks[7], (L, E, DFF, D)), 'e_b2': jnp.zeros((L, E, D), jnp.float32)}
    _L0_ffn_in = _L0_ffn_setup()
    _d = {'L0_attn_a_x': _L0_attn_a_in['x'], 'L0_attn_a_w_qkv': _L0_attn_a_in['w_qkv'], 'L0_attn_a_w_swiglu': _L0_attn_a_in['w_swiglu'], 'L0_attn_a_w_out': _L0_attn_a_in['w_out'], 'L0_attn_b_Wq': _L0_attn_b_in['Wq'], 'L0_attn_b_bq': _L0_attn_b_in['bq'], 'L0_attn_b_Wk': _L0_attn_b_in['Wk'], 'L0_attn_b_bk': _L0_attn_b_in['bk'], 'L0_attn_b_Wv': _L0_attn_b_in['Wv'], 'L0_attn_b_bv': _L0_attn_b_in['bv'], 'L0_attn_b_Wp': _L0_attn_b_in['Wp'], 'L0_ffn_ln1_w': _L0_ffn_in['ln1_w'], 'L0_ffn_ln1_b': _L0_ffn_in['ln1_b'], 'L0_ffn_ln2_w': _L0_ffn_in['ln2_w'], 'L0_ffn_ln2_b': _L0_ffn_in['ln2_b'], 'L0_ffn_wq': _L0_ffn_in['wq'], 'L0_ffn_wk': _L0_ffn_in['wk'], 'L0_ffn_wv': _L0_ffn_in['wv'], 'L0_ffn_wo': _L0_ffn_in['wo'], 'L0_ffn_bq': _L0_ffn_in['bq'], 'L0_ffn_bk': _L0_ffn_in['bk'], 'L0_ffn_bv': _L0_ffn_in['bv'], 'L0_ffn_bo': _L0_ffn_in['bo'], 'L0_ffn_gate_w': _L0_ffn_in['gate_w'], 'L0_ffn_gate_b': _L0_ffn_in['gate_b'], 'L0_ffn_e_w1': _L0_ffn_in['e_w1'], 'L0_ffn_e_b1': _L0_ffn_in['e_b1'], 'L0_ffn_e_w2': _L0_ffn_in['e_w2'], 'L0_ffn_e_b2': _L0_ffn_in['e_b2']}
    _x0 = _d['L0_attn_a_x']
    _d['L0_attn_a_x'] = jax.random.normal(jax.random.fold_in(jax.random.key(seed), 1), (1, 2048, 128), dtype=_x0.dtype)
    del _x0
    return _d

def reference(L0_attn_a_x, L0_attn_a_w_qkv, L0_attn_a_w_swiglu, L0_attn_a_w_out, L0_attn_b_Wq, L0_attn_b_bq, L0_attn_b_Wk, L0_attn_b_bk, L0_attn_b_Wv, L0_attn_b_bv, L0_attn_b_Wp, L0_ffn_ln1_w, L0_ffn_ln1_b, L0_ffn_ln2_w, L0_ffn_ln2_b, L0_ffn_wq, L0_ffn_wk, L0_ffn_wv, L0_ffn_wo, L0_ffn_bq, L0_ffn_bk, L0_ffn_bv, L0_ffn_bo, L0_ffn_gate_w, L0_ffn_gate_b, L0_ffn_e_w1, L0_ffn_e_b1, L0_ffn_e_w2, L0_ffn_e_b2):

    def _L0_attn_a_ref(x, w_qkv, w_swiglu, w_out):
        import jax, jax.numpy as jnp
        import numpy as np
        FP32_EPS = 1.1920929e-07

        def rms_norm(x):
            return x * jax.lax.rsqrt(jnp.mean(x * x, axis=-1, keepdims=True) + FP32_EPS)
        qkv = jnp.einsum('btd,ed->bte', rms_norm(x), w_qkv)
        q, k, v = jnp.split(qkv, 3, axis=-1)
        q = rms_norm(q)
        k = rms_norm(k)
        w = jnp.exp(k)
        kv = w * v
        w = jnp.cumsum(w, axis=1)
        kv = jnp.cumsum(kv, axis=1)
        y = kv / (w + 1e-06)
        y = jax.nn.sigmoid(q) * y
        uv = jnp.einsum('bte,fe->btf', y, w_swiglu)
        u, g = jnp.split(uv, 2, axis=-1)
        return x + jnp.einsum('btd,ed->bte', u * jax.nn.silu(g), w_out)

    def _L0_attn_b_ref(x, Wq, bq, Wk, bk, Wv, bv, Wp):
        import jax, jax.numpy as jnp
        import numpy as np
        import math
        EMBED = 128
        HEADS = 16
        HEAD_DIM = EMBED // HEADS
        B, N = (2, 256)
        Bb, Nn, E = x.shape
        H, D = (HEADS, HEAD_DIM)
        q = (x @ Wq + bq).reshape(Bb, Nn, H, D)
        k = (x @ Wk + bk).reshape(Bb, Nn, H, D)
        v = (x @ Wv + bv).reshape(Bb, Nn, H, D)
        q = jnp.einsum('bnhe,ei->bnhi', q, Wp)
        k = jnp.einsum('bnhe,ei->bnhi', k, Wp)
        scores = jnp.einsum('bnhi,bmhi->bnhm', q, k) / math.sqrt(D)
        attn = jax.nn.softmax(scores, axis=-1)
        out = jnp.einsum('bnhm,bmhe->bnhe', attn, v).reshape(Bb, Nn, E)
        return out

    def _L0_ffn_ref(x, ln1_w, ln1_b, ln2_w, ln2_b, wq, wk, wv, wo, bq, bk, bv, bo, gate_w, gate_b, e_w1, e_b1, e_w2, e_b2):
        import jax, jax.numpy as jnp
        import numpy as np
        B, S, D, H, L, E, K = (4, 128, 128, 16, 2, 8, 2)
        DFF = 4 * D

        def _ln(x, w, b):
            m = x.mean(-1, keepdims=True)
            v = x.var(-1, keepdims=True)
            return (x - m) / jnp.sqrt(v + 1e-05) * w + b

        def _attn(x, wq, wk, wv, wo, bq, bk, bv, bo):
            Bb, T, C = x.shape
            hd = C // H
            q = (x @ wq + bq).reshape(Bb, T, H, hd).transpose(0, 2, 1, 3)
            k = (x @ wk + bk).reshape(Bb, T, H, hd).transpose(0, 2, 1, 3)
            v = (x @ wv + bv).reshape(Bb, T, H, hd).transpose(0, 2, 1, 3)
            att = jnp.einsum('bhqd,bhkd->bhqk', q, k) * hd ** (-0.5)
            causal = jnp.tril(jnp.ones((T, T), bool))
            att = jnp.where(causal, att, -jnp.inf)
            att = jax.nn.softmax(att, axis=-1)
            y = jnp.einsum('bhqk,bhkd->bhqd', att, v).transpose(0, 2, 1, 3).reshape(Bb, T, C)
            return y @ wo + bo

        def _ffn(h, w1, b1, w2, b2):
            return jax.nn.gelu(h @ w1 + b1, approximate=False) @ w2 + b2

        def _combine_weights(logits):
            vals, idx = jax.lax.top_k(logits, K)
            w = jax.nn.softmax(vals, axis=-1)
            onehot = (idx[..., None] == jnp.arange(E)).astype(w.dtype)
            return jnp.sum(w[..., None] * onehot, axis=-2)

        def _token_moe(h, gw, gb, w1, b1, w2, b2):
            cw = _combine_weights(h @ gw + gb)
            out = jnp.zeros_like(h)
            for e in range(E):
                out = out + _ffn(h, w1[e], b1[e], w2[e], b2[e]) * cw[..., e:e + 1]
            return out

        def _seq_moe(h, gw, gb, w1, b1, w2, b2):
            cw = _combine_weights(h.mean(axis=1) @ gw + gb)
            out = jnp.zeros_like(h)
            for e in range(E):
                out = out + _ffn(h, w1[e], b1[e], w2[e], b2[e]) * cw[:, e, None, None]
            return out
        for l in range(L):
            x = x + _attn(_ln(x, ln1_w[l], ln1_b[l]), wq[l], wk[l], wv[l], wo[l], bq[l], bk[l], bv[l], bo[l])
            h = _ln(x, ln2_w[l], ln2_b[l])
            moe = _token_moe if l % 2 == 0 else _seq_moe
            x = x + moe(h, gate_w[l], gate_b[l], e_w1[l], e_b1[l], e_w2[l], e_b2[l])
        return x
    x = L0_attn_a_x
    x = x + _L0_attn_a_ref(_layernorm(x, axis=-1), L0_attn_a_w_qkv, L0_attn_a_w_swiglu, L0_attn_a_w_out)
    x = x + _L0_ffn_ref(_layernorm(x, axis=-1), L0_ffn_ln1_w, L0_ffn_ln1_b, L0_ffn_ln2_w, L0_ffn_ln2_b, L0_ffn_wq, L0_ffn_wk, L0_ffn_wv, L0_ffn_wo, L0_ffn_bq, L0_ffn_bk, L0_ffn_bv, L0_ffn_bo, L0_ffn_gate_w, L0_ffn_gate_b, L0_ffn_e_w1, L0_ffn_e_b1, L0_ffn_e_w2, L0_ffn_e_b2)
    x = x + _L0_attn_b_ref(_layernorm(x, axis=-1), L0_attn_b_Wq, L0_attn_b_bq, L0_attn_b_Wk, L0_attn_b_bk, L0_attn_b_Wv, L0_attn_b_bv, L0_attn_b_Wp)
    x = x + _L0_ffn_ref(_layernorm(x, axis=-1), L0_ffn_ln1_w, L0_ffn_ln1_b, L0_ffn_ln2_w, L0_ffn_ln2_b, L0_ffn_wq, L0_ffn_wk, L0_ffn_wv, L0_ffn_wo, L0_ffn_bq, L0_ffn_bk, L0_ffn_bv, L0_ffn_bo, L0_ffn_gate_w, L0_ffn_gate_b, L0_ffn_e_w1, L0_ffn_e_b1, L0_ffn_e_w2, L0_ffn_e_b2)
    return x

_drawn_inputs = setup_inputs


def setup_inputs(seed=0):
    import zlib

    import numpy as np

    out = dict(_drawn_inputs(seed))
    spreads = {'L0_ffn_ln1_w': (1.0, 0.6),
     'L0_ffn_ln1_b': (0.0, 0.8),
     'L0_ffn_ln2_w': (1.0, 0.6),
     'L0_ffn_ln2_b': (0.0, 0.8),
     'L0_ffn_bq': (0.0, 0.8),
     'L0_ffn_bk': (0.0, 0.8),
     'L0_ffn_bv': (0.0, 0.392),
     'L0_ffn_bo': (0.0, 0.1),
     'L0_ffn_gate_b': (0.0, 0.1),
     'L0_ffn_e_b1': (0.0, 0.586),
     'L0_ffn_e_b2': (0.0, 0.1)}
    factors = {'L0_attn_b_bq': 4.245,
     'L0_attn_b_bk': 8.0,
     'L0_attn_b_bv': 2.996,
     'L0_ffn_wq': 8.0,
     'L0_ffn_wk': 8.0,
     'L0_ffn_wv': 8.0,
     'L0_ffn_wo': 2.689}
    for name, (base, spread) in spreads.items():
        noise = np.random.default_rng([zlib.crc32(name.encode()), seed]).standard_normal(out[name].shape)
        drawn = base * np.exp(spread * noise) if base else spread * noise
        out[name] = jnp.asarray(drawn.astype(out[name].dtype))
    for name, factor in factors.items():
        out[name] = (out[name] * factor).astype(out[name].dtype)
    return out
```

```python
import numpy as np
import concourse.bass as bass
from concourse import mybir
from contextlib import ExitStack

F32 = mybir.dt.float32
BF16 = mybir.dt.bfloat16
I32 = mybir.dt.int32
ALU = mybir.AluOpType
ACT = mybir.ActivationFunctionType
AXIS_X = mybir.AxisListType.X

P = 128
D = 128
S = 2048
TILES = S // P
CH = 512
CHUNKS = S // CH
TPC = CH // P
HEADS, HD = 16, 8
QUAD = 4
QUADS = HEADS // QUAD
E, FF = 8, 512
FB = FF // P
TOPK = 2
LAYERS = 2
LN_EPS = 1e-5
RMS_EPS = 1.1920929e-07
MASKED = -1e30
SOFTMAX_SCALE = HD ** -0.5

Q_PARTS = [0, 0, 1, 1, 0, 2]
K_PARTS = [0, 1, 0, 1, 2, 0]
STACK = len(Q_PARTS) * HD
SHIFT_ROW = 64

LN1_W, LN1_B, LN2_W, LN2_B, BQ, BK = (LAYERS * n for n in range(6))
B_BQ, B_BK = LAYERS * 6, LAYERS * 6 + 1
E_B1 = LAYERS * 6 + 2
N_VEC = E_B1 + E * FB


class Steps:

    def __init__(self, engine, sem, base=0):
        self.engine, self.sem, self.base, self.n = engine, sem, base, 0

    def __call__(self, instruction):
        self.n += 1
        instruction.then_inc(self.sem, 1)
        self.engine.wait_ge(self.sem, self.base + self.n)


def token_tiles(i, n=TPC):
    return bass.ds(i * n, n)


class Memory:

    def phase_semaphores(self):
        self.previous, self.current = self.current, []

        def sem(name):
            if name not in self.named:
                self.named[name] = self.ctx.enter_context(self.nc.semaphore(name))
            self.current.append(self.named[name])
            return self.named[name]

        return sem

    def clear_previous(self, pool):
        for s in self.previous:
            pool.sem_clear(s)

    def __init__(self, nc, ctx, ins):
        self.nc, self.ctx, self.named, self.current, self.previous = nc, ctx, {}, [], []

        def sb(name, shape, dt=F32):
            return ctx.enter_context(nc.sbuf_tensor(name, shape, dt))

        self.ins = ins
        self.x = sb("x_tok", [P, TILES, D])
        self.z = sb("z_tok", [P, TILES, D])
        self.mean = sb("mean", [P, TILES])
        self.rstd = sb("rstd", [P, TILES])
        self.ident = sb("ident", [P, P])
        self.ident_bf = sb("ident_bf", [P, P], BF16)
        self.hide_right = sb("hide_right", [P, P], BF16)
        self.hide_left = sb("hide_left", [P, P], BF16)
        self.upto = sb("upto", [P, P])
        self.ones = sb("ones", [P, P])
        self.rank = sb("rank", [P, E])
        self.neg_half = sb("neg_half", [P, TILES])
        self.w_qkv = sb("w_qkv_t", [P, 3 * D])
        self.w_swiglu = sb("w_swiglu_t", [P, 2 * D])
        self.w_out = sb("w_out_t", [P, D])
        self.vecs = sb("vecs", [P, N_VEC])
        self.w_att = sb("w_att", [P, LAYERS, 4, D])
        self.bv = sb("bv_rows", [P, LAYERS + 1, D])
        self.bo = sb("bo_rows", [P, LAYERS, D])
        self.w_b = sb("w_b", [P, 3, D])
        self.mix = sb("mix", [P, P])
        self.gate_w = sb("gate_w", [P, LAYERS, E])
        self.gate_b = sb("gate_b", [P, LAYERS, E])
        self.b2 = sb("b2", [E, LAYERS, D])
        self.w1 = sb("w1", [P, E, FF])
        self.w2 = sb("w2", [P, E, FB, D])
        self.q_stack = sb("q_stack", [P, CHUNKS, QUAD, CH], BF16)
        self.k_scan = sb("k_scan", [P, QUAD, S], BF16)
        self.k_stack = sb("k_stack", [P, QUAD, S], BF16)
        self.v_all = sb("v_all", [P, TILES, D])
        self.v_quad = sb("v_quad", [P, TILES, QUAD, 32])
        self.ids_int = sb("ids_int", [1, TOPK], I32)
        self.expert_weights_in = ctx.enter_context(nc.semaphore("expert_weights_in"))
        self.k_written = [ctx.enter_context(nc.semaphore(f"k_written{slot}")) for slot in range(2)]
        self.k_writes = 0
        self.q_dram = nc.dram_tensor("q_parts", [STACK, HEADS, S], BF16, kind="Internal").ap()
        self.k_dram = nc.dram_tensor("k_parts", [STACK, HEADS, S], BF16, kind="Internal").ap()
        self.o_dram = nc.dram_tensor("attended", [HEADS, 32, S], F32, kind="Internal").ap()


def set_up(nc, m, n):
    ins = m.ins
    with ExitStack() as ctx:
        raw = ctx.enter_context(nc.sbuf_tensor("raw_weights", [P, 6, D], F32))
        rows = ctx.enter_context(nc.sbuf_tensor("vector_rows", [N_VEC, D], F32))
        ps = ctx.enter_context(nc.psum_tensor("setup_ps", [P, 2, 512], F32))
        sem = m.phase_semaphores()
        raw_in, turned, rest_in, built = sem("s_raw_in"), sem("s_turned"), sem("s_rest_in"), sem("s_built")
        mix_zero, v_zero = sem("s_mix_zero"), sem("s_v_zero")
        block = ctx.enter_context(nc.Block())

        def layer_rows(name, at):
            return rows[at:at + LAYERS, :], ins["L0_ffn_" + name]

        @block.sync
        def _(sp):
            loads = [(raw[:, 0:3, :], ins["L0_attn_a_w_qkv"].rearrange("(g p) d -> p g d", p=P)),
                     (raw[:, 3:5, :], ins["L0_attn_a_w_swiglu"].rearrange("(g p) d -> p g d", p=P)),
                     (raw[:, 5, :], ins["L0_attn_a_w_out"]),
                     layer_rows("ln1_w", LN1_W), layer_rows("ln1_b", LN1_B), layer_rows("ln2_w", LN2_W),
                     layer_rows("ln2_b", LN2_B), layer_rows("bq", BQ), layer_rows("bk", BK),
                     (rows[B_BQ:B_BQ + 1, :], ins["L0_attn_b_bq"].rearrange("(a d) -> a d", a=1)),
                     (rows[B_BK:B_BK + 1, :], ins["L0_attn_b_bk"].rearrange("(a d) -> a d", a=1)),
                     (rows[E_B1:N_VEC, :], ins["L0_ffn_e_b1"][0].rearrange("e (i p) -> (e i) p", p=P))]
            for dst, src in loads:
                sp.dma_start(dst, src).then_inc(raw_in, 16)
            rest = [(m.x[:, :, :], ins["L0_attn_a_x"][0].rearrange("(t p) d -> p t d", p=P))]
            for i, name in enumerate(("wq", "wk", "wv", "wo")):
                rest.append((m.w_att[:, :, i, :], ins["L0_ffn_" + name].rearrange("l p d -> p l d")))
            for i, name in enumerate(("Wq", "Wk", "Wv")):
                rest.append((m.w_b[:, i, :], ins["L0_attn_b_" + name]))
            for layer in range(LAYERS):
                rest.append((m.bv[:, layer, :], ins["L0_ffn_bv"][layer].partition_broadcast(P)))
                rest.append((m.bo[:, layer, :], ins["L0_ffn_bo"][layer].partition_broadcast(P)))
                rest.append((m.gate_b[:, layer, :], ins["L0_ffn_gate_b"][layer].partition_broadcast(P)))
                rest.append((m.gate_w[:, layer, :], ins["L0_ffn_gate_w"][layer]))
                rest.append((m.b2[:, layer, :], ins["L0_ffn_e_b2"][layer]))
            rest.append((m.bv[:, LAYERS, :], ins["L0_attn_b_bv"].partition_broadcast(P)))
            for dst, src in rest:
                sp.dma_start(dst, src).then_inc(rest_in, 16)
            sp.wait_ge(mix_zero, 1)
            for h in range(HEADS):
                sp.dma_start(m.mix[HD * h:HD * h + HD, HD * h:HD * h + HD], ins["L0_attn_b_Wp"]).then_inc(rest_in, 16)
            sp.dma_start(m.w1[:, :, :], ins["L0_ffn_e_w1"][0].rearrange("e p f -> p e f"))\
                .then_inc(m.expert_weights_in, 16)
            for e in range(E):
                sp.dma_start(m.w2[:, e, :, :], ins["L0_ffn_e_w2"][0, e].rearrange("(i p) d -> p i d", p=P))\
                    .then_inc(m.expert_weights_in, 16)
            sp.wait_ge(rest_in, 16 * (len(rest) + HEADS))

        @block.gpsimd
        def _(pool):
            m.clear_previous(pool)
            nc.gpsimd.memset(m.ident[:, :], 0.0).then_inc(built, 1)
            nc.gpsimd.memset(m.ident_bf[:, :], 0.0).then_inc(built, 1)
            nc.gpsimd.memset(m.hide_right[:, :], 0.0).then_inc(built, 1)
            nc.gpsimd.memset(m.hide_left[:, :], 0.0).then_inc(built, 1)
            nc.gpsimd.memset(m.upto[:, :], 1.0).then_inc(built, 1)
            nc.gpsimd.memset(m.ones[:, :], 1.0).then_inc(built, 1)
            pool.wait_ge(built, 6)

            def select(t, op, fill, column, row):
                nc.gpsimd.affine_select(out=t[:, :], in_=t[:, :], compare_op=op, fill=fill, base=0,
                                        pattern=[[column, P]], channel_multiplier=row).then_inc(built, 1)

            select(m.ident, ALU.not_equal, 1.0, -1, 1)
            select(m.ident_bf, ALU.not_equal, 1.0, -1, 1)
            select(m.hide_right, ALU.is_ge, MASKED, -1, 1)
            select(m.hide_left, ALU.is_ge, MASKED, 1, -1)
            select(m.upto, ALU.is_ge, 0.0, 1, -1)
            for e in range(E):
                nc.gpsimd.memset(m.rank[:, e:e + 1], float(E - e))
            nc.gpsimd.memset(m.neg_half[:, :], -0.5)
            nc.gpsimd.memset(m.v_quad[:, :, :, :], 0.0).then_inc(v_zero, 1)
            pool.wait_ge(v_zero, 1)
            nc.gpsimd.memset(m.neg_half[:, :], -0.5)
            nc.gpsimd.memset(m.v_quad[:, :, :, HD:HD + 1], 1.0)

        @block.vector
        def _(dve):
            nc.vector.memset(m.mix[:, :], 0.0).then_inc(mix_zero, 1)
            nc.vector.memset(m.q_stack[:, :, :, :].bitcast(F32), 0.0).then_inc(mix_zero, 1)
            for stack in (m.k_scan, m.k_stack):
                nc.vector.memset(stack[:, :, :].bitcast(F32), 0.0).then_inc(mix_zero, 1)
            dve.wait_ge(mix_zero, 4)
            nc.vector.memset(m.k_stack[SHIFT_ROW:SHIFT_ROW + 1, :, :], 1.0)

        @block.tensor
        def _(pe):
            pe.wait_ge(built, 7)
            pe.wait_ge(raw_in, 16 * 12)
            for g in range(6):
                nc.tensor.transpose(ps[:, g // 4, (g % 4) * P:(g % 4 + 1) * P], raw[:, g, :], m.ident[:, :])\
                    .then_inc(turned, 1)
            nc.tensor.transpose(ps[:, 1, 256:256 + N_VEC], rows[:, :], m.ident[0:N_VEC, 0:N_VEC]).then_inc(turned, 1)

        @block.scalar
        def _(act):
            act.wait_ge(turned, 7)
            nc.scalar.activation(m.w_qkv[:, :], ps[:, 0, 0:3 * P], ACT.Copy)
            nc.scalar.activation(m.w_swiglu[:, 0:P], ps[:, 0, 3 * P:4 * P], ACT.Copy)
            nc.scalar.activation(m.w_swiglu[:, P:2 * P], ps[:, 1, 0:P], ACT.Copy)
            nc.scalar.activation(m.w_out[:, :], ps[:, 1, P:2 * P], ACT.Copy)
            nc.scalar.activation(m.vecs[:, :], ps[:, 1, 256:256 + N_VEC], ACT.Copy)


def row_moments(nc, step, st, mean, var, t1, t2, eps):
    step(nc.vector.tensor_tensor(t1, st[:, :, 1], st[:, :, 4], ALU.subtract))
    step(nc.vector.tensor_tensor(mean, st[:, :, 1], st[:, :, 4], ALU.add))
    step(nc.vector.tensor_tensor(t2, st[:, :, 2], st[:, :, 5], ALU.add))
    step(nc.vector.tensor_scalar(t2, t2, 1.0 / D, None, ALU.mult))
    step(nc.vector.scalar_tensor_tensor(t1, t1, 0.25, t1, ALU.mult, ALU.mult))
    step(nc.vector.tensor_scalar(mean, mean, 0.5, None, ALU.mult))
    return nc.vector.scalar_tensor_tensor(var, t1, eps, t2, ALU.add, ALU.add)


def inverse_root(nc, pool, m, out, in_, in_ready, out_ready, count):
    pool.wait_ge(in_ready, count)
    nc.gpsimd.tensor_tensor(out, in_, m.neg_half[:, 0:out.shape[-1]], ALU.pow).then_inc(out_ready, 1)


def token_stats(nc, step, src, st, m, tmp, var_ready, rstd_ready, count):
    for t in range(TILES):
        last = nc.vector.bn_stats(st[:, t, :], src[:, t, :])
    step(last)
    row_moments(nc, step, st, m.mean[:, :], tmp[:, 0, :], tmp[:, 1, :], tmp[:, 2, :], LN_EPS).then_inc(var_ready, 1)
    step.engine.wait_ge(rstd_ready, count)


def normalise(nc, step, dst, src, m):
    for t in range(TILES):
        last = nc.vector.tensor_scalar(dst[:, t, :], src[:, t, :], m.mean[:, t:t + 1], m.rstd[:, t:t + 1],
                                       ALU.subtract, ALU.mult)
    step(last)


def stage_a(nc, m, n):
    with ExitStack() as ctx:
        def sb(name, shape, dt=F32):
            return ctx.enter_context(nc.sbuf_tensor(name + n, shape, dt))

        sem = m.phase_semaphores()

        h = sb("a_h", [P, TILES, D])
        st = sb("a_st", [P, TILES, 6])
        st8 = sb("a_st8", [P, 2 * TPC, 6])
        tmp = sb("a_tmp", [P, 3, TILES])
        tmp8 = sb("a_tmp8", [P, 6, 2 * TPC])
        rh = sb("a_rh", [P, TILES])
        hn = sb("a_hn", [P, TPC, D])
        hn_t = sb("a_hn_t", [P, CH])
        wkv = sb("a_wkv", [P, TPC, 2 * D])
        eq = sb("a_eq", [P, TPC, D])
        run = sb("a_run", [P, TPC + 1, 2 * D])
        den = sb("a_den", [P, TPC, D])
        y = sb("a_y", [P, TPC, D])
        y_t = sb("a_y_t", [P, CH])
        eg = sb("a_eg", [P, TPC, D])
        ug = sb("a_ug", [P, TPC, D])
        g_t = sb("a_g_t", [P, CH])
        ps_qkv = ctx.enter_context(nc.psum_tensor("a_ps_qkv" + n, [P, TPC, 512], F32))
        ps_turn = ctx.enter_context(nc.psum_tensor("a_ps_turn" + n, [P, CH], F32))
        ps_sum = ctx.enter_context(nc.psum_tensor("a_ps_sum" + n, [P, TPC, 2 * D], F32))
        ps_out = ctx.enter_context(nc.psum_tensor("a_ps_out" + n, [P, TPC, D], F32))
        hn_ready, turned, turn_copied = sem("a_hn_ready"), sem("a_turned"), sem("a_turn_copied")
        qkv_ready, scales_ready, exps_ready = sem("a_qkv_ready"), sem("a_scales_ready"), sem("a_exps_ready")
        sums_in, summed, y_ready = sem("a_sums_in"), sem("a_summed"), sem("a_y_ready")
        uv_ready, neg_ready, gate_ready = sem("a_uv_ready"), sem("a_neg_ready"), sem("a_gate_ready")
        ug_ready, out_ready, dve_steps = sem("a_ug_ready"), sem("a_out_ready"), sem("a_dve_steps")
        var_ready, rstd_ready = sem("a_var_ready"), sem("a_rstd_ready")
        block = ctx.enter_context(nc.Block())
        uv = ps_qkv[:, 0:2, :].rearrange("p b (t f) -> p (b t) f", t=2)

        @block.vector
        def _(dve):
            step = Steps(dve, dve_steps)
            token_stats(nc, step, m.x, st, m, tmp, var_ready, rstd_ready, 1)
            normalise(nc, step, h, m.x, m)
            for t in range(TILES):
                last = nc.vector.bn_stats(st[:, t, :], h[:, t, :])
            step(last)
            step(row_moments(nc, step, st, m.mean[:, :], tmp[:, 0, :], tmp[:, 1, :], tmp[:, 2, :], RMS_EPS))
            step(nc.vector.tensor_tensor(tmp[:, 1, :], m.mean[:, :], m.mean[:, :], ALU.mult))
            nc.vector.tensor_tensor(tmp[:, 0, :], tmp[:, 0, :], tmp[:, 1, :], ALU.add).then_inc(var_ready, 1)
            dve.wait_ge(rstd_ready, 2)
            step(nc.vector.memset(run[:, 0, :], 0.0))
            before, per_round = step.n, 22
            with dve.Fori(0, CHUNKS) as i:
                step = Steps(dve, dve_steps, i * per_round + before)
                for r in range(TPC):
                    last = nc.vector.tensor_scalar(hn[:, r:r + 1, :], h[:, bass.ds(i * TPC + r, 1), :],
                                                   rh[:, bass.ds(i * TPC + r, 1)], None, ALU.mult)
                last.then_inc(hn_ready, 1)
                dve.wait_ge(qkv_ready, i + 1)
                for r in range(TPC):
                    for k in range(2):
                        last = nc.vector.bn_stats(st8[:, 2 * r + k, :], ps_qkv[:, r, k * D:(k + 1) * D])
                step(last)
                step(row_moments(nc, step, st8, tmp8[:, 0, :], tmp8[:, 1, :], tmp8[:, 2, :], tmp8[:, 3, :], RMS_EPS))
                step(nc.vector.tensor_tensor(tmp8[:, 2, :], tmp8[:, 0, :], tmp8[:, 0, :], ALU.mult))
                nc.vector.tensor_tensor(tmp8[:, 1, :], tmp8[:, 1, :], tmp8[:, 2, :], ALU.add).then_inc(var_ready, 1)
                dve.wait_ge(rstd_ready, i + 3)
                nc.vector.tensor_scalar(tmp8[:, 5, :], tmp8[:, 4, :], -1.0, None, ALU.mult).then_inc(scales_ready, 1)
                dve.wait_ge(exps_ready, i + 1)
                step(nc.vector.tensor_tensor(wkv[:, :, D:2 * D], wkv[:, :, 0:D], ps_qkv[:, :, 2 * D:3 * D], ALU.mult))
                for r in range(TPC):
                    step(nc.vector.tensor_tensor(run[:, r + 1, :], run[:, r, :], wkv[:, r, :], ALU.add))
                nc.vector.tensor_scalar(eq[:, :, :], eq[:, :, :], 1.0, None, ALU.add).then_inc(sums_in, 1)
                dve.wait_ge(sums_in, i + 1)
                dve.wait_ge(summed, i + 1)
                step(nc.vector.scalar_tensor_tensor(den[:, :, :], ps_sum[:, :, 0:D], 1e-6, eq[:, :, :],
                                                    ALU.add, ALU.mult))
                step(nc.vector.reciprocal(den[:, :, :], den[:, :, :]))
                nc.vector.tensor_tensor(y[:, :, :], ps_sum[:, :, D:2 * D], den[:, :, :], ALU.mult).then_inc(y_ready, 1)
                step(nc.vector.tensor_copy(run[:, 0, :], run[:, TPC, :]))
                dve.wait_ge(uv_ready, i + 1)
                nc.vector.tensor_scalar(eg[:, :, :], uv[:, :, D:2 * D], -1.0, 80.0, ALU.mult, ALU.min)\
                    .then_inc(neg_ready, 1)
                dve.wait_ge(gate_ready, i + 1)
                step(nc.vector.tensor_scalar(eg[:, :, :], eg[:, :, :], 1.0, None, ALU.add))
                step(nc.vector.reciprocal(eg[:, :, :], eg[:, :, :]))
                step(nc.vector.tensor_tensor(eg[:, :, :], eg[:, :, :], uv[:, :, D:2 * D], ALU.mult))
                nc.vector.tensor_tensor(ug[:, :, :], eg[:, :, :], uv[:, :, 0:D], ALU.mult).then_inc(ug_ready, 1)
                dve.wait_ge(out_ready, i + 1)
                step(nc.vector.tensor_tensor(den[:, :, :], ps_out[:, :, :], h[:, token_tiles(i), :], ALU.add))
                step(nc.vector.tensor_tensor(m.x[:, token_tiles(i), :], m.x[:, token_tiles(i), :], den[:, :, :],
                                             ALU.add))
                assert step.n == per_round, step.n

        @block.gpsimd
        def _(pool):
            m.clear_previous(pool)
            inverse_root(nc, pool, m, m.rstd[:, :], tmp[:, 0, :], var_ready, rstd_ready, 1)
            inverse_root(nc, pool, m, rh[:, :], tmp[:, 0, :], var_ready, rstd_ready, 2)
            with pool.Fori(0, CHUNKS) as i:
                inverse_root(nc, pool, m, tmp8[:, 4, :], tmp8[:, 1, :], var_ready, rstd_ready, i + 3)

        @block.tensor
        def _(pe):
            with pe.Fori(0, CHUNKS) as i:
                pe.wait_ge(hn_ready, i + 1)
                for r in range(TPC):
                    last = nc.tensor.transpose(ps_turn[:, r * P:(r + 1) * P], hn[:, r, :], m.ident[:, :])
                last.then_inc(turned, 1)
                pe.wait_ge(turn_copied, 3 * i + 1)
                for r in range(TPC):
                    last = nc.tensor.matmul(ps_qkv[:, r, 0:3 * D], hn_t[:, r * P:(r + 1) * P], m.w_qkv[:, :],
                                            start=True, stop=True)
                last.then_inc(qkv_ready, 1)
                pe.wait_ge(sums_in, i + 1)
                for r in range(TPC):
                    nc.tensor.matmul(ps_sum[:, r, :], m.upto[:, :], wkv[:, r, :], start=True, stop=False)
                    last = nc.tensor.matmul(ps_sum[:, r, :], m.ones[:, :], run[:, r, :], start=False, stop=True)
                last.then_inc(summed, 1)
                pe.wait_ge(y_ready, i + 1)
                for r in range(TPC):
                    last = nc.tensor.transpose(ps_turn[:, r * P:(r + 1) * P], y[:, r, :], m.ident[:, :])
                last.then_inc(turned, 1)
                pe.wait_ge(turn_copied, 3 * i + 2)
                for r in range(TPC):
                    last = nc.tensor.matmul(uv[:, r, :], y_t[:, r * P:(r + 1) * P], m.w_swiglu[:, :],
                                            start=True, stop=True)
                last.then_inc(uv_ready, 1)
                pe.wait_ge(ug_ready, i + 1)
                for r in range(TPC):
                    last = nc.tensor.transpose(ps_turn[:, r * P:(r + 1) * P], ug[:, r, :], m.ident[:, :])
                last.then_inc(turned, 1)
                pe.wait_ge(turn_copied, 3 * i + 3)
                for r in range(TPC):
                    last = nc.tensor.matmul(ps_out[:, r, :], g_t[:, r * P:(r + 1) * P], m.w_out[:, :],
                                            start=True, stop=True)
                last.then_inc(out_ready, 1)

        @block.scalar
        def _(act):
            with act.Fori(0, CHUNKS) as i:
                act.wait_ge(turned, 3 * i + 1)
                nc.scalar.activation(hn_t[:, :], ps_turn[:, :], ACT.Copy).then_inc(turn_copied, 1)
                act.wait_ge(scales_ready, i + 1)
                for r in range(TPC):
                    nc.scalar.activation(wkv[:, r, 0:D], ps_qkv[:, r, D:2 * D], ACT.Exp,
                                         scale=tmp8[:, 4, 2 * r + 1:2 * r + 2])
                    last = nc.scalar.activation(eq[:, r, :], ps_qkv[:, r, 0:D], ACT.Exp,
                                                scale=tmp8[:, 5, 2 * r:2 * r + 1])
                last.then_inc(exps_ready, 1)
                act.wait_ge(turned, 3 * i + 2)
                nc.scalar.activation(y_t[:, :], ps_turn[:, :], ACT.Copy).then_inc(turn_copied, 1)
                act.wait_ge(neg_ready, i + 1)
                nc.scalar.activation(eg[:, :, :], eg[:, :, :], ACT.Exp).then_inc(gate_ready, 1)
                act.wait_ge(turned, 3 * i + 3)
                nc.scalar.activation(g_t[:, :], ps_turn[:, :], ACT.Copy).then_inc(turn_copied, 1)


def project_qkv(nc, m, n, first=None, layer=None):
    mixing = layer is None
    src = m.x if mixing else m.z
    with ExitStack() as ctx:
        def sb(name, shape, dt=F32):
            return ctx.enter_context(nc.sbuf_tensor(name + n, shape, dt))

        sem = m.phase_semaphores()

        st = sb("p_st", [P, TILES, 6])
        tmp = sb("p_tmp", [P, 3, TILES])
        hn = sb("p_hn", [P, 2, TPC, D])
        h_t = sb("p_h_t", [P, 2, CH])
        raw = sb("p_raw", [P, 2, CH])
        rest = sb("p_rest", [P, 2, CH])
        parts = sb("p_parts", [P, 2, 2, 3, CH], BF16)
        ps_turn = ctx.enter_context(nc.psum_tensor("p_ps_turn" + n, [P, CH], F32))
        ps_qk = ctx.enter_context(nc.psum_tensor("p_ps_qk" + n, [P, 2, 2, CH], F32))
        ps_mixed = ctx.enter_context(nc.psum_tensor("p_ps_mixed" + n, [P, 2, CH], F32))
        ps_v = ctx.enter_context(nc.psum_tensor("p_ps_v" + n, [P, TPC, D], F32))
        hn_ready, turned, h_ready = sem("p_hn_ready"), sem("p_turned"), sem("p_h_ready")
        qk_ready, raw_ready, mixed = sem("p_qk_ready"), sem("p_raw_ready"), sem("p_mixed")
        v_ready, high_ready = sem("p_v_ready"), sem("p_high_ready")
        rest_ready, mid_ready, low_ready = sem("p_rest_ready"), sem("p_mid_ready"), sem("p_low_ready")
        v_kept, dve_steps = sem("p_v_kept"), sem("p_dve_steps")
        written = [[sem(f"p_written{slot}") for slot in range(2)], m.k_written]
        base = [0, m.k_writes]
        m.k_writes += 16 * len(K_PARTS) * CHUNKS // 2
        var_ready, rstd_ready = sem("p_var_ready"), sem("p_rstd_ready")
        block = ctx.enter_context(nc.Block())
        weights = [m.w_b[:, i, :] if mixing else m.w_att[:, layer, i, :] for i in range(3)]
        bias = [m.vecs[:, c:c + 1] for c in ((B_BQ, B_BK) if mixing else (BQ + layer, BK + layer))]
        bv = m.bv[:, LAYERS if mixing else layer, :]
        norms = 2 if first else 1

        def projected(c, k):
            return ps_mixed[:, k, :] if mixing else ps_qk[:, c % 2, k, :]

        def write_parts(engine, c, k):
            dram, parts_of = ((m.q_dram, Q_PARTS), (m.k_dram, K_PARTS))[k]
            engine.wait_ge(high_ready, 2 * c + k + 1)
            engine.wait_ge(mid_ready, 2 * c + k + 1)
            engine.wait_ge(low_ready, 2 * c + k + 1)
            for g, part in enumerate(parts_of):
                dst = dram[g * HD:(g + 1) * HD, :, c * CH:(c + 1) * CH].rearrange("d h q -> h d q")
                engine.dma_start(dst, parts[:, c % 2, k, part, :]).then_inc(written[k][c % 2], 16)

        @block.gpsimd
        def _(pool):
            m.clear_previous(pool)
            for k in range(norms):
                inverse_root(nc, pool, m, m.rstd[:, :], tmp[:, 0, :], var_ready, rstd_ready, k + 1)
            for c in range(CHUNKS):
                write_parts(pool, c, 1)
            for slot in range(2):
                pool.wait_ge(written[1][slot], base[1] + 16 * len(K_PARTS) * CHUNKS // 2)

        @block.sync
        def _(sp):
            for c in range(CHUNKS):
                write_parts(sp, c, 0)
            for slot in range(2):
                sp.wait_ge(written[0][slot], 16 * len(Q_PARTS) * CHUNKS // 2)

        @block.vector
        def _(dve):
            step = Steps(dve, dve_steps)
            if first:
                token_stats(nc, step, m.x, st, m, tmp, var_ready, rstd_ready, 1)
                normalise(nc, step, m.z, m.x, m)
            token_stats(nc, step, src, st, m, tmp, var_ready, rstd_ready, norms)

            def normalise_chunk(c):
                if c >= 2:
                    dve.wait_ge(turned, c - 1)
                for r in range(TPC):
                    t = c * TPC + r
                    last = nc.vector.tensor_scalar(hn[:, c % 2, r, :], src[:, t, :], m.mean[:, t:t + 1],
                                                   m.rstd[:, t:t + 1], ALU.subtract, ALU.mult)
                last.then_inc(hn_ready, 1)

            normalise_chunk(0)
            normalise_chunk(1)
            for c in range(CHUNKS):
                if mixing:
                    for k in range(2):
                        dve.wait_ge(qk_ready, 2 * c + k + 1)
                        nc.vector.tensor_scalar(raw[:, k, :], ps_qk[:, c % 2, k, :], bias[k], None, ALU.add)\
                            .then_inc(raw_ready, 1)
                dve.wait_ge(v_ready, c + 1)
                nc.vector.tensor_tensor(m.v_all[:, c * TPC:(c + 1) * TPC, :], ps_v[:, :, :],
                                        bv.unsqueeze(1).broadcast_to([P, TPC, D]), ALU.add).then_inc(v_kept, 1)
                if c + 2 < CHUNKS:
                    normalise_chunk(c + 2)
                for k in range(2):
                    dve.wait_ge(high_ready, 2 * c + k + 1)
                    if c:
                        dve.wait_ge(low_ready, 2 * (c - 1) + k + 1)
                    if mixing:
                        nc.vector.tensor_tensor(rest[:, k, :], projected(c, k), parts[:, c % 2, k, 0, :],
                                                ALU.subtract).then_inc(rest_ready, 1)
                    else:
                        nc.vector.scalar_tensor_tensor(rest[:, k, :], projected(c, k), bias[k],
                                                       parts[:, c % 2, k, 0, :], ALU.add, ALU.subtract)\
                            .then_inc(rest_ready, 1)
                for k in range(2):
                    dve.wait_ge(mid_ready, 2 * c + k + 1)
                    nc.vector.tensor_tensor(parts[:, c % 2, k, 2, :], rest[:, k, :], parts[:, c % 2, k, 1, :],
                                            ALU.subtract).then_inc(low_ready, 1)

        @block.tensor
        def _(pe):
            def transpose_chunk(c):
                pe.wait_ge(hn_ready, c + 1)
                if c:
                    pe.wait_ge(h_ready, c)
                for r in range(TPC):
                    last = nc.tensor.transpose(ps_turn[:, r * P:(r + 1) * P], hn[:, c % 2, r, :], m.ident[:, :])
                last.then_inc(turned, 1)

            transpose_chunk(0)
            transpose_chunk(1)
            for c in range(CHUNKS):
                pe.wait_ge(h_ready, c + 1)
                if c >= 2:
                    pe.wait_ge(raw_ready if mixing else rest_ready, 2 * (c - 1))
                for k in range(2):
                    nc.tensor.matmul(ps_qk[:, c % 2, k, :], weights[k], h_t[:, c % 2, :], start=True, stop=True)\
                        .then_inc(qk_ready, 1)
                if c:
                    pe.wait_ge(v_kept, c)
                for r in range(TPC):
                    last = nc.tensor.matmul(ps_v[:, r, :], h_t[:, c % 2, r * P:(r + 1) * P], weights[2],
                                            start=True, stop=True)
                last.then_inc(v_ready, 1)
                if mixing:
                    for k in range(2):
                        pe.wait_ge(raw_ready, 2 * c + k + 1)
                        if c:
                            pe.wait_ge(rest_ready, 2 * (c - 1) + k + 1)
                        nc.tensor.matmul(ps_mixed[:, k, :], m.mix[:, :], raw[:, k, :], start=True, stop=True)\
                            .then_inc(mixed, 1)
                if c + 2 < CHUNKS:
                    transpose_chunk(c + 2)

        @block.scalar
        def _(act):
            def copy_chunk(c):
                act.wait_ge(turned, c + 1)
                if c >= 2:
                    act.wait_ge(v_ready, c - 1)
                if mixing:
                    nc.scalar.activation(h_t[:, c % 2, :], ps_turn[:, :], ACT.Copy).then_inc(h_ready, 1)
                else:
                    nc.scalar.activation(h_t[:, c % 2, :], ps_turn[:, :], ACT.Identity,
                                         scale=m.vecs[:, LN1_W + layer:LN1_W + layer + 1],
                                         bias=m.vecs[:, LN1_B + layer:LN1_B + layer + 1]).then_inc(h_ready, 1)

            copy_chunk(0)
            copy_chunk(1)
            for c in range(CHUNKS):
                for k in range(2):
                    act.wait_ge(mixed if mixing else qk_ready, 2 * c + k + 1)
                    if c >= 2:
                        act.wait_ge(written[k][c % 2], base[k] + 16 * len(Q_PARTS) * (c // 2))
                    if mixing:
                        nc.scalar.activation(parts[:, c % 2, k, 0, :], projected(c, k), ACT.Copy)\
                            .then_inc(high_ready, 1)
                    else:
                        nc.scalar.activation(parts[:, c % 2, k, 0, :], projected(c, k), ACT.Identity, bias=bias[k])\
                            .then_inc(high_ready, 1)
                if c + 2 < CHUNKS:
                    copy_chunk(c + 2)
                for k in range(2):
                    act.wait_ge(rest_ready, 2 * c + k + 1)
                    nc.scalar.activation(parts[:, c % 2, k, 1, :], rest[:, k, :], ACT.Copy).then_inc(mid_ready, 1)


SCAN_KEYS = 512
RING_A = 4
RING_S, RING_P = 3, 8
LEAD = 64
PACING = {True: (2500, 3000, 0.9), False: (3500, 3500, 1.0)}


def attention_schedule(causal, last_quad):
    lead = LEAD
    margin, reload, hurry = PACING[causal]
    blocks = [TPC * (c + 1) if causal else TILES for c in range(CHUNKS)]

    pieces = []
    for c in range(CHUNKS):
        for j in range(QUAD):
            for t in range(TPC):
                keys = (TPC * c + t + 1) * P if causal else S
                for p in range(-(-keys // SCAN_KEYS)):
                    pieces.append((c, j, t, p, min(SCAN_KEYS, keys - SCAN_KEYS * p)))
    units = [(c, kb, j) for c in range(CHUNKS) for kb in range(blocks[c]) for j in range(QUAD)]

    def unit_cost(c, kb):
        return (CH - (max(0, kb - TPC * c) * P if causal else 0)) + 40

    starts, total = [], 0
    for c, kb, j in units:
        starts.append(total)
        total += unit_cost(c, kb)
    begins = [starts[units.index((c, 0, 0))] for c in range(CHUNKS)] + [total]
    own, following = pieces[lead:], ([] if last_quad else pieces[:lead])
    work = [(x, False) for x in own] + [(x, True) for x in following]
    costs = [x[4] + 60 for x, _ in work]
    pace = total / sum(x[4] + 60 for x in pieces)
    even, at = [], 0.0
    for cost in costs:
        even.append(at)
        at += cost * pace
    latest, bound = [0.0] * len(work), float(total)
    for i in range(len(work) - 1, -1, -1):
        (c, *_), nxt = work[i]
        if not nxt:
            bound = min(bound, begins[c] - margin)
        bound -= costs[i] * hurry
        latest[i] = bound
    times = []
    for i, ((c, *_), nxt) in enumerate(work):
        when = min(even[i], latest[i])
        if nxt:
            when = max(when, begins[c + 1] + 600, begins[CHUNKS - 1] + reload)
        times.append(max(when, times[-1] if times else when))

    order, pending, given = [], None, 0

    def give(upto_time):
        nonlocal given
        while given < len(work) and times[given] <= upto_time:
            (c, j, t, p, width), nxt = work[given]
            order.append(("scan", c, j, t, p, width, nxt))
            given += 1
            if given == len(work) or work[given][0][0] != c:
                if (c, j, t) == (c, QUAD - 1, TPC - 1):
                    order.append(("rows", c, nxt))

    for u, (c, kb, j) in enumerate(units):
        order.append(("scores", c, kb, j))
        give(starts[u])
        if j == QUAD - 1:
            if pending:
                order.append(("values", *pending))
                if pending[1] == blocks[pending[0]] - 1:
                    order.append(("drain", pending[0]))
            pending = (c, kb)
    give(float("inf"))
    order += [("values", *pending), ("drain", pending[0])]
    first = []
    for i, (c, j, t, p, width) in enumerate(pieces[:lead]):
        first.append(("scan", c, j, t, p, width, False))
        if pieces[i + 1][0] != c:
            first.append(("rows", c, False))
    return first, order, blocks


def attention_heads(nc, m, n, causal):
    first, order, blocks = attention_schedule(causal, False)
    _, order_last, _ = attention_schedule(causal, True)
    scans_first = sum(x[0] == "scan" for x in first)
    scans = sum(x[0] == "scan" for x in order)
    units = QUAD * sum(blocks)
    before = [QUAD * sum(blocks[:c]) for c in range(CHUNKS)]

    def unit(c, kb, j):
        return before[c] + kb * QUAD + j

    def previous(u, ring):
        return u - ring if u >= ring else u + ring * ((units - 1 - u) // ring) - units

    with ExitStack() as ctx:
        def sb(name, shape, dt=F32):
            return ctx.enter_context(nc.sbuf_tensor(name + n, shape, dt))

        sem = m.phase_semaphores()

        probs = sb("h_probs", [P, RING_P, CH])
        maxima = sb("h_maxima", [P, 2, QUAD * TPC, S // SCAN_KEYS])
        negated = sb("h_negated", [P, 32], BF16)
        neg_rows = sb("h_neg_rows", [P, 2, 32], BF16)
        drained_sb = sb("h_drained", [P, 2, CH])
        ps_scan = ctx.enter_context(nc.psum_tensor("h_ps_scan" + n, [P, RING_A, SCAN_KEYS], F32))
        ps_scores = ctx.enter_context(nc.psum_tensor("h_ps_scores" + n, [P, RING_S, CH], F32))
        ps_values = ctx.enter_context(nc.psum_tensor("h_ps_values" + n, [P, CH], F32))
        scanned, reduced, scored, exped, valued = (sem(s) for s in ("h_scanned", "h_reduced", "h_scored", "h_exped",
                                                                    "h_valued"))
        drained, neg_ready, neg_turned, v_in = (sem(s) for s in ("h_drained_", "h_neg_ready", "h_neg_turned", "h_v_in"))
        q_in = [sem(f"h_q_in{c}") for c in range(CHUNKS)]
        scan_in = [sem(f"h_scan_in{c}") for c in range(CHUNKS)]
        k_in = [sem(f"h_k_in{c}") for c in range(CHUNKS)]
        rows_in = [sem(f"h_rows_in{c}") for c in range(CHUNKS)]
        out_done = [sem(f"h_out_done{c}") for c in range(2)]
        block = ctx.enter_context(nc.Block())

        def cols(c):
            return slice(c * CH, (c + 1) * CH)

        @block.tensor
        def _(pe):
            def scan(q, a, c, j, t, p, width):
                if (j, t, p) == (0, 0, 0):
                    pe.wait_ge(q_in[c], 16 * (q + 1))
                    for k in ([c] if causal or c else range(CHUNKS)):
                        pe.wait_ge(scan_in[k], 16 * (q + 1))
                if not (isinstance(a, int) and a < RING_A):
                    pe.wait_ge(reduced, a - RING_A + 1)
                slot = piece[0] % RING_A
                piece[0] += 1
                at = (TPC * c + t) * P
                queries = m.q_stack[:, c, j, t * P:(t + 1) * P]
                for o in range(0, width, CH):
                    w = min(CH, width - o)
                    diag = causal and SCAN_KEYS * p + o + w == at + P
                    last = nc.tensor.matmul(ps_scan[:, slot, o:o + w], queries,
                                            m.k_scan[:, j, SCAN_KEYS * p + o:SCAN_KEYS * p + o + w],
                                            start=True, stop=not diag)
                    if diag:
                        last = nc.tensor.matmul(ps_scan[:, slot, o + w - P:o + w], m.ident_bf[:, :],
                                                m.hide_right[:, :], start=False, stop=True)
                last.then_inc(scanned, 1)

            def scores(q, c, kb, j):
                u = unit(c, kb, j)
                if j == 0 and kb == 0:
                    pe.wait_ge(rows_in[c], 64 * (q + 1))
                if j == 0 and kb % TPC == 0:
                    pe.wait_ge(k_in[kb // TPC], 16 * (q + 1))
                pe.wait_ge(exped, units * (q + 1) + previous(u, RING_S) + 1)
                off = max(0, kb - TPC * c) * P if causal else 0
                diag = causal and kb >= TPC * c
                last = nc.tensor.matmul(ps_scores[:, u % RING_S, off:CH], m.k_stack[:, j, kb * P:(kb + 1) * P],
                                        m.q_stack[:, c, j, off:CH], start=True, stop=not diag)
                if diag:
                    last = nc.tensor.matmul(ps_scores[:, u % RING_S, off:off + P], m.ident_bf[:, :],
                                            m.hide_left[:, :], start=False, stop=True)
                last.then_inc(scored, 1)

            def values(q, c, kb):
                if kb == 0:
                    pe.wait_ge(drained, CHUNKS * q + c)
                if kb % TPC == 0:
                    pe.wait_ge(v_in, CHUNKS * q + kb // TPC + 1)
                pe.wait_ge(exped, units * (q + 1) + unit(c, kb, QUAD - 1) + 1)
                off = max(0, kb - TPC * c) * P if causal else 0
                for j in range(QUAD):
                    nc.tensor.matmul(ps_values[32 * j:32 * j + 32, off:CH], m.v_quad[:, kb, j, :],
                                     probs[:, unit(c, kb, j) % RING_P, off:CH],
                                     start=kb == 0, stop=kb == blocks[c] - 1).then_inc(valued, 1)

            def run(q, steps, a):
                for s in steps:
                    if s[0] == "scan":
                        scan(q + 1 if s[6] else q, a, *s[1:6])
                        a = a + 1
                    elif s[0] == "scores":
                        scores(q, *s[1:])
                    elif s[0] == "values":
                        values(q, *s[1:])

            pe.sem_inc(valued, units)
            piece = [0]
            run(0, first, 0)
            with pe.Fori(0, QUADS - 1) as q:
                run(q, order, q * scans + scans_first)
            run(QUADS - 1, order_last, (QUADS - 1) * scans + scans_first)

        @block.scalar
        def _(act):
            act.sem_inc(exped, units)

            def run(q, steps):
                for s in steps:
                    if s[0] == "scores":
                        c, kb, j = s[1:]
                        u = unit(c, kb, j)
                        off = max(0, kb - TPC * c) * P if causal else 0
                        act.wait_ge(scored, units * q + u + 1)
                        act.wait_ge(valued, units * (q + 1) + previous(u, RING_P) + 1)
                        nc.scalar.activation(probs[:, u % RING_P, off:CH], ps_scores[:, u % RING_S, off:CH], ACT.Exp,
                                             scale=SOFTMAX_SCALE).then_inc(exped, 1)

            with act.Fori(0, QUADS - 1) as q:
                run(q, order)
            run(QUADS - 1, order_last)

        @block.vector
        def _(dve):
            nc.vector.memset(negated[:, :], 0.0).then_inc(neg_ready, 1)
            dve.wait_ge(neg_ready, 1)

            def run(q, steps, a, r):
                for s in steps:
                    if s[0] == "scan":
                        c, j, t, p, width = s[1:6]
                        slot = piece[0] % RING_A
                        piece[0] += 1
                        dve.wait_ge(scanned, a + 1)
                        nc.vector.reduce_max(maxima[:, c % 2, TPC * j + t, p:p + 1], ps_scan[:, slot, 0:width],
                                             AXIS_X).then_inc(reduced, 1)
                        a = a + 1
                    elif s[0] == "rows":
                        c, own = s[1], (q + 1 if s[2] else q)
                        dve.wait_ge(reduced, a)
                        n_pieces = -(-(S if not causal else (c + 1) * CH) // SCAN_KEYS)
                        if n_pieces > 1:
                            nc.vector.tensor_reduce(negated[:, 0:QUAD * TPC], maxima[:, c % 2, :, 0:n_pieces], AXIS_X, ALU.max,
                                                    negate=True).then_inc(neg_ready, 1)
                        else:
                            nc.vector.tensor_scalar(negated[:, 0:QUAD * TPC], maxima[:, c % 2, :, 0], -1.0, None,
                                                    ALU.mult).then_inc(neg_ready, 1)
                        dve.wait_ge(neg_ready, r + 2)
                        if c >= 2:
                            dve.wait_ge(rows_in[c - 2], 64 * (own + 1))
                        elif not (isinstance(own, int) and own == 0):
                            dve.wait_ge(rows_in[c + 2], 64 * own)
                        nc.vector.transpose(neg_rows[:, c % 2, :], negated[:, :]).then_inc(neg_turned, 1)
                        dve.wait_ge(neg_turned, r + 1)
                        r = r + 1
                    elif s[0] == "drain":
                        c = s[1]
                        dve.wait_ge(valued, units * (q + 1) + unit(c, blocks[c] - 1, QUAD - 1) + 1)
                        dve.wait_ge(out_done[c % 2], 16 * (2 * q + c // 2))
                        nc.vector.tensor_copy(drained_sb[:, c % 2, :], ps_values[:, :]).then_inc(drained, 1)

            piece = [0]
            ahead = sum(x[0] == "rows" for x in first)
            run(0, first, 0, 0)
            with dve.Fori(0, QUADS - 1) as q:
                run(q, order, q * scans + scans_first, q * CHUNKS + ahead)
            run(QUADS - 1, order_last, (QUADS - 1) * scans + scans_first, (QUADS - 1) * CHUNKS + ahead)

        @block.gpsimd
        def _(pool):
            m.clear_previous(pool)
            def copy_values(q, i):
                nc.gpsimd.tensor_copy(m.v_quad[:, TPC * i:TPC * (i + 1), :, 0:HD],
                                      m.v_all[:, TPC * i:TPC * (i + 1), bass.ds(q * (QUAD * HD), QUAD * HD)]
                                      .rearrange("p k (j d) -> p k j d", d=HD)).then_inc(v_in, 1)

            for i in range(CHUNKS):
                copy_values(0, i)
            with pool.Fori(0, QUADS - 1) as q:
                for i in range(CHUNKS):
                    pool.wait_ge(valued, units * (q + 1) + unit(CHUNKS - 1, TPC * i + TPC - 1, QUAD - 1) + 1)
                    copy_values(q + 1, i)

        @block.sync
        def _(sp):
            def load(dst, dram, q, c, sem_):
                at = dst[0:STACK, c, :, :] if dst is m.q_stack else dst[0:STACK, :, cols(c)]
                sp.dma_start(at, dram[:, bass.ds(q * QUAD, QUAD), cols(c)]).then_inc(sem_, 16)

            def run(q, steps, a, r, reload):
                for s in steps:
                    if s[0] == "scan":
                        a = a + 1
                    elif s[0] == "rows":
                        c = s[1]
                        r = r + 1
                        sp.wait_ge(neg_turned, r)
                        rows = m.q_stack[SHIFT_ROW:SHIFT_ROW + 1, c, :, :]\
                            .rearrange("p j (t b k) -> p (j t) b k", t=TPC, k=32)
                        for b in range(4):
                            sp.dma_start(rows[:, :, b, :], neg_rows[32 * b:32 * b + QUAD * TPC, c % 2, :])\
                                .then_inc(rows_in[c], 16)
                        if reload and c == CHUNKS - 1:
                            sp.wait_ge(scanned, a)
                            for k in range(CHUNKS):
                                load(m.k_scan, m.k_dram, q + 1, k, scan_in[k])
                    elif s[0] == "scores" and reload and s[3] == QUAD - 1:
                        c, kb = s[1:3]
                        if kb == blocks[c] - 1:
                            sp.wait_ge(scored, units * q + unit(c, kb, QUAD - 1) + 1)
                            load(m.q_stack, m.q_dram, q + 1, c, q_in[c])
                        if c == CHUNKS - 1 and kb % TPC == TPC - 1:
                            sp.wait_ge(scored, units * q + unit(c, kb, QUAD - 1) + 1)
                            load(m.k_stack, m.k_dram, q + 1, kb // TPC, k_in[kb // TPC])
                    elif s[0] == "drain":
                        c = s[1]
                        sp.wait_ge(drained, CHUNKS * q + c + 1)
                        sp.dma_start(m.o_dram[bass.ds(q * QUAD, QUAD), :, cols(c)], drained_sb[:, c % 2, :])\
                            .then_inc(out_done[c % 2], 16)

            for c in range(CHUNKS):
                load(m.q_stack, m.q_dram, 0, c, q_in[c])
                load(m.k_scan, m.k_dram, 0, c, scan_in[c])
            for c in range(CHUNKS):
                load(m.k_stack, m.k_dram, 0, c, k_in[c])
            ahead = sum(x[0] == "rows" for x in first)
            run(0, first, 0, 0, False)
            with sp.Fori(0, QUADS - 1) as q:
                run(q, order, q * scans + scans_first, q * CHUNKS + ahead, True)
            run(QUADS - 1, order_last, (QUADS - 1) * scans + scans_first, (QUADS - 1) * CHUNKS + ahead, False)
            for half in range(2):
                sp.wait_ge(out_done[half], 16 * QUADS * CHUNKS // 2)


def finish_attention(nc, m, n, layer=None):
    dst = m.x if layer is None else m.z
    with ExitStack() as ctx:
        def sb(name, shape, dt=F32):
            return ctx.enter_context(nc.sbuf_tensor(name + n, shape, dt))

        sem = m.phase_semaphores()

        y = sb("f_y", [P, CHUNKS, CH])
        sums = sb("f_sums", [P, CHUNKS, CH])
        ps = ctx.enter_context(nc.psum_tensor("f_ps" + n, [P, CHUNKS, TPC, D], F32))
        loaded = [sem(f"f_loaded{c}") for c in range(CHUNKS)]
        y_ready, projected, dve_steps = sem("f_y_ready"), sem("f_projected"), sem("f_dve_steps")
        block = ctx.enter_context(nc.Block())

        @block.gpsimd
        def _(pool):
            m.clear_previous(pool)

        @block.sync
        def _(sp):
            for c in range(CHUNKS):
                q = slice(c * CH, (c + 1) * CH)
                sp.dma_start(y[:, c, :], m.o_dram[:, 0:HD, q]).then_inc(loaded[c], 16)
                sp.dma_start(sums[:, c, :], m.o_dram[:, HD:HD + 1, q].broadcast_to([HEADS, HD, CH]))\
                    .then_inc(loaded[c], 16)

        @block.vector
        def _(dve):
            step = Steps(dve, dve_steps)
            for c in range(CHUNKS):
                dve.wait_ge(loaded[c], 32)
                step(nc.vector.reciprocal(sums[:, c, :], sums[:, c, :]))
                nc.vector.tensor_tensor(y[:, c, :], y[:, c, :], sums[:, c, :], ALU.mult).then_inc(y_ready, 1)
            for c in range(CHUNKS):
                tiles = dst[:, c * TPC:(c + 1) * TPC, :]
                if layer is not None:
                    step(nc.vector.tensor_tensor(tiles, tiles, m.bo[:, layer:layer + 1, :]
                                                 .broadcast_to([P, TPC, D]), ALU.add))
                dve.wait_ge(projected, c + 1)
                step(nc.vector.tensor_tensor(tiles, tiles, ps[:, c, :, :], ALU.add))

        @block.tensor
        def _(pe):
            right = m.ident[:, :] if layer is None else m.w_att[:, layer, 3, :]
            for c in range(CHUNKS):
                pe.wait_ge(y_ready, c + 1)
                for r in range(TPC):
                    last = nc.tensor.matmul(ps[:, c, r, :], y[:, c, r * P:(r + 1) * P], right, start=True, stop=True)
                last.then_inc(projected, 1)


def top2(nc, step, t, logits, rank):
    full = list(logits.shape)
    v = nc.vector

    def pick(values, onehot, top):
        step(v.tensor_reduce(t[top], values, AXIS_X, ALU.max))
        step(v.tensor_tensor(t["s"], values, t[top].broadcast_to(full), ALU.is_equal))
        step(v.tensor_tensor(t["s"], t["s"], rank.broadcast_to(full), ALU.mult))
        step(v.tensor_reduce(t["r"], t["s"], AXIS_X, ALU.max))
        step(v.tensor_tensor(t[onehot], t["s"], t["r"].broadcast_to(full), ALU.is_equal))

    pick(logits, "h1", "m1")
    step(v.scalar_tensor_tensor(t["l2"], t["h1"], -3e38, logits, ALU.mult, ALU.add))
    pick(t["l2"], "h2", "m2")
    return v.tensor_tensor(t["d"], t["m2"], t["m1"], ALU.subtract)


def top2_combine(nc, step, t, full):
    v = nc.vector
    step(v.tensor_scalar(t["r"], t["ed"], 1.0, None, ALU.add))
    step(v.reciprocal(t["r"], t["r"]))
    step(v.tensor_tensor(t["h2"], t["h2"], t["ed"].broadcast_to(full), ALU.mult))
    step(v.tensor_tensor(t["s"], t["h1"], t["h2"], ALU.add))
    return v.tensor_tensor(t["cw"], t["s"], t["r"].broadcast_to(full), ALU.mult)


TOP2_STEPS = 11 + 4


def router_tiles(nc, ctx, n, parts, groups):
    t = {}
    for name in ("s", "h1", "h2", "l2", "cw", "lg"):
        t[name] = ctx.enter_context(nc.sbuf_tensor(f"t_{name}{n}", [parts, groups, E], F32))[:, :, :]
    for name in ("m1", "m2", "r", "d", "ed"):
        t[name] = ctx.enter_context(nc.sbuf_tensor(f"t_{name}{n}", [parts, groups, 1], F32))[:, :, :]
    return t


def experts(nc, m, n, layer, last):
    by_token = layer == 0
    n_exp = E if by_token else TOPK
    with ExitStack() as ctx:
        def sb(name, shape, dt=F32):
            return ctx.enter_context(nc.sbuf_tensor(name + n, shape, dt))

        sem = m.phase_semaphores()

        st = sb("e_st", [P, TILES, 6])
        tmp = sb("e_tmp", [P, 3, TILES])
        hn = sb("e_hn", [P, TPC, D])
        h_t = sb("e_h_t", [P, CH])
        hidden = sb("e_hidden", [P, 2, FB, CH])
        cw_t = sb("e_cw_t", [E, CH])
        if by_token:
            t = router_tiles(nc, ctx, n, P, TPC)
            w1, w2 = m.w1, m.w2
        else:
            t = router_tiles(nc, ctx, n, 1, 1)
            w1, w2 = sb("e_w1", [P, TOPK, FF]), sb("e_w2", [P, TOPK, FB, D])
            b1 = sb("e_b1", [P, TOPK, FB])
            sums = sb("e_sums", [P, CHUNKS, 1])
            mean_h = sb("e_mean_h", [P, 1])
            ids = sb("e_ids", [1, TOPK])
            pair = sb("e_pair", [1, TOPK])
            pair_rows = sb("e_pair_rows", [P, TOPK])
        ps_turn = ctx.enter_context(nc.psum_tensor("e_ps_turn" + n, [P, CH], F32))
        ps_h = ctx.enter_context(nc.psum_tensor("e_ps_h" + n, [P, FB, CH], F32))
        ps_y = ctx.enter_context(nc.psum_tensor("e_ps_y" + n, [P, 2, TPC, D], F32))
        ps_b2 = ctx.enter_context(nc.psum_tensor("e_ps_b2" + n, [P, TPC, D], F32))
        hn_ready, turned, h_ready, logits_ready = (sem(s) for s in ("e_hn_ready", "e_turned", "e_h_ready", "e_logits"))
        top_ready, exp_ready, cw_ready, cw_turned = (sem(s) for s in ("e_top", "e_exp", "e_cw", "e_cw_turned"))
        cwt_ready, b2_ready, b2_added = (sem(s) for s in ("e_cwt", "e_b2_ready", "e_b2_added"))
        up_ready, gelu_ready, down_ready, added = (sem(s) for s in ("e_up", "e_gelu", "e_down", "e_added"))
        dve_steps, weights_in, summed, mean_ready = (sem(s) for s in ("e_dve", "e_weights_in", "e_summed", "e_mean"))
        pair_ready, pair_spread = sem("e_pair_ready"), sem("e_pair_spread")
        block = ctx.enter_context(nc.Block())
        ln_w = m.vecs[:, LN2_W + layer:LN2_W + layer + 1]
        ln_b = m.vecs[:, LN2_B + layer:LN2_B + layer + 1]
        passes = 1 if by_token else 2
        full = [P, TPC, E]
        var_ready, rstd_ready = sem("e_var_ready"), sem("e_rstd_ready")

        @block.gpsimd
        def _(pool):
            m.clear_previous(pool)
            inverse_root(nc, pool, m, m.rstd[:, :], tmp[:, 0, :], var_ready, rstd_ready, 1)

        @block.vector
        def _(dve):
            step = Steps(dve, dve_steps)
            token_stats(nc, step, m.z, st, m, tmp, var_ready, rstd_ready, 1)

            def normalise_chunk(i):
                for r in range(TPC):
                    at = bass.ds(i * TPC + r, 1)
                    last_ = nc.vector.tensor_scalar(hn[:, r:r + 1, :], m.z[:, at, :], m.mean[:, at], m.rstd[:, at],
                                                    ALU.subtract, ALU.mult)
                last_.then_inc(hn_ready, 1)

            if not by_token:
                with dve.Fori(0, CHUNKS) as i:
                    dve.wait_ge(turned, i)
                    normalise_chunk(i)
                dve.wait_ge(summed, CHUNKS)
                step(nc.vector.tensor_reduce(mean_h[:, :], sums[:, :, 0], AXIS_X, ALU.add))
                nc.vector.tensor_scalar(mean_h[:, :], mean_h[:, :], 1.0 / S, None, ALU.mult).then_inc(mean_ready, 1)
                dve.wait_ge(logits_ready, 1)
                step(nc.vector.tensor_tensor(t["lg"], ps_b2[0:1, 0:1, 0:E], m.gate_b[0:1, layer:layer + 1, :], ALU.add))
                top2(nc, step, t, t["lg"], m.rank[0:1, :].unsqueeze(1)).then_inc(top_ready, 1)
                dve.wait_ge(exp_ready, 1)
                for k, onehot in enumerate(("h1", "h2")):
                    step(nc.vector.tensor_tensor(t["s"], t[onehot], m.rank[0:1, :].unsqueeze(1), ALU.mult))
                    step(nc.vector.tensor_reduce(ids[:, k:k + 1], t["s"], AXIS_X, ALU.add))
                step(nc.vector.tensor_scalar(ids[:, :], ids[:, :], -1.0, float(E), ALU.mult, ALU.add))
                step(nc.vector.tensor_copy(m.ids_int[:, :], ids[:, :]))
                step(top2_combine(nc, step, t, [1, 1, E]))
                step(nc.vector.tensor_copy(pair[:, 0:1], t["r"][:, :, 0]))
                nc.vector.tensor_tensor(pair[:, 1:2], t["ed"][:, :, 0], t["r"][:, :, 0], ALU.mult)\
                    .then_inc(pair_ready, 1)
                dve.wait_ge(pair_spread, 1)
                step(nc.vector.tensor_copy(pair_rows[:, :], ps_b2[:, 0, E:E + TOPK]))
            before = step.n
            per_round = 1 + TOP2_STEPS if by_token else 0
            with dve.Fori(0, CHUNKS) as i:
                step = Steps(dve, dve_steps, i * per_round + before)
                done = CHUNKS if not by_token else 0
                dve.wait_ge(turned, i + done)
                normalise_chunk(i)
                if by_token:
                    dve.wait_ge(logits_ready, i + 1)
                    step(nc.vector.tensor_tensor(t["lg"], ps_turn[:, 0:TPC * E].rearrange("p (t e) -> p t e", e=E),
                                                 m.gate_b[:, layer:layer + 1, :].broadcast_to(full), ALU.add))
                    top2(nc, step, t, t["lg"], m.rank[:, :].unsqueeze(1)).then_inc(top_ready, 1)
                    dve.wait_ge(exp_ready, i + 1)
                    top2_combine(nc, step, t, full).then_inc(cw_ready, 1)
                    dve.wait_ge(cw_ready, i + 1)
                dve.wait_ge(b2_ready, i + 1)
                nc.vector.tensor_tensor(m.z[:, token_tiles(i), :], m.z[:, token_tiles(i), :], ps_b2[:, :, :], ALU.add)\
                    .then_inc(b2_added, 1)
                dve.wait_ge(b2_added, i + 1)
                for e in range(n_exp):
                    dve.wait_ge(down_ready, n_exp * i + e + 1)
                    if e:
                        dve.wait_ge(added, n_exp * i + e)
                    for r in range(TPC):
                        at = bass.ds(i * TPC + r, 1)
                        weight = t["cw"][:, r, e:e + 1] if by_token else pair_rows[:, e:e + 1]
                        last_ = nc.vector.scalar_tensor_tensor(m.z[:, at, :], ps_y[:, e % 2, r:r + 1, :], weight,
                                                               m.z[:, at, :], ALU.mult, ALU.add)
                    last_.then_inc(added, 1)
                dve.wait_ge(added, n_exp * (i + 1))
                if last:
                    nc.vector.tensor_tensor(m.x[:, token_tiles(i), :], m.x[:, token_tiles(i), :],
                                            m.z[:, token_tiles(i), :], ALU.add)
                assert step.n == per_round, step.n

        @block.tensor
        def _(pe):
            def turn(i, k):
                pe.wait_ge(hn_ready, i + 1)
                for r in range(TPC):
                    last_ = nc.tensor.transpose(ps_turn[:, r * P:(r + 1) * P], hn[:, r, :], m.ident[:, :])
                last_.then_inc(turned, 1)

            if not by_token:
                with pe.Fori(0, CHUNKS) as i:
                    pe.wait_ge(summed, i)
                    turn(i, 0)
                pe.wait_ge(mean_ready, 1)
                nc.tensor.matmul(ps_b2[0:1, 0, 0:E], mean_h[:, :], m.gate_w[:, layer, :], start=True, stop=True)\
                    .then_inc(logits_ready, 1)
                pe.wait_ge(pair_ready, 1)
                nc.tensor.matmul(ps_b2[:, 0, E:E + TOPK], m.ones[0:1, :], pair[:, :], start=True, stop=True)\
                    .then_inc(pair_spread, 1)
                for r in range(TPC):
                    last_ = nc.tensor.matmul(ps_turn[0:E, r * P:(r + 1) * P], t["cw"][:, 0, :], m.ones[0:1, :],
                                             start=True, stop=True)
                last_.then_inc(cw_turned, 1)
                pe.wait_ge(cwt_ready, 1)
                pe.wait_ge(weights_in, 16 * 3 * TOPK)
            else:
                pe.wait_ge(m.expert_weights_in, 16 * (E + 1))
            with pe.Fori(0, CHUNKS) as i:
                turn(i + (0 if by_token else CHUNKS), 0)
                pe.wait_ge(h_ready, i + 1)
                if by_token:
                    for r in range(TPC):
                        last_ = nc.tensor.matmul(ps_turn[:, r * E:(r + 1) * E], h_t[:, r * P:(r + 1) * P],
                                                 m.gate_w[:, layer, :], start=True, stop=True)
                    last_.then_inc(logits_ready, 1)

                def up(e):
                    for b in range(FB):
                        pe.wait_ge(gelu_ready, FB * (n_exp * i + e) + b - FB + 1 + FB)
                        nc.tensor.matmul(ps_h[:, b, :], w1[:, e, b * P:(b + 1) * P], h_t[:, :],
                                         start=True, stop=True).then_inc(up_ready, 1)

                up(0)
                if by_token:
                    pe.wait_ge(cw_ready, i + 1)
                    for r in range(TPC):
                        last_ = nc.tensor.transpose(ps_turn[0:E, r * P:(r + 1) * P], t["cw"][:, r, :], m.ident[:, :])
                    last_.then_inc(cw_turned, 1)
                    pe.wait_ge(cwt_ready, i + 1)
                pe.wait_ge(b2_added, i)
                for r in range(TPC):
                    last_ = nc.tensor.matmul(ps_b2[:, r, :], cw_t[:, r * P:(r + 1) * P], m.b2[:, layer, :],
                                             start=True, stop=True)
                last_.then_inc(b2_ready, 1)
                for e in range(n_exp):
                    if e + 1 < n_exp:
                        up(e + 1)
                    pe.wait_ge(gelu_ready, FB * (n_exp * i + e + 1) + FB)
                    pe.wait_ge(added, n_exp * i + (e - 1 if e >= 2 else 0))
                    for r in range(TPC):
                        for b in range(FB):
                            last_ = nc.tensor.matmul(ps_y[:, e % 2, r, :], hidden[:, e % 2, b, r * P:(r + 1) * P],
                                                     w2[:, e, b, :], start=b == 0, stop=b == FB - 1)
                    last_.then_inc(down_ready, 1)

        @block.scalar
        def _(act):
            act.sem_inc(gelu_ready, FB)
            if not by_token:
                with act.Fori(0, CHUNKS) as i:
                    act.wait_ge(turned, i + 1)
                    nc.scalar.activation(h_t[:, :], ps_turn[:, :], ACT.Identity, scale=ln_w, bias=ln_b,
                                         accum_out=sums[:, bass.ds(i, 1), 0]).then_inc(summed, 1)
                act.wait_ge(top_ready, 1)
                nc.scalar.activation(t["ed"], t["d"], ACT.Exp).then_inc(exp_ready, 1)
                act.wait_ge(cw_turned, 1)
                nc.scalar.activation(cw_t[:, :], ps_turn[0:E, :], ACT.Copy).then_inc(cwt_ready, 1)
            with act.Fori(0, CHUNKS) as i:
                act.wait_ge(turned, i + 1 + (0 if by_token else CHUNKS))
                act.wait_ge(down_ready, n_exp * i)
                nc.scalar.activation(h_t[:, :], ps_turn[:, :], ACT.Identity, scale=ln_w, bias=ln_b)\
                    .then_inc(h_ready, 1)
                if by_token:
                    act.wait_ge(top_ready, i + 1)
                    nc.scalar.activation(t["ed"], t["d"], ACT.Exp).then_inc(exp_ready, 1)

                def gelu(e):
                    for b in range(FB):
                        act.wait_ge(up_ready, FB * (n_exp * i + e) + b + 1)
                        if e >= 2 and b == 0:
                            act.wait_ge(down_ready, n_exp * i + e - 1)
                        bias = m.vecs[:, E_B1 + FB * e + b:E_B1 + FB * e + b + 1] if by_token else b1[:, e, b:b + 1]
                        nc.scalar.activation(hidden[:, e % 2, b, :], ps_h[:, b, :], ACT.Gelu, bias=bias)\
                            .then_inc(gelu_ready, 1)

                for e in range(n_exp):
                    gelu(e)
                    if e == 0 and by_token:
                        act.wait_ge(cw_turned, i + 1)
                        nc.scalar.activation(cw_t[:, :], ps_turn[0:E, :], ACT.Copy).then_inc(cwt_ready, 1)

        if not by_token:
            @block.sync
            def _(sp):
                sp.wait_ge(pair_ready, 1)
                for k in range(TOPK):
                    e = sp.value_load(m.ids_int[0:1, k:k + 1], min_val=0, max_val=E - 1)
                    one = bass.ds(e, 1)
                    sp.dma_start(w1[:, k, :], m.ins["L0_ffn_e_w1"][layer, one].rearrange("e p f -> (e p) f"))\
                        .then_inc(weights_in, 16)
                    sp.dma_start(w2[:, k, :, :], m.ins["L0_ffn_e_w2"][layer, one]
                                 .rearrange("e (i p) d -> p (e i) d", p=P)).then_inc(weights_in, 16)
                    sp.dma_start(b1[:, k, :], m.ins["L0_ffn_e_b1"][layer, one].rearrange("e (i p) -> p (e i)", p=P),
                                 allow_slow_non_contiguous=True)\
                        .then_inc(weights_in, 16)
                sp.wait_ge(weights_in, 16 * 3 * TOPK)


def write_out(nc, m, out):
    with ExitStack() as ctx:
        written = ctx.enter_context(nc.semaphore("written"))
        block = ctx.enter_context(nc.Block())

        @block.sync
        def _(sp):
            sp.dma_start(out[0].rearrange("(t p) d -> p t d", p=P), m.x[:, :, :]).then_inc(written, 16)
            sp.wait_ge(written, 16)


def feed_forward(nc, m, n):
    for layer in range(LAYERS):
        tag = f"{n}{layer}"
        project_qkv(nc, m, tag, first=layer == 0, layer=layer)
        attention_heads(nc, m, tag, causal=True)
        finish_attention(nc, m, tag, layer)
        experts(nc, m, tag, layer, last=layer == LAYERS - 1)


def build(nc, ins, out):
    with ExitStack() as ctx:
        m = Memory(nc, ctx, ins)
        set_up(nc, m, "s")
        stage_a(nc, m, "a")
        feed_forward(nc, m, "f")
        project_qkv(nc, m, "b", layer=None)
        attention_heads(nc, m, "b", causal=False)
        finish_attention(nc, m, "b")
        feed_forward(nc, m, "g")
        write_out(nc, m, out)


def kernel(**inputs):
    import concourse.bacc as bacc
    from concourse.bass_utils import run_bass_kernel_spmd

    nc = bacc.Bacc("TRN2", target_bir_lowering=False, num_devices=1)
    arrays, ins = {}, {}
    for name, value in inputs.items():
        a = np.ascontiguousarray(value)
        arrays["in_" + name] = a
        ins[name] = nc.dram_tensor("in_" + name, a.shape, mybir.dt.from_np(a.dtype), kind="ExternalInput").ap()
    out = nc.dram_tensor("out", [1, S, D], F32, kind="ExternalOutput").ap()
    build(nc, ins, out)
    result = run_bass_kernel_spmd(nc, [arrays], core_ids=[0])
    return result.results[0]["out"]
```

```python
import numpy as np
import concourse.bass as bass
from concourse import mybir
from contextlib import ExitStack

F32 = mybir.dt.float32
BF16 = mybir.dt.bfloat16
I32 = mybir.dt.int32
F32R = mybir.dt.float32r
ALU = mybir.AluOpType
ACT = mybir.ActivationFunctionType
AXIS_X = mybir.AxisListType.X

P = 128
D = 128
S = 2048
TILES = S // P
CH = 512
CHUNKS = S // CH
TPC = CH // P
HEADS, HD = 16, 8
QUAD = 4
QUADS = HEADS // QUAD
E, FF = 8, 512
FB = FF // P
TOPK = 2
LAYERS = 2
LN_EPS = 1e-5
RMS_EPS = 1.1920929e-07
MASKED = -1e30
SOFTMAX_SCALE = HD ** -0.5

Q_PARTS = [0, 0, 0, 1, 1, 2]
K_PARTS = [1, 0, 2, 0, 1, 0]
STACK = len(Q_PARTS) * HD
SHIFT_ROW = 64

LN1_W, LN1_B, LN2_W, LN2_B, BQ, BK = (LAYERS * n for n in range(6))
B_BQ, B_BK = LAYERS * 6, LAYERS * 6 + 1
E_B1 = LAYERS * 6 + 2
N_VEC = E_B1 + E * FB


class Steps:

    def __init__(self, engine, sem, base=0):
        self.engine, self.sem, self.base, self.n = engine, sem, base, 0

    def __call__(self, instruction):
        self.n += 1
        instruction.then_inc(self.sem, 1)
        self.engine.wait_ge(self.sem, self.base + self.n)


def by_dim(ap):
    return ap.rearrange("p (h d) -> p d h", d=HD)


def token_tiles(i, n=TPC):
    return bass.ds(i * n, n)


class Memory:

    def phase_semaphores(self):
        self.previous, self.current = self.current, []

        def sem(name):
            if name not in self.named:
                self.named[name] = self.ctx.enter_context(self.nc.semaphore(name))
            self.current.append(self.named[name])
            return self.named[name]

        return sem

    def clear_previous(self, pool):
        for s in self.previous:
            pool.sem_clear(s)

    def __init__(self, nc, ctx, ins):
        self.nc, self.ctx, self.named, self.current, self.previous = nc, ctx, {}, [], []

        def sb(name, shape, dt=F32):
            return ctx.enter_context(nc.sbuf_tensor(name, shape, dt))

        self.ins = ins
        self.x = sb("x_tok", [P, TILES, D])
        self.z = sb("z_tok", [P, TILES, D])
        self.mean = sb("mean", [P, TILES])
        self.rstd = sb("rstd", [P, TILES])
        self.ident = sb("ident", [P, P])
        self.ident_bf = sb("ident_bf", [P, P], BF16)
        self.hide_right = sb("hide_right", [P, P], BF16)
        self.hide_left = sb("hide_left", [P, P], BF16)
        self.upto = sb("upto", [P, P])
        self.ones = sb("ones", [P, P])
        self.rank = sb("rank", [P, E])
        self.neg_half = sb("neg_half", [P, TILES])
        self.w_qkv = sb("w_qkv_t", [P, 3 * D])
        self.w_swiglu = sb("w_swiglu_t", [P, 2 * D])
        self.w_out = sb("w_out_t", [P, D])
        self.vecs = sb("vecs", [P, N_VEC])
        self.vecs_dh = sb("vecs_dh", [P, N_VEC])
        self.w_att = sb("w_att", [P, LAYERS, 4, D])
        self.bv = sb("bv_rows", [P, LAYERS + 1, D])
        self.bo = sb("bo_rows", [P, LAYERS, D])
        self.w_b = sb("w_b", [P, 3, D])
        self.mix_dh = sb("mix_dh", [P, P])
        self.w_dh = sb("w_dh", [P, LAYERS, 2, D])
        self.gate_w = sb("gate_w", [P, LAYERS, E])
        self.gate_b = sb("gate_b", [P, LAYERS, E])
        self.b2 = sb("b2", [E, LAYERS, D])
        self.gate_hi = sb("gate_hi", [P, LAYERS, E], F32R)
        self.gate_lo = sb("gate_lo", [P, LAYERS, E], F32R)
        self.w1_hi = sb("w1_hi", [P, E, FF], F32R)
        self.w1_lo = sb("w1_lo", [P, E, FF], F32R)
        self.w2 = sb("w2", [P, E, FB, D])
        self.q_stack = sb("q_stack", [P, CHUNKS, QUAD, CH], BF16)
        self.k_scan = sb("k_scan", [P, QUAD, S], BF16)
        self.k_stack = sb("k_stack", [P, QUAD, S], BF16)
        self.v_all = sb("v_all", [P, TILES, D])
        self.v_quad = sb("v_quad", [P, TILES, QUAD, 32])
        self.ids_int = sb("ids_int", [1, TOPK], I32)
        self.w2_in = ctx.enter_context(nc.semaphore("w2_in"))
        self.weights_in = [ctx.enter_context(nc.semaphore(f"weights_in{k}")) for k in range(2)]
        self.weights_hi = ctx.enter_context(nc.semaphore("weights_hi"))
        self.weights_split = ctx.enter_context(nc.semaphore("weights_split"))
        self.q_dram = nc.dram_tensor("q_parts", [STACK, HEADS, S], BF16, kind="Internal").ap()
        self.k_dram = nc.dram_tensor("k_parts", [STACK, HEADS, S], BF16, kind="Internal").ap()
        self.o_dram = nc.dram_tensor("attended", [HEADS, 32, S], F32, kind="Internal").ap()


REST_LOADS = 19


def set_up(nc, m, n):
    ins = m.ins
    with ExitStack() as ctx:
        raw = ctx.enter_context(nc.sbuf_tensor("raw_weights", [P, 6, D], F32))
        rows = ctx.enter_context(nc.sbuf_tensor("vector_rows", [N_VEC, D], F32))
        rows_dh = ctx.enter_context(nc.sbuf_tensor("vector_rows_dh", [N_VEC, D], F32))
        mix = ctx.enter_context(nc.sbuf_tensor("mix", [P, P], F32))
        ps = ctx.enter_context(nc.psum_tensor("setup_ps", [P, 2, 512], F32))
        sem = m.phase_semaphores()
        raw_in, turned, rest_in, built = sem("s_raw_in"), sem("s_turned"), sem("s_rest_in"), sem("s_built")
        mix_zero, v_zero, rows_turned = sem("s_mix_zero"), sem("s_v_zero"), sem("s_rows_turned")
        block = ctx.enter_context(nc.Block())

        def layer_rows(name, at):
            return rows[at:at + LAYERS, :], ins["L0_ffn_" + name]

        @block.sync
        def _(sp):
            loads = [(raw[:, 0:3, :], ins["L0_attn_a_w_qkv"].rearrange("(g p) d -> p g d", p=P)),
                     (raw[:, 3:5, :], ins["L0_attn_a_w_swiglu"].rearrange("(g p) d -> p g d", p=P)),
                     (raw[:, 5, :], ins["L0_attn_a_w_out"]),
                     layer_rows("ln1_w", LN1_W), layer_rows("ln1_b", LN1_B), layer_rows("ln2_w", LN2_W),
                     layer_rows("ln2_b", LN2_B), layer_rows("bq", BQ), layer_rows("bk", BK),
                     (rows[B_BQ:B_BQ + 1, :], ins["L0_attn_b_bq"].rearrange("(a d) -> a d", a=1)),
                     (rows[B_BK:B_BK + 1, :], ins["L0_attn_b_bk"].rearrange("(a d) -> a d", a=1)),
                     (rows[E_B1:N_VEC, :], ins["L0_ffn_e_b1"][0].rearrange("e (i p) -> (e i) p", p=P))]
            for dst, src in loads:
                sp.dma_start(dst, src).then_inc(raw_in, 16)
            rest = [(m.x[:, :, :], ins["L0_attn_a_x"][0].rearrange("(t p) d -> p t d", p=P))]
            for i, name in enumerate(("wq", "wk", "wv", "wo")):
                rest.append((m.w_att[:, :, i, :], ins["L0_ffn_" + name].rearrange("l p d -> p l d")))
            for i, name in enumerate(("Wq", "Wk", "Wv")):
                rest.append((m.w_b[:, i, :], ins["L0_attn_b_" + name]))
            for layer in range(LAYERS):
                rest.append((m.bv[:, layer, :], ins["L0_ffn_bv"][layer].partition_broadcast(P)))
                rest.append((m.bo[:, layer, :], ins["L0_ffn_bo"][layer].partition_broadcast(P)))
                rest.append((m.gate_b[:, layer, :], ins["L0_ffn_gate_b"][layer].partition_broadcast(P)))
                rest.append((m.gate_w[:, layer, :], ins["L0_ffn_gate_w"][layer]))
                rest.append((m.b2[:, layer, :], ins["L0_ffn_e_b2"][layer]))
            rest.append((m.bv[:, LAYERS, :], ins["L0_attn_b_bv"].partition_broadcast(P)))
            for dst, src in rest:
                sp.dma_start(dst, src).then_inc(rest_in, 16)
            sp.wait_ge(mix_zero, 1)
            for h in range(HEADS):
                sp.dma_start(mix[HD * h:HD * h + HD, HD * h:HD * h + HD], ins["L0_attn_b_Wp"]).then_inc(rest_in, 16)
            assert len(rest) == REST_LOADS
            for e in range(E):
                sp.dma_start(m.w2[:, e, :, :], ins["L0_ffn_e_w2"][0, e].rearrange("(i p) d -> p i d", p=P))\
                    .then_inc(m.w2_in, 16)
            sp.wait_ge(rest_in, 16 * (REST_LOADS + HEADS))

        @block.gpsimd
        def _(pool):
            m.clear_previous(pool)
            nc.gpsimd.memset(m.ident[:, :], 0.0).then_inc(built, 1)
            nc.gpsimd.memset(m.ident_bf[:, :], 0.0).then_inc(built, 1)
            nc.gpsimd.memset(m.hide_right[:, :], 0.0).then_inc(built, 1)
            nc.gpsimd.memset(m.hide_left[:, :], 0.0).then_inc(built, 1)
            nc.gpsimd.memset(m.upto[:, :], 1.0).then_inc(built, 1)
            nc.gpsimd.memset(m.ones[:, :], 1.0).then_inc(built, 1)
            pool.wait_ge(built, 6)

            def select(t, op, fill, column, row):
                nc.gpsimd.affine_select(out=t[:, :], in_=t[:, :], compare_op=op, fill=fill, base=0,
                                        pattern=[[column, P]], channel_multiplier=row).then_inc(built, 1)

            select(m.ident, ALU.not_equal, 1.0, -1, 1)
            select(m.ident_bf, ALU.not_equal, 1.0, -1, 1)
            select(m.hide_right, ALU.is_ge, MASKED, -1, 1)
            select(m.hide_left, ALU.is_ge, MASKED, 1, -1)
            select(m.upto, ALU.is_ge, 0.0, 1, -1)
            for e in range(E):
                nc.gpsimd.memset(m.rank[:, e:e + 1], float(E - e))
            nc.gpsimd.memset(m.neg_half[:, :], -0.5)
            nc.gpsimd.memset(m.v_quad[:, :, :, :], 0.0).then_inc(v_zero, 1)
            pool.wait_ge(v_zero, 1)
            nc.gpsimd.memset(m.neg_half[:, :], -0.5)
            nc.gpsimd.memset(m.v_quad[:, :, :, HD:HD + 1], 1.0)

        @block.vector
        def _(dve):
            nc.vector.memset(mix[:, :], 0.0).then_inc(mix_zero, 1)
            nc.vector.memset(m.q_stack[:, :, :, :].bitcast(F32), 0.0).then_inc(mix_zero, 1)
            for stack in (m.k_scan, m.k_stack):
                nc.vector.memset(stack[:, :, :].bitcast(F32), 0.0).then_inc(mix_zero, 1)
            dve.wait_ge(mix_zero, 4)
            dve.wait_ge(rest_in, 16 * (REST_LOADS + HEADS))
            nc.vector.tensor_copy(m.gate_hi[:, :, :], m.gate_w[:, :, :]).then_inc(mix_zero, 1)
            dve.wait_ge(mix_zero, 5)
            nc.vector.tensor_tensor(m.gate_lo[:, :, :], m.gate_w[:, :, :], m.gate_hi[:, :, :].bitcast(F32),
                                    ALU.subtract)
            nc.vector.memset(m.k_stack[SHIFT_ROW:SHIFT_ROW + 1, :, :], 1.0)

        @block.tensor
        def _(pe):
            pe.wait_ge(built, 7)
            pe.wait_ge(raw_in, 16 * 12)
            for g in range(6):
                nc.tensor.transpose(ps[:, g // 4, (g % 4) * P:(g % 4 + 1) * P], raw[:, g, :], m.ident[:, :])\
                    .then_inc(turned, 1)
            nc.tensor.transpose(ps[:, 1, 256:256 + N_VEC], rows[:, :], m.ident[0:N_VEC, 0:N_VEC]).then_inc(turned, 1)
            pe.wait_ge(rows_turned, 1)
            nc.tensor.transpose(ps[:, 1, 320:320 + N_VEC], rows_dh[:, :], m.ident[0:N_VEC, 0:N_VEC])\
                .then_inc(turned, 1)

        @block.scalar
        def _(act):
            act.wait_ge(raw_in, 16 * 12)
            nc.scalar.activation(rows_dh[:, :].rearrange("p (d h) -> p d h", d=HD), by_dim(rows[:, :]), ACT.Copy)\
                .then_inc(rows_turned, 1)
            act.wait_ge(turned, 8)
            nc.scalar.activation(m.w_qkv[:, :], ps[:, 0, 0:3 * P], ACT.Copy)
            nc.scalar.activation(m.w_swiglu[:, 0:P], ps[:, 0, 3 * P:4 * P], ACT.Copy)
            nc.scalar.activation(m.w_swiglu[:, P:2 * P], ps[:, 1, 0:P], ACT.Copy)
            nc.scalar.activation(m.w_out[:, :], ps[:, 1, P:2 * P], ACT.Copy)
            nc.scalar.activation(m.vecs[:, :], ps[:, 1, 256:256 + N_VEC], ACT.Copy)
            nc.scalar.activation(m.vecs_dh[:, :], ps[:, 1, 320:320 + N_VEC], ACT.Copy)
            act.wait_ge(rest_in, 16 * (REST_LOADS + HEADS))
            for layer in range(LAYERS):
                for k in range(2):
                    nc.scalar.activation(m.w_dh[:, layer, k, :].rearrange("p (d h) -> p d h", d=HD),
                                         by_dim(m.w_att[:, layer, k, :]), ACT.Copy)
            nc.scalar.activation(m.mix_dh[:, :].rearrange("p (d h) -> p d h", d=HD), by_dim(mix[:, :]), ACT.Copy)


def row_moments(nc, step, st, mean, var, t1, t2, eps):
    step(nc.vector.tensor_tensor(t1, st[:, :, 1], st[:, :, 4], ALU.subtract))
    step(nc.vector.tensor_tensor(mean, st[:, :, 1], st[:, :, 4], ALU.add))
    step(nc.vector.tensor_tensor(t2, st[:, :, 2], st[:, :, 5], ALU.add))
    step(nc.vector.tensor_scalar(t2, t2, 1.0 / D, None, ALU.mult))
    step(nc.vector.scalar_tensor_tensor(t1, t1, 0.25, t1, ALU.mult, ALU.mult))
    step(nc.vector.tensor_scalar(mean, mean, 0.5, None, ALU.mult))
    return nc.vector.scalar_tensor_tensor(var, t1, eps, t2, ALU.add, ALU.add)


def inverse_root(nc, pool, m, out, in_, in_ready, out_ready, count):
    pool.wait_ge(in_ready, count)
    nc.gpsimd.tensor_tensor(out, in_, m.neg_half[:, 0:out.shape[-1]], ALU.pow).then_inc(out_ready, 1)


def token_stats(nc, step, src, st, m, tmp, var_ready, rstd_ready, count):
    for t in range(TILES):
        last = nc.vector.bn_stats(st[:, t, :], src[:, t, :])
    step(last)
    row_moments(nc, step, st, m.mean[:, :], tmp[:, 0, :], tmp[:, 1, :], tmp[:, 2, :], LN_EPS).then_inc(var_ready, 1)
    step.engine.wait_ge(rstd_ready, count)


def normalise(nc, step, dst, src, m):
    for t in range(TILES):
        last = nc.vector.tensor_scalar(dst[:, t, :], src[:, t, :], m.mean[:, t:t + 1], m.rstd[:, t:t + 1],
                                       ALU.subtract, ALU.mult)
    step(last)


def stage_a(nc, m, n):
    with ExitStack() as ctx:
        def sb(name, shape, dt=F32):
            return ctx.enter_context(nc.sbuf_tensor(name + n, shape, dt))

        sem = m.phase_semaphores()

        h = sb("a_h", [P, TILES, D])
        st = sb("a_st", [P, TILES, 6])
        st8 = sb("a_st8", [P, 2 * TPC, 6])
        tmp = sb("a_tmp", [P, 3, TILES])
        tmp8 = sb("a_tmp8", [P, 6, 2 * TPC])
        rh = sb("a_rh", [P, TILES])
        hn = sb("a_hn", [P, TPC, D])
        hn_t = sb("a_hn_t", [P, CH])
        wkv = sb("a_wkv", [P, TPC, 2 * D])
        eq = sb("a_eq", [P, TPC, D])
        run = sb("a_run", [P, TPC + 1, 2 * D])
        den = sb("a_den", [P, TPC, D])
        y = sb("a_y", [P, TPC, D])
        y_t = sb("a_y_t", [P, CH])
        eg = sb("a_eg", [P, TPC, D])
        ug = sb("a_ug", [P, TPC, D])
        g_t = sb("a_g_t", [P, CH])
        ps_qkv = ctx.enter_context(nc.psum_tensor("a_ps_qkv" + n, [P, TPC, 512], F32))
        ps_turn = ctx.enter_context(nc.psum_tensor("a_ps_turn" + n, [P, CH], F32))
        ps_sum = ctx.enter_context(nc.psum_tensor("a_ps_sum" + n, [P, TPC, 2 * D], F32))
        ps_out = ctx.enter_context(nc.psum_tensor("a_ps_out" + n, [P, TPC, D], F32))
        hn_ready, turned, turn_copied = sem("a_hn_ready"), sem("a_turned"), sem("a_turn_copied")
        qkv_ready, scales_ready, exps_ready = sem("a_qkv_ready"), sem("a_scales_ready"), sem("a_exps_ready")
        sums_in, summed, y_ready = sem("a_sums_in"), sem("a_summed"), sem("a_y_ready")
        uv_ready, neg_ready, gate_ready = sem("a_uv_ready"), sem("a_neg_ready"), sem("a_gate_ready")
        ug_ready, out_ready, dve_steps = sem("a_ug_ready"), sem("a_out_ready"), sem("a_dve_steps")
        var_ready, rstd_ready = sem("a_var_ready"), sem("a_rstd_ready")
        block = ctx.enter_context(nc.Block())
        uv = ps_qkv[:, 0:2, :].rearrange("p b (t f) -> p (b t) f", t=2)

        @block.vector
        def _(dve):
            step = Steps(dve, dve_steps)
            token_stats(nc, step, m.x, st, m, tmp, var_ready, rstd_ready, 1)
            normalise(nc, step, h, m.x, m)
            for t in range(TILES):
                last = nc.vector.bn_stats(st[:, t, :], h[:, t, :])
            step(last)
            step(row_moments(nc, step, st, m.mean[:, :], tmp[:, 0, :], tmp[:, 1, :], tmp[:, 2, :], RMS_EPS))
            step(nc.vector.tensor_tensor(tmp[:, 1, :], m.mean[:, :], m.mean[:, :], ALU.mult))
            nc.vector.tensor_tensor(tmp[:, 0, :], tmp[:, 0, :], tmp[:, 1, :], ALU.add).then_inc(var_ready, 1)
            dve.wait_ge(rstd_ready, 2)
            step(nc.vector.memset(run[:, 0, :], 0.0))
            before, per_round = step.n, 22
            with dve.Fori(0, CHUNKS) as i:
                step = Steps(dve, dve_steps, i * per_round + before)
                for r in range(TPC):
                    last = nc.vector.tensor_scalar(hn[:, r:r + 1, :], h[:, bass.ds(i * TPC + r, 1), :],
                                                   rh[:, bass.ds(i * TPC + r, 1)], None, ALU.mult)
                last.then_inc(hn_ready, 1)
                dve.wait_ge(qkv_ready, i + 1)
                for r in range(TPC):
                    for k in range(2):
                        last = nc.vector.bn_stats(st8[:, 2 * r + k, :], ps_qkv[:, r, k * D:(k + 1) * D])
                step(last)
                step(row_moments(nc, step, st8, tmp8[:, 0, :], tmp8[:, 1, :], tmp8[:, 2, :], tmp8[:, 3, :], RMS_EPS))
                step(nc.vector.tensor_tensor(tmp8[:, 2, :], tmp8[:, 0, :], tmp8[:, 0, :], ALU.mult))
                nc.vector.tensor_tensor(tmp8[:, 1, :], tmp8[:, 1, :], tmp8[:, 2, :], ALU.add).then_inc(var_ready, 1)
                dve.wait_ge(rstd_ready, i + 3)
                nc.vector.tensor_scalar(tmp8[:, 5, :], tmp8[:, 4, :], -1.0, None, ALU.mult).then_inc(scales_ready, 1)
                dve.wait_ge(exps_ready, i + 1)
                step(nc.vector.tensor_tensor(wkv[:, :, D:2 * D], wkv[:, :, 0:D], ps_qkv[:, :, 2 * D:3 * D], ALU.mult))
                for r in range(TPC):
                    step(nc.vector.tensor_tensor(run[:, r + 1, :], run[:, r, :], wkv[:, r, :], ALU.add))
                nc.vector.tensor_scalar(eq[:, :, :], eq[:, :, :], 1.0, None, ALU.add).then_inc(sums_in, 1)
                dve.wait_ge(sums_in, i + 1)
                dve.wait_ge(summed, i + 1)
                step(nc.vector.scalar_tensor_tensor(den[:, :, :], ps_sum[:, :, 0:D], 1e-6, eq[:, :, :],
                                                    ALU.add, ALU.mult))
                step(nc.vector.reciprocal(den[:, :, :], den[:, :, :]))
                nc.vector.tensor_tensor(y[:, :, :], ps_sum[:, :, D:2 * D], den[:, :, :], ALU.mult).then_inc(y_ready, 1)
                step(nc.vector.tensor_copy(run[:, 0, :], run[:, TPC, :]))
                dve.wait_ge(uv_ready, i + 1)
                nc.vector.tensor_scalar(eg[:, :, :], uv[:, :, D:2 * D], -1.0, 80.0, ALU.mult, ALU.min)\
                    .then_inc(neg_ready, 1)
                dve.wait_ge(gate_ready, i + 1)
                step(nc.vector.tensor_scalar(eg[:, :, :], eg[:, :, :], 1.0, None, ALU.add))
                step(nc.vector.reciprocal(eg[:, :, :], eg[:, :, :]))
                step(nc.vector.tensor_tensor(eg[:, :, :], eg[:, :, :], uv[:, :, D:2 * D], ALU.mult))
                nc.vector.tensor_tensor(ug[:, :, :], eg[:, :, :], uv[:, :, 0:D], ALU.mult).then_inc(ug_ready, 1)
                dve.wait_ge(out_ready, i + 1)
                step(nc.vector.tensor_tensor(den[:, :, :], ps_out[:, :, :], h[:, token_tiles(i), :], ALU.add))
                step(nc.vector.tensor_tensor(m.x[:, token_tiles(i), :], m.x[:, token_tiles(i), :], den[:, :, :],
                                             ALU.add))
                assert step.n == per_round, step.n

        @block.gpsimd
        def _(pool):
            m.clear_previous(pool)
            inverse_root(nc, pool, m, m.rstd[:, :], tmp[:, 0, :], var_ready, rstd_ready, 1)
            inverse_root(nc, pool, m, rh[:, :], tmp[:, 0, :], var_ready, rstd_ready, 2)
            with pool.Fori(0, CHUNKS) as i:
                inverse_root(nc, pool, m, tmp8[:, 4, :], tmp8[:, 1, :], var_ready, rstd_ready, i + 3)

        @block.tensor
        def _(pe):
            with pe.Fori(0, CHUNKS) as i:
                pe.wait_ge(hn_ready, i + 1)
                for r in range(TPC):
                    last = nc.tensor.transpose(ps_turn[:, r * P:(r + 1) * P], hn[:, r, :], m.ident[:, :])
                last.then_inc(turned, 1)
                pe.wait_ge(turn_copied, 3 * i + 1)
                for r in range(TPC):
                    last = nc.tensor.matmul(ps_qkv[:, r, 0:3 * D], hn_t[:, r * P:(r + 1) * P], m.w_qkv[:, :],
                                            start=True, stop=True)
                last.then_inc(qkv_ready, 1)
                pe.wait_ge(sums_in, i + 1)
                for r in range(TPC):
                    nc.tensor.matmul(ps_sum[:, r, :], m.upto[:, :], wkv[:, r, :], start=True, stop=False)
                    last = nc.tensor.matmul(ps_sum[:, r, :], m.ones[:, :], run[:, r, :], start=False, stop=True)
                last.then_inc(summed, 1)
                pe.wait_ge(y_ready, i + 1)
                for r in range(TPC):
                    last = nc.tensor.transpose(ps_turn[:, r * P:(r + 1) * P], y[:, r, :], m.ident[:, :])
                last.then_inc(turned, 1)
                pe.wait_ge(turn_copied, 3 * i + 2)
                for r in range(TPC):
                    last = nc.tensor.matmul(uv[:, r, :], y_t[:, r * P:(r + 1) * P], m.w_swiglu[:, :],
                                            start=True, stop=True)
                last.then_inc(uv_ready, 1)
                pe.wait_ge(ug_ready, i + 1)
                for r in range(TPC):
                    last = nc.tensor.transpose(ps_turn[:, r * P:(r + 1) * P], ug[:, r, :], m.ident[:, :])
                last.then_inc(turned, 1)
                pe.wait_ge(turn_copied, 3 * i + 3)
                for r in range(TPC):
                    last = nc.tensor.matmul(ps_out[:, r, :], g_t[:, r * P:(r + 1) * P], m.w_out[:, :],
                                            start=True, stop=True)
                last.then_inc(out_ready, 1)

        @block.scalar
        def _(act):
            with act.Fori(0, CHUNKS) as i:
                act.wait_ge(turned, 3 * i + 1)
                nc.scalar.activation(hn_t[:, :], ps_turn[:, :], ACT.Copy).then_inc(turn_copied, 1)
                act.wait_ge(scales_ready, i + 1)
                for r in range(TPC):
                    nc.scalar.activation(wkv[:, r, 0:D], ps_qkv[:, r, D:2 * D], ACT.Exp,
                                         scale=tmp8[:, 4, 2 * r + 1:2 * r + 2])
                    last = nc.scalar.activation(eq[:, r, :], ps_qkv[:, r, 0:D], ACT.Exp,
                                                scale=tmp8[:, 5, 2 * r:2 * r + 1])
                last.then_inc(exps_ready, 1)
                act.wait_ge(turned, 3 * i + 2)
                nc.scalar.activation(y_t[:, :], ps_turn[:, :], ACT.Copy).then_inc(turn_copied, 1)
                act.wait_ge(neg_ready, i + 1)
                nc.scalar.activation(eg[:, :, :], eg[:, :, :], ACT.Exp).then_inc(gate_ready, 1)
                act.wait_ge(turned, 3 * i + 3)
                nc.scalar.activation(g_t[:, :], ps_turn[:, :], ACT.Copy).then_inc(turn_copied, 1)


def project_qkv(nc, m, n, first=None, layer=None):
    mixing = layer is None
    src = m.x if mixing else m.z
    with ExitStack() as ctx:
        def sb(name, shape, dt=F32):
            return ctx.enter_context(nc.sbuf_tensor(name + n, shape, dt))

        sem = m.phase_semaphores()

        st = sb("p_st", [P, TILES, 6])
        tmp = sb("p_tmp", [P, 3, TILES])
        hn = sb("p_hn", [P, 2, TPC, D])
        h_t = sb("p_h_t", [P, 2, CH])
        raw = sb("p_raw", [P, 2, CH])
        rest = sb("p_rest", [P, 2, CH])
        parts = sb("p_parts", [P, 2, 2, 3, CH], BF16)
        ps_turn = ctx.enter_context(nc.psum_tensor("p_ps_turn" + n, [P, CH], F32))
        ps_qk = ctx.enter_context(nc.psum_tensor("p_ps_qk" + n, [P, 2, 2, CH], F32))
        ps_mixed = ctx.enter_context(nc.psum_tensor("p_ps_mixed" + n, [P, 2, CH], F32))
        ps_v = ctx.enter_context(nc.psum_tensor("p_ps_v" + n, [P, TPC, D], F32))
        hn_ready, turned, h_ready = sem("p_hn_ready"), sem("p_turned"), sem("p_h_ready")
        qk_ready, raw_ready, mixed = sem("p_qk_ready"), sem("p_raw_ready"), sem("p_mixed")
        v_ready, high_ready = sem("p_v_ready"), sem("p_high_ready")
        rest_ready, mid_ready, low_ready = sem("p_rest_ready"), sem("p_mid_ready"), sem("p_low_ready")
        v_kept, dve_steps = sem("p_v_kept"), sem("p_dve_steps")
        written = [[sem(f"p_written{k}{slot}") for slot in range(2)] for k in range(2)]
        var_ready, rstd_ready = sem("p_var_ready"), sem("p_rstd_ready")
        block = ctx.enter_context(nc.Block())
        weights = [m.w_b[:, i, :] if mixing else m.w_dh[:, layer, i, :] for i in range(2)]
        weights.append(m.w_b[:, 2, :] if mixing else m.w_att[:, layer, 2, :])
        bias = [(m.vecs if mixing else m.vecs_dh)[:, c:c + 1]
                for c in ((B_BQ, B_BK) if mixing else (BQ + layer, BK + layer))]
        bv = m.bv[:, LAYERS if mixing else layer, :]
        norms = 2 if first else 1

        def projected(c, k):
            return ps_mixed[:, k, :] if mixing else ps_qk[:, c % 2, k, :]

        def write_part(sp, c, k, part):
            dram, parts_of = ((m.q_dram, Q_PARTS), (m.k_dram, K_PARTS))[k]
            places = [g for g, of in enumerate(parts_of) if of == part]
            stride = places[1] - places[0] if len(places) > 1 else 1
            dst = dram.rearrange("(g d) h q -> (d h) g q", d=HD)[:, places[0]:places[-1] + 1:stride,
                                                               c * CH:(c + 1) * CH]
            sp.dma_start(dst, parts[:, c % 2, k, part:part + 1, :].broadcast_to([P, len(places), CH]))\
                .then_inc(written[k][c % 2], 16)

        @block.gpsimd
        def _(pool):
            m.clear_previous(pool)
            for k in range(norms):
                inverse_root(nc, pool, m, m.rstd[:, :], tmp[:, 0, :], var_ready, rstd_ready, k + 1)

        @block.sync
        def _(sp):
            for c in range(CHUNKS):
                for part, ready in enumerate((high_ready, mid_ready, low_ready)):
                    for k in range(2):
                        sp.wait_ge(ready, 2 * c + k + 1)
                        write_part(sp, c, k, part)
            for k in range(2):
                for slot in range(2):
                    sp.wait_ge(written[k][slot], 16 * 3 * CHUNKS // 2)

        @block.vector
        def _(dve):
            step = Steps(dve, dve_steps)
            if first:
                token_stats(nc, step, m.x, st, m, tmp, var_ready, rstd_ready, 1)
                normalise(nc, step, m.z, m.x, m)
            token_stats(nc, step, src, st, m, tmp, var_ready, rstd_ready, norms)

            def normalise_chunk(c):
                if c >= 2:
                    dve.wait_ge(turned, c - 1)
                for r in range(TPC):
                    t = c * TPC + r
                    last = nc.vector.tensor_scalar(hn[:, c % 2, r, :], src[:, t, :], m.mean[:, t:t + 1],
                                                   m.rstd[:, t:t + 1], ALU.subtract, ALU.mult)
                last.then_inc(hn_ready, 1)

            normalise_chunk(0)
            normalise_chunk(1)
            for c in range(CHUNKS):
                if mixing:
                    for k in range(2):
                        dve.wait_ge(qk_ready, 2 * c + k + 1)
                        nc.vector.tensor_scalar(raw[:, k, :], ps_qk[:, c % 2, k, :], bias[k], None, ALU.add)\
                            .then_inc(raw_ready, 1)
                dve.wait_ge(v_ready, c + 1)
                nc.vector.tensor_tensor(m.v_all[:, c * TPC:(c + 1) * TPC, :], ps_v[:, :, :],
                                        bv.unsqueeze(1).broadcast_to([P, TPC, D]), ALU.add).then_inc(v_kept, 1)
                if c + 2 < CHUNKS:
                    normalise_chunk(c + 2)
                for k in range(2):
                    dve.wait_ge(high_ready, 2 * c + k + 1)
                    if c:
                        dve.wait_ge(low_ready, 2 * (c - 1) + k + 1)
                    if mixing:
                        nc.vector.tensor_tensor(rest[:, k, :], projected(c, k), parts[:, c % 2, k, 0, :],
                                                ALU.subtract).then_inc(rest_ready, 1)
                    else:
                        nc.vector.scalar_tensor_tensor(rest[:, k, :], projected(c, k), bias[k],
                                                       parts[:, c % 2, k, 0, :], ALU.add, ALU.subtract)\
                            .then_inc(rest_ready, 1)
                for k in range(2):
                    dve.wait_ge(mid_ready, 2 * c + k + 1)
                    nc.vector.tensor_tensor(parts[:, c % 2, k, 2, :], rest[:, k, :], parts[:, c % 2, k, 1, :],
                                            ALU.subtract).then_inc(low_ready, 1)

        @block.tensor
        def _(pe):
            def transpose_chunk(c):
                pe.wait_ge(hn_ready, c + 1)
                if c:
                    pe.wait_ge(h_ready, c)
                for r in range(TPC):
                    last = nc.tensor.transpose(ps_turn[:, r * P:(r + 1) * P], hn[:, c % 2, r, :], m.ident[:, :])
                last.then_inc(turned, 1)

            transpose_chunk(0)
            transpose_chunk(1)
            for c in range(CHUNKS):
                pe.wait_ge(h_ready, c + 1)
                if c >= 2:
                    pe.wait_ge(raw_ready if mixing else rest_ready, 2 * (c - 1))
                for k in range(2):
                    nc.tensor.matmul(ps_qk[:, c % 2, k, :], weights[k],
                                     h_t[:, c % 2, :], start=True, stop=True)\
                        .then_inc(qk_ready, 1)
                if c:
                    pe.wait_ge(v_kept, c)
                for r in range(TPC):
                    last = nc.tensor.matmul(ps_v[:, r, :], h_t[:, c % 2, r * P:(r + 1) * P], weights[2],
                                            start=True, stop=True)
                last.then_inc(v_ready, 1)
                if mixing:
                    for k in range(2):
                        pe.wait_ge(raw_ready, 2 * c + k + 1)
                        if c:
                            pe.wait_ge(rest_ready, 2 * (c - 1) + k + 1)
                        nc.tensor.matmul(ps_mixed[:, k, :], m.mix_dh[:, :], raw[:, k, :], start=True, stop=True)\
                            .then_inc(mixed, 1)
                if c + 2 < CHUNKS:
                    transpose_chunk(c + 2)

        @block.scalar
        def _(act):
            def copy_chunk(c):
                act.wait_ge(turned, c + 1)
                if c >= 2:
                    act.wait_ge(v_ready, c - 1)
                if mixing:
                    nc.scalar.activation(h_t[:, c % 2, :], ps_turn[:, :], ACT.Copy).then_inc(h_ready, 1)
                else:
                    nc.scalar.activation(h_t[:, c % 2, :], ps_turn[:, :], ACT.Identity,
                                         scale=m.vecs[:, LN1_W + layer:LN1_W + layer + 1],
                                         bias=m.vecs[:, LN1_B + layer:LN1_B + layer + 1]).then_inc(h_ready, 1)

            copy_chunk(0)
            copy_chunk(1)
            for c in range(CHUNKS):
                for k in range(2):
                    act.wait_ge(mixed if mixing else qk_ready, 2 * c + k + 1)
                    if c >= 2:
                        act.wait_ge(written[k][c % 2], 16 * 3 * (c // 2))
                    if mixing:
                        nc.scalar.activation(parts[:, c % 2, k, 0, :], projected(c, k), ACT.Copy)\
                            .then_inc(high_ready, 1)
                    else:
                        nc.scalar.activation(parts[:, c % 2, k, 0, :], projected(c, k), ACT.Identity, bias=bias[k])\
                            .then_inc(high_ready, 1)
                if c + 2 < CHUNKS:
                    copy_chunk(c + 2)
                for k in range(2):
                    act.wait_ge(rest_ready, 2 * c + k + 1)
                    nc.scalar.activation(parts[:, c % 2, k, 1, :], rest[:, k, :], ACT.Copy).then_inc(mid_ready, 1)


SCAN_KEYS = 512
RING_A = 4
RING_S, RING_P = 3, 8
LEAD = 64
PACING = {True: (2500, 3000, 0.9), False: (3500, 3500, 1.0)}


def attention_schedule(causal, last_quad):
    lead = LEAD
    margin, reload, hurry = PACING[causal]
    blocks = [TPC * (c + 1) if causal else TILES for c in range(CHUNKS)]

    pieces = []
    for c in range(CHUNKS):
        for j in range(QUAD):
            for t in range(TPC):
                keys = (TPC * c + t + 1) * P if causal else S
                for p in range(-(-keys // SCAN_KEYS)):
                    pieces.append((c, j, t, p, min(SCAN_KEYS, keys - SCAN_KEYS * p)))
    units = [(c, kb, j) for c in range(CHUNKS) for kb in range(blocks[c]) for j in range(QUAD)]

    def unit_cost(c, kb):
        return (CH - (max(0, kb - TPC * c) * P if causal else 0)) + 40

    starts, total = [], 0
    for c, kb, j in units:
        starts.append(total)
        total += unit_cost(c, kb)
    begins = [starts[units.index((c, 0, 0))] for c in range(CHUNKS)] + [total]
    own, following = pieces[lead:], ([] if last_quad else pieces[:lead])
    work = [(x, False) for x in own] + [(x, True) for x in following]
    costs = [x[4] + 60 for x, _ in work]
    pace = total / sum(x[4] + 60 for x in pieces)
    even, at = [], 0.0
    for cost in costs:
        even.append(at)
        at += cost * pace
    latest, bound = [0.0] * len(work), float(total)
    for i in range(len(work) - 1, -1, -1):
        (c, *_), nxt = work[i]
        if not nxt:
            bound = min(bound, begins[c] - margin)
        bound -= costs[i] * hurry
        latest[i] = bound
    times = []
    for i, ((c, *_), nxt) in enumerate(work):
        when = min(even[i], latest[i])
        if nxt:
            when = max(when, begins[c + 1] + 600, begins[CHUNKS - 1] + reload)
        times.append(max(when, times[-1] if times else when))

    order, pending, given = [], None, 0

    def give(upto_time):
        nonlocal given
        while given < len(work) and times[given] <= upto_time:
            (c, j, t, p, width), nxt = work[given]
            order.append(("scan", c, j, t, p, width, nxt))
            given += 1
            if given == len(work) or work[given][0][0] != c:
                if (c, j, t) == (c, QUAD - 1, TPC - 1):
                    order.append(("rows", c, nxt))

    for u, (c, kb, j) in enumerate(units):
        order.append(("scores", c, kb, j))
        give(starts[u])
        if j == QUAD - 1:
            if pending:
                order.append(("values", *pending))
                if pending[1] == blocks[pending[0]] - 1:
                    order.append(("drain", pending[0]))
            pending = (c, kb)
    give(float("inf"))
    order += [("values", *pending), ("drain", pending[0])]
    first = []
    for i, (c, j, t, p, width) in enumerate(pieces[:lead]):
        first.append(("scan", c, j, t, p, width, False))
        if pieces[i + 1][0] != c:
            first.append(("rows", c, False))
    return first, order, blocks


def split_expert_weights(nc, m, pool, raw):
    pieces = [(m.ins["L0_ffn_e_w1"][0, e], m.w1_hi[:, e, :], m.w1_lo[:, e, :]) for e in range(E)]

    def place(k):
        return raw[:, k % 2, :]

    for k in range(2):
        pool.dma_start(place(k), pieces[k][0]).then_inc(m.weights_in[k], 16)
    for k, (_, hi, lo) in enumerate(pieces):
        pool.wait_ge(m.weights_in[k % 2], 16 * (k // 2 + 1))
        nc.gpsimd.tensor_copy(hi, place(k)).then_inc(m.weights_hi, 1)
        pool.wait_ge(m.weights_hi, k + 1)
        nc.gpsimd.tensor_tensor(lo, place(k), hi.bitcast(F32), ALU.subtract).then_inc(m.weights_split, 1)
        if k + 2 < len(pieces):
            pool.wait_ge(m.weights_split, k + 1)
            pool.dma_start(place(k), pieces[k + 2][0]).then_inc(m.weights_in[k % 2], 16)


def attention_heads(nc, m, n, causal, load_experts=False):
    first, order, blocks = attention_schedule(causal, False)
    _, order_last, _ = attention_schedule(causal, True)
    scans_first = sum(x[0] == "scan" for x in first)
    scans = sum(x[0] == "scan" for x in order)
    units = QUAD * sum(blocks)
    before = [QUAD * sum(blocks[:c]) for c in range(CHUNKS)]

    def unit(c, kb, j):
        return before[c] + kb * QUAD + j

    def previous(u, ring):
        return u - ring if u >= ring else u + ring * ((units - 1 - u) // ring) - units

    with ExitStack() as ctx:
        def sb(name, shape, dt=F32):
            return ctx.enter_context(nc.sbuf_tensor(name + n, shape, dt))

        sem = m.phase_semaphores()

        probs = sb("h_probs", [P, RING_P, CH])
        maxima = sb("h_maxima", [P, 2, QUAD * TPC, S // SCAN_KEYS])
        negated = sb("h_negated", [P, 32], BF16)
        neg_rows = sb("h_neg_rows", [P, 2, 32], BF16)
        drained_sb = sb("h_drained", [P, 2, CH])
        raw_weights = sb("h_raw_weights", [P, 2, FF]) if load_experts else None
        ps_scan = ctx.enter_context(nc.psum_tensor("h_ps_scan" + n, [P, RING_A, SCAN_KEYS], F32))
        ps_scores = ctx.enter_context(nc.psum_tensor("h_ps_scores" + n, [P, RING_S, CH], F32))
        ps_values = ctx.enter_context(nc.psum_tensor("h_ps_values" + n, [P, CH], F32))
        scanned, reduced, scored, exped, valued = (sem(s) for s in ("h_scanned", "h_reduced", "h_scored", "h_exped",
                                                                    "h_valued"))
        drained, neg_ready, neg_turned, v_in = (sem(s) for s in ("h_drained_", "h_neg_ready", "h_neg_turned", "h_v_in"))
        q_in = [sem(f"h_q_in{c}") for c in range(CHUNKS)]
        scan_in = [sem(f"h_scan_in{c}") for c in range(CHUNKS)]
        k_in = [sem(f"h_k_in{c}") for c in range(CHUNKS)]
        rows_in = [sem(f"h_rows_in{c}") for c in range(CHUNKS)]
        out_done = [sem(f"h_out_done{c}") for c in range(2)]
        block = ctx.enter_context(nc.Block())

        def cols(c):
            return slice(c * CH, (c + 1) * CH)

        @block.tensor
        def _(pe):
            def scan(q, a, c, j, t, p, width):
                if (j, t, p) == (0, 0, 0):
                    pe.wait_ge(q_in[c], 16 * (q + 1))
                    for k in ([c] if causal or c else range(CHUNKS)):
                        pe.wait_ge(scan_in[k], 16 * (q + 1))
                if not (isinstance(a, int) and a < RING_A):
                    pe.wait_ge(reduced, a - RING_A + 1)
                slot = piece[0] % RING_A
                piece[0] += 1
                at = (TPC * c + t) * P
                queries = m.q_stack[:, c, j, t * P:(t + 1) * P]
                for o in range(0, width, CH):
                    w = min(CH, width - o)
                    diag = causal and SCAN_KEYS * p + o + w == at + P
                    last = nc.tensor.matmul(ps_scan[:, slot, o:o + w], queries,
                                            m.k_scan[:, j, SCAN_KEYS * p + o:SCAN_KEYS * p + o + w],
                                            start=True, stop=not diag)
                    if diag:
                        last = nc.tensor.matmul(ps_scan[:, slot, o + w - P:o + w], m.ident_bf[:, :],
                                                m.hide_right[:, :], start=False, stop=True)
                last.then_inc(scanned, 1)

            def scores(q, c, kb, j):
                u = unit(c, kb, j)
                if j == 0 and kb == 0:
                    pe.wait_ge(rows_in[c], 64 * (q + 1))
                if j == 0 and kb % TPC == 0:
                    pe.wait_ge(k_in[kb // TPC], 16 * (q + 1))
                pe.wait_ge(exped, units * (q + 1) + previous(u, RING_S) + 1)
                off = max(0, kb - TPC * c) * P if causal else 0
                diag = causal and kb >= TPC * c
                last = nc.tensor.matmul(ps_scores[:, u % RING_S, off:CH], m.k_stack[:, j, kb * P:(kb + 1) * P],
                                        m.q_stack[:, c, j, off:CH], start=True, stop=not diag)
                if diag:
                    last = nc.tensor.matmul(ps_scores[:, u % RING_S, off:off + P], m.ident_bf[:, :],
                                            m.hide_left[:, :], start=False, stop=True)
                last.then_inc(scored, 1)

            def values(q, c, kb):
                if kb == 0:
                    pe.wait_ge(drained, CHUNKS * q + c)
                if kb % TPC == 0:
                    pe.wait_ge(v_in, CHUNKS * q + kb // TPC + 1)
                pe.wait_ge(exped, units * (q + 1) + unit(c, kb, QUAD - 1) + 1)
                off = max(0, kb - TPC * c) * P if causal else 0
                for j in range(QUAD):
                    nc.tensor.matmul(ps_values[32 * j:32 * j + 32, off:CH], m.v_quad[:, kb, j, :],
                                     probs[:, unit(c, kb, j) % RING_P, off:CH],
                                     start=kb == 0, stop=kb == blocks[c] - 1).then_inc(valued, 1)

            def run(q, steps, a):
                for s in steps:
                    if s[0] == "scan":
                        scan(q + 1 if s[6] else q, a, *s[1:6])
                        a = a + 1
                    elif s[0] == "scores":
                        scores(q, *s[1:])
                    elif s[0] == "values":
                        values(q, *s[1:])

            pe.sem_inc(valued, units)
            piece = [0]
            run(0, first, 0)
            with pe.Fori(0, QUADS - 1) as q:
                run(q, order, q * scans + scans_first)
            run(QUADS - 1, order_last, (QUADS - 1) * scans + scans_first)

        @block.scalar
        def _(act):
            act.sem_inc(exped, units)

            def run(q, steps):
                for s in steps:
                    if s[0] == "scores":
                        c, kb, j = s[1:]
                        u = unit(c, kb, j)
                        off = max(0, kb - TPC * c) * P if causal else 0
                        act.wait_ge(scored, units * q + u + 1)
                        act.wait_ge(valued, units * (q + 1) + previous(u, RING_P) + 1)
                        nc.scalar.activation(probs[:, u % RING_P, off:CH], ps_scores[:, u % RING_S, off:CH], ACT.Exp,
                                             scale=SOFTMAX_SCALE).then_inc(exped, 1)

            with act.Fori(0, QUADS - 1) as q:
                run(q, order)
            run(QUADS - 1, order_last)

        @block.vector
        def _(dve):
            nc.vector.memset(negated[:, :], 0.0).then_inc(neg_ready, 1)
            dve.wait_ge(neg_ready, 1)

            def run(q, steps, a, r):
                for s in steps:
                    if s[0] == "scan":
                        c, j, t, p, width = s[1:6]
                        slot = piece[0] % RING_A
                        piece[0] += 1
                        dve.wait_ge(scanned, a + 1)
                        nc.vector.reduce_max(maxima[:, c % 2, TPC * j + t, p:p + 1], ps_scan[:, slot, 0:width],
                                             AXIS_X).then_inc(reduced, 1)
                        a = a + 1
                    elif s[0] == "rows":
                        c, own = s[1], (q + 1 if s[2] else q)
                        dve.wait_ge(reduced, a)
                        n_pieces = -(-(S if not causal else (c + 1) * CH) // SCAN_KEYS)
                        if n_pieces > 1:
                            nc.vector.tensor_reduce(negated[:, 0:QUAD * TPC], maxima[:, c % 2, :, 0:n_pieces], AXIS_X, ALU.max,
                                                    negate=True).then_inc(neg_ready, 1)
                        else:
                            nc.vector.tensor_scalar(negated[:, 0:QUAD * TPC], maxima[:, c % 2, :, 0], -1.0, None,
                                                    ALU.mult).then_inc(neg_ready, 1)
                        dve.wait_ge(neg_ready, r + 2)
                        if c >= 2:
                            dve.wait_ge(rows_in[c - 2], 64 * (own + 1))
                        elif not (isinstance(own, int) and own == 0):
                            dve.wait_ge(rows_in[c + 2], 64 * own)
                        nc.vector.transpose(neg_rows[:, c % 2, :], negated[:, :]).then_inc(neg_turned, 1)
                        dve.wait_ge(neg_turned, r + 1)
                        r = r + 1
                    elif s[0] == "drain":
                        c = s[1]
                        dve.wait_ge(valued, units * (q + 1) + unit(c, blocks[c] - 1, QUAD - 1) + 1)
                        dve.wait_ge(out_done[c % 2], 16 * (2 * q + c // 2))
                        nc.vector.tensor_copy(drained_sb[:, c % 2, :], ps_values[:, :]).then_inc(drained, 1)

            piece = [0]
            ahead = sum(x[0] == "rows" for x in first)
            run(0, first, 0, 0)
            with dve.Fori(0, QUADS - 1) as q:
                run(q, order, q * scans + scans_first, q * CHUNKS + ahead)
            run(QUADS - 1, order_last, (QUADS - 1) * scans + scans_first, (QUADS - 1) * CHUNKS + ahead)

        @block.gpsimd
        def _(pool):
            m.clear_previous(pool)
            def copy_values(q, i):
                nc.gpsimd.tensor_copy(m.v_quad[:, TPC * i:TPC * (i + 1), :, 0:HD],
                                      m.v_all[:, TPC * i:TPC * (i + 1), bass.ds(q * (QUAD * HD), QUAD * HD)]
                                      .rearrange("p k (j d) -> p k j d", d=HD)).then_inc(v_in, 1)

            for i in range(CHUNKS):
                copy_values(0, i)
            if load_experts:
                split_expert_weights(nc, m, pool, raw_weights)
            with pool.Fori(0, QUADS - 1) as q:
                for i in range(CHUNKS):
                    pool.wait_ge(valued, units * (q + 1) + unit(CHUNKS - 1, TPC * i + TPC - 1, QUAD - 1) + 1)
                    copy_values(q + 1, i)

        @block.sync
        def _(sp):
            def load(dst, dram, q, c, sem_):
                at = dst[0:STACK, c, :, :] if dst is m.q_stack else dst[0:STACK, :, cols(c)]
                sp.dma_start(at, dram[:, bass.ds(q * QUAD, QUAD), cols(c)]).then_inc(sem_, 16)

            def run(q, steps, a, r, reload):
                for s in steps:
                    if s[0] == "scan":
                        a = a + 1
                    elif s[0] == "rows":
                        c = s[1]
                        r = r + 1
                        sp.wait_ge(neg_turned, r)
                        rows = m.q_stack[SHIFT_ROW:SHIFT_ROW + 1, c, :, :]\
                            .rearrange("p j (t b k) -> p (j t) b k", t=TPC, k=32)
                        for b in range(4):
                            sp.dma_start(rows[:, :, b, :], neg_rows[32 * b:32 * b + QUAD * TPC, c % 2, :])\
                                .then_inc(rows_in[c], 16)
                        if reload and c == CHUNKS - 1:
                            sp.wait_ge(scanned, a)
                            for k in range(CHUNKS):
                                load(m.k_scan, m.k_dram, q + 1, k, scan_in[k])
                    elif s[0] == "scores" and reload and s[3] == QUAD - 1:
                        c, kb = s[1:3]
                        if kb == blocks[c] - 1:
                            sp.wait_ge(scored, units * q + unit(c, kb, QUAD - 1) + 1)
                            load(m.q_stack, m.q_dram, q + 1, c, q_in[c])
                        if c == CHUNKS - 1 and kb % TPC == TPC - 1:
                            sp.wait_ge(scored, units * q + unit(c, kb, QUAD - 1) + 1)
                            load(m.k_stack, m.k_dram, q + 1, kb // TPC, k_in[kb // TPC])
                    elif s[0] == "drain":
                        c = s[1]
                        sp.wait_ge(drained, CHUNKS * q + c + 1)
                        sp.dma_start(m.o_dram[bass.ds(q * QUAD, QUAD), :, cols(c)], drained_sb[:, c % 2, :])\
                            .then_inc(out_done[c % 2], 16)

            for c in range(CHUNKS):
                load(m.q_stack, m.q_dram, 0, c, q_in[c])
                load(m.k_scan, m.k_dram, 0, c, scan_in[c])
            for c in range(CHUNKS):
                load(m.k_stack, m.k_dram, 0, c, k_in[c])
            ahead = sum(x[0] == "rows" for x in first)
            run(0, first, 0, 0, False)
            with sp.Fori(0, QUADS - 1) as q:
                run(q, order, q * scans + scans_first, q * CHUNKS + ahead, True)
            run(QUADS - 1, order_last, (QUADS - 1) * scans + scans_first, (QUADS - 1) * CHUNKS + ahead, False)
            for half in range(2):
                sp.wait_ge(out_done[half], 16 * QUADS * CHUNKS // 2)


def finish_attention(nc, m, n, layer=None):
    dst = m.x if layer is None else m.z
    with ExitStack() as ctx:
        def sb(name, shape, dt=F32):
            return ctx.enter_context(nc.sbuf_tensor(name + n, shape, dt))

        sem = m.phase_semaphores()

        y = sb("f_y", [P, CHUNKS, CH])
        sums = sb("f_sums", [P, CHUNKS, CH])
        ps = ctx.enter_context(nc.psum_tensor("f_ps" + n, [P, CHUNKS, TPC, D], F32))
        loaded = [sem(f"f_loaded{c}") for c in range(CHUNKS)]
        y_ready, projected, dve_steps = sem("f_y_ready"), sem("f_projected"), sem("f_dve_steps")
        block = ctx.enter_context(nc.Block())

        @block.gpsimd
        def _(pool):
            m.clear_previous(pool)

        @block.sync
        def _(sp):
            for c in range(CHUNKS):
                q = slice(c * CH, (c + 1) * CH)
                sp.dma_start(y[:, c, :], m.o_dram[:, 0:HD, q]).then_inc(loaded[c], 16)
                sp.dma_start(sums[:, c, :], m.o_dram[:, HD:HD + 1, q].broadcast_to([HEADS, HD, CH]))\
                    .then_inc(loaded[c], 16)

        @block.vector
        def _(dve):
            step = Steps(dve, dve_steps)
            for c in range(CHUNKS):
                dve.wait_ge(loaded[c], 32)
                step(nc.vector.reciprocal(sums[:, c, :], sums[:, c, :]))
                nc.vector.tensor_tensor(y[:, c, :], y[:, c, :], sums[:, c, :], ALU.mult).then_inc(y_ready, 1)
            for c in range(CHUNKS):
                tiles = dst[:, c * TPC:(c + 1) * TPC, :]
                if layer is not None:
                    step(nc.vector.tensor_tensor(tiles, tiles, m.bo[:, layer:layer + 1, :]
                                                 .broadcast_to([P, TPC, D]), ALU.add))
                dve.wait_ge(projected, c + 1)
                step(nc.vector.tensor_tensor(tiles, tiles, ps[:, c, :, :], ALU.add))

        @block.tensor
        def _(pe):
            right = m.ident[:, :] if layer is None else m.w_att[:, layer, 3, :]
            for c in range(CHUNKS):
                pe.wait_ge(y_ready, c + 1)
                for r in range(TPC):
                    last = nc.tensor.matmul(ps[:, c, r, :], y[:, c, r * P:(r + 1) * P], right, start=True, stop=True)
                last.then_inc(projected, 1)


def top2(nc, step, t, logits, rank):
    full = list(logits.shape)
    v = nc.vector

    def pick(values, onehot, top):
        step(v.tensor_reduce(t[top], values, AXIS_X, ALU.max))
        step(v.tensor_tensor(t["s"], values, t[top].broadcast_to(full), ALU.is_equal))
        step(v.tensor_tensor(t["s"], t["s"], rank.broadcast_to(full), ALU.mult))
        step(v.tensor_reduce(t["r"], t["s"], AXIS_X, ALU.max))
        step(v.tensor_tensor(t[onehot], t["s"], t["r"].broadcast_to(full), ALU.is_equal))

    pick(logits, "h1", "m1")
    step(v.scalar_tensor_tensor(t["l2"], t["h1"], -3e38, logits, ALU.mult, ALU.add))
    pick(t["l2"], "h2", "m2")
    return v.tensor_tensor(t["d"], t["m2"], t["m1"], ALU.subtract)


def top2_combine(nc, step, t, full):
    v = nc.vector
    step(v.tensor_scalar(t["r"], t["ed"], 1.0, None, ALU.add))
    step(v.reciprocal(t["r"], t["r"]))
    step(v.tensor_tensor(t["h2"], t["h2"], t["ed"].broadcast_to(full), ALU.mult))
    step(v.tensor_tensor(t["s"], t["h1"], t["h2"], ALU.add))
    return v.tensor_tensor(t["cw"], t["s"], t["r"].broadcast_to(full), ALU.mult)


TOP2_STEPS = 11 + 4


def router_tiles(nc, ctx, n, parts, groups):
    t = {}
    for name in ("s", "h1", "h2", "l2", "cw", "lg"):
        t[name] = ctx.enter_context(nc.sbuf_tensor(f"t_{name}{n}", [parts, groups, E], F32))[:, :, :]
    for name in ("m1", "m2", "r", "d", "ed"):
        t[name] = ctx.enter_context(nc.sbuf_tensor(f"t_{name}{n}", [parts, groups, 1], F32))[:, :, :]
    return t


def experts(nc, m, n, layer, last):
    by_token = layer == 0
    n_exp = E if by_token else TOPK
    blocks = n_exp * FB
    ring_h = 4
    lag = 2
    with ExitStack() as ctx:
        def sb(name, shape, dt=F32):
            return ctx.enter_context(nc.sbuf_tensor(name + n, shape, dt))

        sem = m.phase_semaphores()

        st = sb("e_st", [P, TILES, 6])
        tmp = sb("e_tmp", [P, 3, TILES])
        hn = m.v_all
        h_hi = sb("e_h_hi", [P, CHUNKS, CH], F32R)
        h_lo = sb("e_h_lo", [P, CHUNKS, CH], F32R)
        hidden = sb("e_hidden", [P, ring_h, CH])
        cw_t = sb("e_cw_t", [E, CH])
        if by_token:
            t = router_tiles(nc, ctx, n, P, TILES)
            cw_now = sb("e_cw_now", [P, TPC, E])
            w1_hi, w1_lo, w2 = m.w1_hi, m.w1_lo, m.w2
        else:
            t = router_tiles(nc, ctx, n, 1, 1)
            w1_hi, w1_lo = sb("e_w1_hi", [P, TOPK, FF], F32R), sb("e_w1_lo", [P, TOPK, FF], F32R)
            w2 = sb("e_w2", [P, TOPK, FB, D])
            raw_w1 = m.v_all[:, 0:TOPK * FB, :].rearrange("p (k b) d -> p k (b d)", k=TOPK)
            b1 = sb("e_b1", [P, TOPK, FB])
            sums = sb("e_sums", [P, CHUNKS])
            mean_h = sb("e_mean_h", [P, 1])
            ids = sb("e_ids", [1, TOPK])
            pair = sb("e_pair", [1, TOPK])
            pair_rows = sb("e_pair_rows", [P, TOPK])
        ps_turn = ctx.enter_context(nc.psum_tensor("e_ps_turn" + n, [P, 2, CH], F32))
        ps_h = ctx.enter_context(nc.psum_tensor("e_ps_h" + n, [P, FB, CH], F32))
        ps_y = ctx.enter_context(nc.psum_tensor("e_ps_y" + n, [P, 2, TPC, D], F32))
        ps_b2 = ps_turn[:, 1, :].rearrange("p (t d) -> p t d", d=D)
        ps_logits = ps_y[:, 0, 0, :].rearrange("p (t e) -> p t e", e=E)
        hn_ready, turned, h_ready, h_split = (sem(s) for s in ("e_hn_ready", "e_turned", "e_h_ready", "e_h_split"))
        logits_ready, top_ready, exp_ready, cw_ready = (sem(s) for s in ("e_logits", "e_top", "e_exp", "e_cw"))
        cw_turned, cwt_ready, b2_ready, b2_added = (sem(s) for s in ("e_cw_turned", "e_cwt", "e_b2_ready",
                                                                     "e_b2_added"))
        up_ready, gelu_ready, down_ready, added = (sem(s) for s in ("e_up", "e_gelu", "e_down", "e_added"))
        dve_steps, weights_in, weights_split = sem("e_dve"), sem("e_weights_in"), sem("e_weights_split")
        mean_ready, pair_ready, pair_spread = sem("e_mean"), sem("e_pair_ready"), sem("e_pair_spread")
        cw_set, h_ready_hi = sem("e_cw_set"), sem("e_h_ready_hi")
        pair_kept = sem("e_pair_kept")
        var_ready, rstd_ready = sem("e_var_ready"), sem("e_rstd_ready")
        block = ctx.enter_context(nc.Block())
        ln_w = m.vecs[:, LN2_W + layer:LN2_W + layer + 1]
        ln_b = m.vecs[:, LN2_B + layer:LN2_B + layer + 1]
        full = [P, TILES, E]

        @block.gpsimd
        def _(pool):
            m.clear_previous(pool)
            inverse_root(nc, pool, m, m.rstd[:, :], tmp[:, 0, :], var_ready, rstd_ready, 1)

        @block.vector
        def _(dve):
            step = Steps(dve, dve_steps)
            token_stats(nc, step, m.z, st, m, tmp, var_ready, rstd_ready, 1)
            for c in range(CHUNKS):
                for r in range(TPC):
                    i = c * TPC + r
                    last_ = nc.vector.tensor_scalar(hn[:, i, :], m.z[:, i, :], m.mean[:, i:i + 1],
                                                    m.rstd[:, i:i + 1], ALU.subtract, ALU.mult)
                last_.then_inc(hn_ready, 1)
            for c in range(CHUNKS):
                dve.wait_ge(h_ready, c + 1)
                nc.vector.tensor_tensor(h_lo[:, c, :], ps_turn[:, c % 2, :], h_hi[:, c, :].bitcast(F32),
                                        ALU.subtract).then_inc(h_split, 1)
            if by_token:
                dve.wait_ge(logits_ready, 1)
                step(nc.vector.tensor_tensor(t["lg"], ps_logits, m.gate_b[:, layer:layer + 1, :].broadcast_to(full),
                                             ALU.add))
                top2(nc, step, t, t["lg"], m.rank[:, :].unsqueeze(1)).then_inc(top_ready, 1)
                dve.wait_ge(exp_ready, 1)
                step(top2_combine(nc, step, t, full))
            else:
                step(nc.vector.tensor_reduce(mean_h[:, :], sums[:, :], AXIS_X, ALU.add))
                nc.vector.tensor_scalar(mean_h[:, :], mean_h[:, :], 1.0 / S, None, ALU.mult).then_inc(mean_ready, 1)
                dve.wait_ge(logits_ready, 1)
                step(nc.vector.tensor_tensor(t["lg"], ps_logits[0:1, 0:1, :], m.gate_b[0:1, layer:layer + 1, :],
                                             ALU.add))
                top2(nc, step, t, t["lg"], m.rank[0:1, :].unsqueeze(1)).then_inc(top_ready, 1)
                for k, onehot in enumerate(("h1", "h2")):
                    step(nc.vector.tensor_tensor(t["s"], t[onehot], m.rank[0:1, :].unsqueeze(1), ALU.mult))
                    step(nc.vector.tensor_reduce(ids[:, k:k + 1], t["s"], AXIS_X, ALU.add))
                step(nc.vector.tensor_scalar(ids[:, :], ids[:, :], -1.0, float(E), ALU.mult, ALU.add))
                nc.vector.tensor_copy(m.ids_int[:, :], ids[:, :]).then_inc(cw_set, 1)
                dve.wait_ge(exp_ready, 1)
                step(top2_combine(nc, step, t, [1, 1, E]))
                step(nc.vector.tensor_copy(pair[:, 0:1], t["r"][:, :, 0]))
                nc.vector.tensor_tensor(pair[:, 1:2], t["ed"][:, :, 0], t["r"][:, :, 0], ALU.mult)\
                    .then_inc(pair_ready, 1)
                dve.wait_ge(pair_spread, 1)
                nc.vector.tensor_copy(pair_rows[:, :], ps_y[:, 0, 0, E:E + TOPK]).then_inc(pair_kept, 1)
                dve.wait_ge(pair_kept, 1)
                dve.wait_ge(weights_in, 16 * 3 * TOPK)
                step(nc.vector.tensor_copy(w1_hi[:, :, :], raw_w1))
                nc.vector.tensor_tensor(w1_lo[:, :, :], raw_w1, w1_hi[:, :, :].bitcast(F32), ALU.subtract)\
                    .then_inc(weights_split, 1)

            with dve.Fori(0, CHUNKS) as i:
                def add_expert(e):
                    dve.wait_ge(down_ready, blocks * i + FB * (e + 1) + ring_h)
                    if e:
                        dve.wait_ge(added, n_exp * i + e)
                    else:
                        dve.wait_ge(b2_added, i + 1)
                    for r in range(TPC):
                        at = bass.ds(i * TPC + r, 1)
                        weight = cw_now[:, r, e:e + 1] if by_token else pair_rows[:, e:e + 1]
                        last_ = nc.vector.scalar_tensor_tensor(m.z[:, at, :], ps_y[:, e % 2, r:r + 1, :], weight,
                                                               m.z[:, at, :], ALU.mult, ALU.add)
                    last_.then_inc(added, 1)

                if by_token:
                    dve.wait_ge(added, n_exp * i)
                    nc.vector.tensor_copy(cw_now[:, :, :], t["cw"][:, token_tiles(i), :]).then_inc(cw_set, 1)
                dve.wait_ge(b2_ready, i + 1)
                if by_token:
                    dve.wait_ge(cw_set, i + 1)
                nc.vector.tensor_tensor(m.z[:, token_tiles(i), :], m.z[:, token_tiles(i), :], ps_b2, ALU.add)\
                    .then_inc(b2_added, 1)
                for e in range(n_exp):
                    add_expert(e)
                dve.wait_ge(added, n_exp * (i + 1))
                if last:
                    nc.vector.tensor_tensor(m.x[:, token_tiles(i), :], m.x[:, token_tiles(i), :],
                                            m.z[:, token_tiles(i), :], ALU.add)

        @block.tensor
        def _(pe):
            def turn(c):
                pe.wait_ge(hn_ready, c + 1)
                if c >= 2:
                    pe.wait_ge(h_split, c - 1)
                for r in range(TPC):
                    last_ = nc.tensor.transpose(ps_turn[:, c % 2, r * P:(r + 1) * P], hn[:, c * TPC + r, :],
                                                m.ident[:, :])
                last_.then_inc(turned, 1)

            def product(out, left, right, start, stop):
                nc.tensor.matmul(out, left[0], right[0], start=start, stop=False, skip_group_check=True)
                nc.tensor.matmul(out, left[1], right[0], start=False, stop=False, skip_group_check=True)
                return nc.tensor.matmul(out, left[0], right[1], start=False, stop=stop, skip_group_check=True)

            pe.sem_inc(down_ready, ring_h)
            turn(0)
            turn(1)
            for c in range(CHUNKS):
                pe.wait_ge(h_split, c + 1)
                if by_token:
                    for r in range(TPC):
                        q = slice(r * P, (r + 1) * P)
                        last_ = product(ps_logits[:, c * TPC + r, :], (h_hi[:, c, q], h_lo[:, c, q]),
                                        (m.gate_hi[:, layer, :], m.gate_lo[:, layer, :]), True, True)
                if c + 2 < CHUNKS:
                    turn(c + 2)
            if by_token:
                last_.then_inc(logits_ready, 1)
                pe.wait_ge(m.weights_split, E)
                pe.wait_ge(m.w2_in, 16 * E)
            else:
                pe.wait_ge(mean_ready, 1)
                nc.tensor.matmul(ps_logits[0:1, 0, :], mean_h[:, :], m.gate_w[:, layer, :], start=True, stop=True)\
                    .then_inc(logits_ready, 1)
                pe.wait_ge(pair_ready, 1)
                nc.tensor.matmul(ps_y[:, 0, 0, E:E + TOPK], m.ones[0:1, :], pair[:, :], start=True, stop=True)\
                    .then_inc(pair_spread, 1)
                for r in range(TPC):
                    last_ = nc.tensor.matmul(ps_turn[0:E, 0, r * P:(r + 1) * P], t["cw"][:, 0, :], m.ones[0:1, :],
                                             start=True, stop=True)
                last_.then_inc(cw_turned, 1)
                pe.wait_ge(pair_kept, 1)
                pe.wait_ge(weights_split, 1)
            with pe.Fori(0, CHUNKS) as i:
                now = (h_hi[:, bass.ds(i, 1), :], h_lo[:, bass.ds(i, 1), :])

                def up(k):
                    e, b = k // FB, k % FB
                    pe.wait_ge(gelu_ready, blocks * i + k + 1)
                    q = slice(b * P, (b + 1) * P)
                    product(ps_h[:, b, :], (w1_hi[:, e, q], w1_lo[:, e, q]), now, True, True).then_inc(up_ready, 1)

                def down(k):
                    e, b = k // FB, k % FB
                    pe.wait_ge(gelu_ready, blocks * i + k + 1 + FB)
                    if b == 0:
                        pe.wait_ge(added, n_exp * i + (e - 1 if e >= 2 else 0))
                        if by_token and e == 0:
                            pe.wait_ge(cw_set, i + 1)
                    for r in range(TPC):
                        q = slice(r * P, (r + 1) * P)
                        last_ = nc.tensor.matmul(ps_y[:, e % 2, r, :], hidden[:, k % ring_h, q], w2[:, e, b, :],
                                                 start=b == 0 and r == 0, stop=b == FB - 1, skip_group_check=True)
                    last_.then_inc(down_ready, 1)

                for k in range(blocks):
                    up(k)
                    if k == 0:
                        if by_token:
                            pe.wait_ge(cw_set, i + 1)
                            for r in range(TPC):
                                last_ = nc.tensor.transpose(ps_turn[0:E, 0, r * P:(r + 1) * P], cw_now[:, r, :],
                                                            m.ident[:, :])
                            last_.then_inc(cw_turned, 1)
                    if k == 1:
                        pe.wait_ge(cwt_ready, i + 1 if by_token else 1)
                        pe.wait_ge(b2_added, i)
                        for r in range(TPC):
                            last_ = nc.tensor.matmul(ps_b2[:, r, :], cw_t[:, r * P:(r + 1) * P], m.b2[:, layer, :],
                                                     start=True, stop=True)
                        last_.then_inc(b2_ready, 1)
                    if k >= lag:
                        down(k - lag)
                for k in range(blocks - lag, blocks):
                    down(k)

        @block.scalar
        def _(act):
            for c in range(CHUNKS):
                act.wait_ge(turned, c + 1)
                nc.scalar.activation(h_hi[:, c, :], ps_turn[:, c % 2, :], ACT.Identity, scale=ln_w, bias=ln_b)\
                    .then_inc(h_ready_hi, 1)
                act.wait_ge(h_ready_hi, c + 1)
                nc.scalar.activation(ps_turn[:, c % 2, :], ps_turn[:, c % 2, :], ACT.Identity, scale=ln_w, bias=ln_b,
                                     accum_out=None if by_token else sums[:, c:c + 1]).then_inc(h_ready, 1)
            act.sem_inc(gelu_ready, FB)
            act.wait_ge(top_ready, 1)
            nc.scalar.activation(t["ed"], t["d"], ACT.Exp).then_inc(exp_ready, 1)
            if not by_token:
                act.wait_ge(cw_turned, 1)
                nc.scalar.activation(cw_t[:, :], ps_turn[0:E, 0, :], ACT.Copy).then_inc(cwt_ready, 1)
            with act.Fori(0, CHUNKS) as i:
                for k in range(blocks):
                    e, b = k // FB, k % FB
                    act.wait_ge(up_ready, blocks * i + k + 1)
                    act.wait_ge(down_ready, blocks * i + k + 1)
                    bias = m.vecs[:, E_B1 + k:E_B1 + k + 1] if by_token else b1[:, e, b:b + 1]
                    nc.scalar.activation(hidden[:, k % ring_h, :], ps_h[:, b, :], ACT.Gelu, bias=bias)\
                        .then_inc(gelu_ready, 1)
                    if k == 0 and by_token:
                        act.wait_ge(cw_turned, i + 1)
                        nc.scalar.activation(cw_t[:, :], ps_turn[0:E, 0, :], ACT.Copy).then_inc(cwt_ready, 1)

        if not by_token:
            @block.sync
            def _(sp):
                sp.wait_ge(cw_set, 1)
                sp.wait_ge(turned, CHUNKS)
                for k in range(TOPK):
                    one = bass.ds(sp.value_load(m.ids_int[0:1, k:k + 1], min_val=0, max_val=E - 1), 1)
                    sp.dma_start(raw_w1[:, k, :], m.ins["L0_ffn_e_w1"][layer, one].rearrange("e p f -> (e p) f"))\
                        .then_inc(weights_in, 16)
                    sp.dma_start(w2[:, k, :, :], m.ins["L0_ffn_e_w2"][layer, one]
                                 .rearrange("e (i p) d -> p (e i) d", p=P)).then_inc(weights_in, 16)
                    sp.dma_start(b1[:, k, :], m.ins["L0_ffn_e_b1"][layer, one].rearrange("e (i p) -> p (e i)", p=P),
                                 allow_slow_non_contiguous=True).then_inc(weights_in, 16)
                sp.wait_ge(weights_in, 16 * 3 * TOPK)


def write_out(nc, m, out):
    with ExitStack() as ctx:
        written = ctx.enter_context(nc.semaphore("written"))
        block = ctx.enter_context(nc.Block())

        @block.sync
        def _(sp):
            sp.dma_start(out[0].rearrange("(t p) d -> p t d", p=P), m.x[:, :, :]).then_inc(written, 16)
            sp.wait_ge(written, 16)


def feed_forward(nc, m, n, load_experts=False):
    for layer in range(LAYERS):
        tag = f"{n}{layer}"
        project_qkv(nc, m, tag, first=layer == 0, layer=layer)
        attention_heads(nc, m, tag, causal=True, load_experts=load_experts and layer == 0)
        finish_attention(nc, m, tag, layer)
        experts(nc, m, tag, layer, last=layer == LAYERS - 1)


def build(nc, ins, out):
    with ExitStack() as ctx:
        m = Memory(nc, ctx, ins)
        set_up(nc, m, "s")
        stage_a(nc, m, "a")
        feed_forward(nc, m, "f", load_experts=True)
        project_qkv(nc, m, "b", layer=None)
        attention_heads(nc, m, "b", causal=False)
        finish_attention(nc, m, "b")
        feed_forward(nc, m, "g")
        write_out(nc, m, out)


def kernel(**inputs):
    import concourse.bacc as bacc
    from concourse.bass_utils import run_bass_kernel_spmd

    nc = bacc.Bacc("TRN2", target_bir_lowering=False, num_devices=1)
    arrays, ins = {}, {}
    for name, value in inputs.items():
        a = np.ascontiguousarray(value)
        arrays["in_" + name] = a
        ins[name] = nc.dram_tensor("in_" + name, a.shape, mybir.dt.from_np(a.dtype), kind="ExternalInput").ap()
    out = nc.dram_tensor("out", [1, S, D], F32, kind="ExternalOutput").ap()
    build(nc, ins, out)
    result = run_bass_kernel_spmd(nc, [arrays], core_ids=[0])
    return result.results[0]["out"]
```

```python
import numpy as np
import concourse.bass as bass
from concourse import mybir
from contextlib import ExitStack

F32 = mybir.dt.float32
BF16 = mybir.dt.bfloat16
I32 = mybir.dt.int32
F32R = mybir.dt.float32r
ALU = mybir.AluOpType
ACT = mybir.ActivationFunctionType
AXIS_X = mybir.AxisListType.X

P = 128
D = 128
S = 2048
TILES = S // P
CH = 512
CHUNKS = S // CH
TPC = CH // P
HEADS, HD = 16, 8
QUAD = 4
QUADS = HEADS // QUAD
E, FF = 8, 512
FB = FF // P
TOPK = 2
LAYERS = 2
LN_EPS = 1e-5
RMS_EPS = 1.1920929e-07
MASKED = -1e30
SOFTMAX_SCALE = HD ** -0.5

Q_PARTS = [0, 0, 0, 1, 1, 2]
K_PARTS = [1, 0, 2, 0, 1, 0]
STACK = len(Q_PARTS) * HD
SHIFT_ROW = 64

LN1_W, LN1_B, LN2_W, LN2_B, BQ, BK = (LAYERS * n for n in range(6))
B_BQ, B_BK = LAYERS * 6, LAYERS * 6 + 1
E_B1 = LAYERS * 6 + 2
N_VEC = E_B1 + E * FB


class Steps:

    def __init__(self, engine, sem, base=0):
        self.engine, self.sem, self.base, self.n = engine, sem, base, 0

    def __call__(self, instruction):
        self.n += 1
        instruction.then_inc(self.sem, 1)
        self.engine.wait_ge(self.sem, self.base + self.n)


def by_dim(ap):
    return ap.rearrange("p (h d) -> p d h", d=HD)


def token_tiles(i, n=TPC):
    return bass.ds(i * n, n)


class Memory:

    def phase_semaphores(self):
        self.previous, self.current = self.current, []

        def sem(name):
            if name not in self.named:
                self.named[name] = self.ctx.enter_context(self.nc.semaphore(name))
            self.current.append(self.named[name])
            return self.named[name]

        return sem

    def clear_previous(self, pool):
        for s in self.previous:
            pool.sem_clear(s)

    def __init__(self, nc, ctx, ins):
        self.nc, self.ctx, self.named, self.current, self.previous = nc, ctx, {}, [], []

        def sb(name, shape, dt=F32):
            return ctx.enter_context(nc.sbuf_tensor(name, shape, dt))

        self.ins = ins
        self.x = sb("x_tok", [P, TILES, D])
        self.z = sb("z_tok", [P, TILES, D])
        self.st = sb("st", [P, TILES, 6])
        self.mean = sb("mean", [P, TILES])
        self.rstd = sb("rstd", [P, TILES])
        self.ident = sb("ident", [P, P])
        self.ident_bf = sb("ident_bf", [P, P], BF16)
        self.hide_right = sb("hide_right", [P, P], BF16)
        self.hide_left = sb("hide_left", [P, P], BF16)
        self.upto = sb("upto", [P, P])
        self.ones = sb("ones", [P, P])
        self.rank = sb("rank", [P, E])
        self.neg_half = sb("neg_half", [P, TILES])
        self.w_qkv = sb("w_qkv_t", [P, 3 * D])
        self.w_swiglu = sb("w_swiglu_t", [P, 2 * D])
        self.w_out = sb("w_out_t", [P, D])
        self.vecs = sb("vecs", [P, N_VEC])
        self.vecs_dh = sb("vecs_dh", [P, N_VEC])
        self.w_att = sb("w_att", [P, LAYERS, 4, D])
        self.bv = sb("bv_rows", [P, LAYERS + 1, D])
        self.bo = sb("bo_rows", [P, LAYERS, D])
        self.w_b = sb("w_b", [P, 3, D])
        self.mix_dh = sb("mix_dh", [P, P])
        self.w_dh = sb("w_dh", [P, LAYERS, 2, D])
        self.gate_w = sb("gate_w", [P, LAYERS, E])
        self.gate_b = sb("gate_b", [P, LAYERS, E])
        self.b2 = sb("b2", [E, LAYERS, D])
        self.gate_hi = sb("gate_hi", [P, LAYERS, E], F32R)
        self.gate_lo = sb("gate_lo", [P, LAYERS, E], F32R)
        self.w1_hi = sb("w1_hi", [P, E, FF], F32R)
        self.w1_lo = sb("w1_lo", [P, E, FF], F32R)
        self.w2 = sb("w2", [P, E, FB, D])
        self.q_stack = sb("q_stack", [P, CHUNKS, QUAD, CH], BF16)
        self.k_scan = sb("k_scan", [P, QUAD, S], BF16)
        self.k_stack = sb("k_stack", [P, QUAD, S], BF16)
        self.v_all = sb("v_all", [P, TILES, D])
        self.v_quad = sb("v_quad", [P, TILES, QUAD, 32])
        self.ids_int = sb("ids_int", [1, TOPK], I32)
        self.w2_in = ctx.enter_context(nc.semaphore("w2_in"))
        self.weights_in = [ctx.enter_context(nc.semaphore(f"weights_in{k}")) for k in range(2)]
        self.weights_hi = ctx.enter_context(nc.semaphore("weights_hi"))
        self.weights_split = ctx.enter_context(nc.semaphore("weights_split"))
        self.q_dram = nc.dram_tensor("q_parts", [STACK, HEADS, S], BF16, kind="Internal").ap()
        self.k_dram = nc.dram_tensor("k_parts", [STACK, HEADS, S], BF16, kind="Internal").ap()
        self.r_dram = nc.dram_tensor("inverse_sums", [HEADS, S], F32, kind="Internal").ap()
        self.o_dram = nc.dram_tensor("attended", [HEADS, 32, S], F32, kind="Internal").ap()


REST_LOADS = 14


def set_up(nc, m, n):
    ins = m.ins
    with ExitStack() as ctx:
        raw = ctx.enter_context(nc.sbuf_tensor("raw_weights", [P, 6, D], F32))
        rows = ctx.enter_context(nc.sbuf_tensor("vector_rows", [N_VEC, D], F32))
        rows_dh = ctx.enter_context(nc.sbuf_tensor("vector_rows_dh", [N_VEC, D], F32))
        wp = ctx.enter_context(nc.sbuf_tensor("wp_rows", [P, HD], F32))
        ps = ctx.enter_context(nc.psum_tensor("setup_ps", [P, 2, 512], F32))
        sem = m.phase_semaphores()
        raw_in, turned, rest_in, built = sem("s_raw_in"), sem("s_turned"), sem("s_rest_in"), sem("s_built")
        v_zero, k_zero, rows_turned, mixed = sem("s_v_zero"), sem("s_k_zero"), sem("s_rows_turned"), sem("s_mixed")
        gate_split = sem("s_gate_split")
        x_in = sem("s_x_in")
        block = ctx.enter_context(nc.Block())

        def layer_rows(name, at):
            return rows[at:at + LAYERS, :], ins["L0_ffn_" + name]

        @block.sync
        def _(sp):
            loads = [(raw[:, 0:3, :], ins["L0_attn_a_w_qkv"].rearrange("(g p) d -> p g d", p=P)),
                     (raw[:, 3:5, :], ins["L0_attn_a_w_swiglu"].rearrange("(g p) d -> p g d", p=P)),
                     (raw[:, 5, :], ins["L0_attn_a_w_out"]),
                     layer_rows("ln1_w", LN1_W), layer_rows("ln1_b", LN1_B), layer_rows("ln2_w", LN2_W),
                     layer_rows("ln2_b", LN2_B), layer_rows("bq", BQ), layer_rows("bk", BK),
                     (rows[B_BQ:B_BQ + 1, :], ins["L0_attn_b_bq"].rearrange("(a d) -> a d", a=1)),
                     (rows[B_BK:B_BK + 1, :], ins["L0_attn_b_bk"].rearrange("(a d) -> a d", a=1)),
                     (rows[E_B1:N_VEC, :], ins["L0_ffn_e_b1"][0].rearrange("e (i p) -> (e i) p", p=P))]
            sp.dma_start(m.x[:, :, :], ins["L0_attn_a_x"][0].rearrange("(t p) d -> p t d", p=P)).then_inc(x_in, 16)
            for dst, src in loads:
                sp.dma_start(dst, src).then_inc(raw_in, 16)
            rest = [(wp[:, :], ins["L0_attn_b_Wp"].unsqueeze(0).broadcast_to([HEADS, HD, HD]))]
            for i, name in enumerate(("wq", "wk", "wv", "wo")):
                rest.append((m.w_att[:, :, i, :], ins["L0_ffn_" + name].rearrange("l p d -> p l d")))
            for i, name in enumerate(("Wq", "Wk", "Wv")):
                rest.append((m.w_b[:, i, :], ins["L0_attn_b_" + name]))
            for dst, name in ((m.bv[:, 0:LAYERS, :], "bv"), (m.bo[:, :, :], "bo"), (m.gate_b[:, :, :], "gate_b")):
                rest.append((dst, ins["L0_ffn_" + name].partition_broadcast(P)))
            rest.append((m.bv[:, LAYERS, :], ins["L0_attn_b_bv"].partition_broadcast(P)))
            rest.append((m.gate_w[:, :, :], ins["L0_ffn_gate_w"].rearrange("l p e -> p l e")))
            rest.append((m.b2[:, :, :], ins["L0_ffn_e_b2"].rearrange("l e d -> e l d")))
            assert len(rest) == REST_LOADS
            for dst, src in rest:
                sp.dma_start(dst, src).then_inc(rest_in, 16)
            sp.dma_start(m.w2[:, :, :, :], ins["L0_ffn_e_w2"][0].rearrange("e (i p) d -> p (e i) d", p=P))\
                .then_inc(m.w2_in, 16)
            sp.wait_ge(rest_in, 16 * REST_LOADS)
            sp.wait_ge(x_in, 16)

        @block.gpsimd
        def _(pool):
            m.clear_previous(pool)
            nc.gpsimd.memset(m.ident[:, :], 0.0).then_inc(built, 1)
            nc.gpsimd.memset(m.ident_bf[:, :], 0.0).then_inc(built, 1)
            nc.gpsimd.memset(m.hide_right[:, :], 0.0).then_inc(built, 1)
            nc.gpsimd.memset(m.hide_left[:, :], 0.0).then_inc(built, 1)
            nc.gpsimd.memset(m.upto[:, :], 1.0).then_inc(built, 1)
            nc.gpsimd.memset(m.ones[:, :], 1.0).then_inc(built, 1)
            pool.wait_ge(built, 6)

            def select(t, op, fill, column, row):
                nc.gpsimd.affine_select(out=t[:, :], in_=t[:, :], compare_op=op, fill=fill, base=0,
                                        pattern=[[column, P]], channel_multiplier=row).then_inc(built, 1)

            select(m.ident, ALU.not_equal, 1.0, -1, 1)
            select(m.ident_bf, ALU.not_equal, 1.0, -1, 1)
            select(m.hide_right, ALU.is_ge, MASKED, -1, 1)
            select(m.hide_left, ALU.is_ge, MASKED, 1, -1)
            select(m.upto, ALU.is_ge, 0.0, 1, -1)
            for e in range(E):
                nc.gpsimd.memset(m.rank[:, e:e + 1], float(E - e))
            nc.gpsimd.memset(m.neg_half[:, :], -0.5)
            nc.gpsimd.memset(m.v_quad[:, :, :, :], 0.0).then_inc(v_zero, 1)
            pool.wait_ge(v_zero, 1)
            nc.gpsimd.memset(m.v_quad[:, :, :, HD:HD + 1], 1.0)
            nc.gpsimd.memset(m.k_stack[:, :, :].bitcast(F32), 0.0).then_inc(k_zero, 1)
            nc.gpsimd.memset(m.q_stack[:, :, :, :].bitcast(F32), 0.0)
            pool.wait_ge(mixed, 1)
            by_head = m.mix_dh[:, :].rearrange("p (d h) -> p d h", d=HD)
            for base, row, column in ((0, 1, -HD), (HD - 1, -1, HD)):
                nc.gpsimd.affine_select(out=by_head, in_=by_head, compare_op=ALU.is_ge, fill=0.0, base=base,
                                        pattern=[[0, HD], [column, HEADS]], channel_multiplier=row).then_inc(mixed, 1)
                pool.wait_ge(mixed, 2 if row == 1 else 3)

        @block.vector
        def _(dve):
            nc.vector.memset(m.k_scan[:, :, :].bitcast(F32), 0.0)
            dve.wait_ge(x_in, 16)
            for c in range(CHUNKS):
                chunk_stats(nc, m, m.x, c)
            dve.wait_ge(k_zero, 1)
            nc.vector.memset(m.k_stack[SHIFT_ROW:SHIFT_ROW + 1, :, :], 1.0)
            dve.wait_ge(rest_in, 16 * REST_LOADS)
            nc.vector.tensor_copy(m.gate_hi[:, :, :], m.gate_w[:, :, :]).then_inc(gate_split, 1)
            dve.wait_ge(gate_split, 1)
            nc.vector.tensor_tensor(m.gate_lo[:, :, :], m.gate_w[:, :, :], m.gate_hi[:, :, :].bitcast(F32),
                                    ALU.subtract)

        @block.tensor
        def _(pe):
            pe.wait_ge(built, 7)
            pe.wait_ge(raw_in, 16 * 12)
            for g in range(6):
                nc.tensor.transpose(ps[:, g // 4, (g % 4) * P:(g % 4 + 1) * P], raw[:, g, :], m.ident[:, :])\
                    .then_inc(turned, 1)
            nc.tensor.transpose(ps[:, 1, 256:256 + N_VEC], rows[:, :], m.ident[0:N_VEC, 0:N_VEC]).then_inc(turned, 1)
            pe.wait_ge(rows_turned, 1)
            nc.tensor.transpose(ps[:, 1, 320:320 + N_VEC], rows_dh[:, :], m.ident[0:N_VEC, 0:N_VEC])\
                .then_inc(turned, 1)

        @block.scalar
        def _(act):
            act.wait_ge(raw_in, 16 * 12)
            nc.scalar.activation(rows_dh[:, :].rearrange("p (d h) -> p d h", d=HD), by_dim(rows[:, :]), ACT.Copy)\
                .then_inc(rows_turned, 1)
            act.wait_ge(turned, 8)
            nc.scalar.activation(m.w_qkv[:, :], ps[:, 0, 0:3 * P], ACT.Copy)
            nc.scalar.activation(m.w_swiglu[:, 0:P], ps[:, 0, 3 * P:4 * P], ACT.Copy)
            nc.scalar.activation(m.w_swiglu[:, P:2 * P], ps[:, 1, 0:P], ACT.Copy)
            nc.scalar.activation(m.w_out[:, :], ps[:, 1, P:2 * P], ACT.Copy)
            nc.scalar.activation(m.vecs[:, :], ps[:, 1, 256:256 + N_VEC], ACT.Copy)
            nc.scalar.activation(m.vecs_dh[:, :], ps[:, 1, 320:320 + N_VEC], ACT.Copy)
            act.wait_ge(rest_in, 16 * REST_LOADS)
            for layer in range(LAYERS):
                for k in range(2):
                    nc.scalar.activation(m.w_dh[:, layer, k, :].rearrange("p (d h) -> p d h", d=HD),
                                         by_dim(m.w_att[:, layer, k, :]), ACT.Copy)
            nc.scalar.activation(m.mix_dh[:, :].rearrange("p (d h) -> p d h", d=HD),
                                 wp[:, :].unsqueeze(2).broadcast_to([P, HD, HEADS]), ACT.Copy).then_inc(mixed, 1)


def row_moments(nc, step, st, mean, var, t1, t2, eps):
    step(nc.vector.tensor_tensor(t1, st[:, :, 1], st[:, :, 4], ALU.subtract))
    step(nc.vector.tensor_tensor(mean, st[:, :, 1], st[:, :, 4], ALU.add))
    step(nc.vector.tensor_tensor(t2, st[:, :, 2], st[:, :, 5], ALU.add))
    step(nc.vector.tensor_scalar(t2, t2, 1.0 / D, None, ALU.mult))
    step(nc.vector.scalar_tensor_tensor(t1, t1, 0.25, t1, ALU.mult, ALU.mult))
    step(nc.vector.tensor_scalar(mean, mean, 0.5, None, ALU.mult))
    return nc.vector.scalar_tensor_tensor(var, t1, eps, t2, ALU.add, ALU.add)


def inverse_root(nc, pool, m, out, in_, in_ready, out_ready, count):
    pool.wait_ge(in_ready, count)
    nc.gpsimd.tensor_tensor(out, in_, m.neg_half[:, 0:out.shape[-1]], ALU.pow).then_inc(out_ready, 1)


def chunk_stats(nc, m, src, c):
    for t in range(c * TPC, (c + 1) * TPC):
        nc.vector.bn_stats(m.st[:, t, :], src[:, t, :])


def token_stats(nc, step, m, tmp, var_ready, rstd_ready, count):
    row_moments(nc, step, m.st, m.mean[:, :], tmp[:, 0, :], tmp[:, 1, :], tmp[:, 2, :], LN_EPS).then_inc(var_ready, 1)
    step.engine.wait_ge(rstd_ready, count)


def normalise(nc, step, dst, src, m):
    for t in range(TILES):
        last = nc.vector.tensor_scalar(dst[:, t, :], src[:, t, :], m.mean[:, t:t + 1], m.rstd[:, t:t + 1],
                                       ALU.subtract, ALU.mult)
    step(last)


def stage_a(nc, m, n):
    with ExitStack() as ctx:
        def sb(name, shape, dt=F32):
            return ctx.enter_context(nc.sbuf_tensor(name + n, shape, dt))

        sem = m.phase_semaphores()

        hn = sb("a_hn", [P, TILES, D])
        st8 = sb("a_st8", [P, 2 * TPC, 6])
        tmp = sb("a_tmp", [P, 3, TILES])
        tmp8 = sb("a_tmp8", [P, 4, 2 * TPC])
        rms = sb("a_rms", [P, 2, 2 * TPC])
        rh = sb("a_rh", [P, TILES])
        plus, minus = sb("a_plus", [P, TILES]), sb("a_minus", [P, TILES])
        hn_t = sb("a_hn_t", [P, CH])
        wkv = sb("a_wkv", [P, TPC, 2 * D])
        eq = sb("a_eq", [P, TPC, D])
        run = sb("a_run", [P, 2 * TPC, 2 * D])
        den = sb("a_den", [P, TPC, D])
        y = sb("a_y", [P, TPC, D])
        y_t = sb("a_y_t", [P, CH])
        eg = sb("a_eg", [P, TPC, D])
        ug = sb("a_ug", [P, TPC, D])
        g_t = sb("a_g_t", [P, CH])
        ps_qk = ctx.enter_context(nc.psum_tensor("a_ps_qk" + n, [P, TPC, 2 * D], F32))
        ps_v = ctx.enter_context(nc.psum_tensor("a_ps_v" + n, [P, TPC, D], F32))
        ps_pair = ctx.enter_context(nc.psum_tensor("a_ps_pair" + n, [P, 2, TPC, 2 * D], F32))
        ps_out = ctx.enter_context(nc.psum_tensor("a_ps_out" + n, [P, CH], F32))
        hn_ready, hn_turned, hn_copied = sem("a_hn_ready"), sem("a_hn_turned"), sem("a_hn_copied")
        qkv_ready, scales_ready, exps_ready, v_used = (sem(s) for s in ("a_qkv_ready", "a_scales_ready",
                                                                        "a_exps_ready", "a_v_used"))
        sums_in, summed, y_ready = sem("a_sums_in"), sem("a_summed"), sem("a_y_ready")
        y_turned, y_copied, uv_ready = sem("a_y_turned"), sem("a_y_copied"), sem("a_uv_ready")
        neg_ready, gate_ready, ug_ready = sem("a_neg_ready"), sem("a_gate_ready"), sem("a_ug_ready")
        ug_turned, ug_copied, out_ready = sem("a_ug_turned"), sem("a_ug_copied"), sem("a_out_ready")
        x_added, dve_steps = sem("a_x_added"), sem("a_dve_steps")
        var_ready, rstd_ready = sem("a_var_ready"), sem("a_rstd_ready")
        block = ctx.enter_context(nc.Block())

        def turned_in(c):
            return ps_pair[:, c % 2, 0:2, :].rearrange("p t f -> p (t f)")

        def stages(t):
            return [t - k if 0 <= t - k < CHUNKS else None for k in range(4)]

        @block.vector
        def _(dve):
            step = Steps(dve, dve_steps)
            step(nc.vector.memset(run[:, 0, :], 0.0))
            token_stats(nc, step, m, tmp, var_ready, rstd_ready, 1)
            step(nc.vector.tensor_tensor(tmp[:, 1, :], tmp[:, 1, :], tmp[:, 2, :], ALU.add))
            step(nc.vector.tensor_tensor(tmp[:, 2, :], m.rstd[:, :], m.rstd[:, :], ALU.mult))
            step(nc.vector.tensor_tensor(tmp[:, 1, :], tmp[:, 1, :], tmp[:, 2, :], ALU.mult))
            nc.vector.tensor_scalar(tmp[:, 0, :], tmp[:, 1, :], RMS_EPS, None, ALU.add).then_inc(var_ready, 1)
            step(nc.vector.tensor_scalar(plus[:, :], m.rstd[:, :], 1.0, None, ALU.add))
            step(nc.vector.tensor_tensor(minus[:, :], m.rstd[:, :], m.mean[:, :], ALU.mult))
            dve.wait_ge(rstd_ready, 2)
            step(nc.vector.tensor_tensor(rh[:, :], rh[:, :], m.rstd[:, :], ALU.mult))
            for t in range(TILES):
                last = nc.vector.tensor_scalar(hn[:, t, :], m.x[:, t, :], m.mean[:, t:t + 1], rh[:, t:t + 1],
                                               ALU.subtract, ALU.mult)
                if t % TPC == TPC - 1:
                    last.then_inc(hn_ready, 1)
            dve.wait_ge(hn_ready, CHUNKS)
            for t in range(TILES):
                last = nc.vector.tensor_scalar(m.x[:, t, :], m.x[:, t, :], plus[:, t:t + 1], minus[:, t:t + 1],
                                               ALU.mult, ALU.subtract)
            step(last)

            def divide(c):
                sums = ps_pair[:, c % 2, :, :]
                dve.wait_ge(summed, c + 1)
                step(nc.vector.scalar_tensor_tensor(den[:, :, :], sums[:, :, 0:D], 1e-6, eq[:, :, :],
                                                    ALU.add, ALU.mult))
                step(nc.vector.reciprocal(den[:, :, :], den[:, :, :]))
                if c:
                    dve.wait_ge(y_turned, c)
                nc.vector.tensor_tensor(y[:, :, :], sums[:, :, D:2 * D], den[:, :, :], ALU.mult).then_inc(y_ready, 1)

            def scales(c):
                dve.wait_ge(qkv_ready, c + 1)
                for r in range(TPC):
                    for k in range(2):
                        last = nc.vector.bn_stats(st8[:, 2 * r + k, :], ps_qk[:, r, k * D:(k + 1) * D])
                step(last)
                step(row_moments(nc, step, st8, tmp8[:, 0, :], tmp8[:, 1, :], tmp8[:, 2, :], tmp8[:, 3, :], RMS_EPS))
                step(nc.vector.tensor_tensor(tmp8[:, 2, :], tmp8[:, 0, :], tmp8[:, 0, :], ALU.mult))
                nc.vector.tensor_tensor(tmp8[:, 1, :], tmp8[:, 1, :], tmp8[:, 2, :], ALU.add).then_inc(var_ready, 1)

            def add(c):
                tiles = m.x[:, c * TPC:(c + 1) * TPC, :]
                dve.wait_ge(out_ready, c + 1)
                nc.vector.tensor_tensor(tiles, tiles, ps_out[:, :].rearrange("p (t d) -> p t d", d=D), ALU.add)\
                    .then_inc(x_added, 1)
                dve.wait_ge(x_added, c + 1)
                chunk_stats(nc, m, m.x, c)

            for t in range(CHUNKS + 3):
                _, weigh, split, gate = stages(t)
                if gate is not None:
                    g = ps_pair[:, gate % 2, :, D:2 * D]
                    dve.wait_ge(uv_ready, gate + 1)
                    if gate:
                        dve.wait_ge(ug_ready, gate)
                    nc.vector.tensor_scalar(eg[:, :, :], g, -1.0, 80.0, ALU.mult, ALU.min).then_inc(neg_ready, 1)
                if split is not None:
                    divide(split)
                if gate:
                    add(gate - 1)
                if weigh is not None:
                    scales(weigh)
                if gate is not None:
                    dve.wait_ge(gate_ready, gate + 1)
                    step(nc.vector.tensor_scalar(eg[:, :, :], eg[:, :, :], 1.0, None, ALU.add))
                    step(nc.vector.reciprocal(eg[:, :, :], eg[:, :, :]))
                    step(nc.vector.tensor_tensor(eg[:, :, :], eg[:, :, :], g, ALU.mult))
                    if gate:
                        dve.wait_ge(ug_turned, gate)
                    nc.vector.tensor_tensor(ug[:, :, :], eg[:, :, :], ps_pair[:, gate % 2, :, 0:D], ALU.mult)\
                        .then_inc(ug_ready, 1)
                if weigh is not None:
                    dve.wait_ge(rstd_ready, weigh + 3)
                    nc.vector.tensor_scalar(rms[:, 1, :], rms[:, 0, :], -1.0, None, ALU.mult).then_inc(scales_ready, 1)
                if weigh is not None:
                    dve.wait_ge(exps_ready, weigh + 1)
                    nc.vector.tensor_tensor(wkv[:, :, D:2 * D], wkv[:, :, 0:D], ps_v[:, :, :], ALU.mult)\
                        .then_inc(v_used, 1)
                    dve.wait_ge(v_used, weigh + 1)
                    for r in range(TPC):
                        k = TPC * weigh + r
                        if k < TILES - 1:
                            step(nc.vector.tensor_tensor(run[:, (k + 1) % (2 * TPC), :], run[:, k % (2 * TPC), :],
                                                         wkv[:, r, :], ALU.add))
                    nc.vector.tensor_scalar(eq[:, :, :], eq[:, :, :], 1.0, None, ALU.add).then_inc(sums_in, 1)
                    dve.wait_ge(sums_in, weigh + 1)
            add(CHUNKS - 1)

        @block.gpsimd
        def _(pool):
            m.clear_previous(pool)
            inverse_root(nc, pool, m, m.rstd[:, :], tmp[:, 0, :], var_ready, rstd_ready, 1)
            inverse_root(nc, pool, m, rh[:, :], tmp[:, 0, :], var_ready, rstd_ready, 2)
            for c in range(CHUNKS):
                inverse_root(nc, pool, m, rms[:, 0, :], tmp8[:, 1, :], var_ready, rstd_ready, c + 3)

        @block.tensor
        def _(pe):
            for t in range(CHUNKS + 3):
                project, weigh, split, gate = stages(t)
                if project is not None:
                    pe.wait_ge(hn_ready, project + 1)
                    for r in range(TPC):
                        last = nc.tensor.transpose(ps_out[:, r * P:(r + 1) * P], hn[:, project * TPC + r, :],
                                                   m.ident[:, :])
                    last.then_inc(hn_turned, 1)
                if split is not None:
                    pe.wait_ge(y_ready, split + 1)
                    for r in range(TPC):
                        last = nc.tensor.transpose(turned_in(split)[:, r * P:(r + 1) * P], y[:, r, :], m.ident[:, :])
                    last.then_inc(y_turned, 1)
                    pe.wait_ge(y_copied, split + 1)
                    for r in range(TPC):
                        last = nc.tensor.matmul(ps_pair[:, split % 2, r, :], y_t[:, r * P:(r + 1) * P],
                                                m.w_swiglu[:, :], start=True, stop=True)
                    last.then_inc(uv_ready, 1)
                if gate is not None:
                    pe.wait_ge(ug_ready, gate + 1)
                    for r in range(TPC):
                        last = nc.tensor.transpose(turned_in(gate)[:, r * P:(r + 1) * P], ug[:, r, :], m.ident[:, :])
                    last.then_inc(ug_turned, 1)
                if weigh is not None:
                    pe.wait_ge(v_used, weigh + 1)
                    if weigh >= 2:
                        pe.wait_ge(ug_copied, weigh - 1)
                    for r in range(TPC):
                        nc.tensor.matmul(ps_pair[:, weigh % 2, r, :], m.upto[:, :], wkv[:, r, :],
                                         start=r % 2 == 0, stop=False, skip_group_check=True)
                    pe.wait_ge(sums_in, weigh + 1)
                    for r in range(TPC):
                        last = nc.tensor.matmul(ps_pair[:, weigh % 2, r, :], m.ones[:, :],
                                                run[:, (TPC * weigh + r) % (2 * TPC), :], start=False, stop=True,
                                                skip_group_check=True)
                    last.then_inc(summed, 1)
                if gate is not None:
                    pe.wait_ge(ug_copied, gate + 1)
                    if gate:
                        pe.wait_ge(x_added, gate)
                    pe.wait_ge(hn_copied, min(t + 1, CHUNKS))
                    for r in range(TPC):
                        last = nc.tensor.matmul(ps_out[:, r * P:(r + 1) * P], g_t[:, r * P:(r + 1) * P],
                                                m.w_out[:, :], start=True, stop=True)
                    last.then_inc(out_ready, 1)
                if project is not None:
                    pe.wait_ge(hn_copied, project + 1)
                    if project:
                        pe.wait_ge(exps_ready, project)
                        pe.wait_ge(v_used, project)
                    for r in range(TPC):
                        nc.tensor.matmul(ps_qk[:, r, :], hn_t[:, r * P:(r + 1) * P], m.w_qkv[:, 0:2 * D],
                                         start=True, stop=True)
                        last = nc.tensor.matmul(ps_v[:, r, :], hn_t[:, r * P:(r + 1) * P], m.w_qkv[:, 2 * D:3 * D],
                                                start=True, stop=True)
                    last.then_inc(qkv_ready, 1)

        @block.scalar
        def _(act):
            for t in range(CHUNKS + 3):
                project, weigh, split, gate = stages(t)
                if project is not None:
                    act.wait_ge(hn_turned, project + 1)
                    if project:
                        act.wait_ge(qkv_ready, project)
                    nc.scalar.activation(hn_t[:, :], ps_out[:, :], ACT.Copy).then_inc(hn_copied, 1)
                if gate is not None:
                    act.wait_ge(neg_ready, gate + 1)
                    nc.scalar.activation(eg[:, :, :], eg[:, :, :], ACT.Exp).then_inc(gate_ready, 1)
                if split is not None:
                    act.wait_ge(y_turned, split + 1)
                    if split:
                        act.wait_ge(uv_ready, split)
                    nc.scalar.activation(y_t[:, :], turned_in(split), ACT.Copy).then_inc(y_copied, 1)
                if weigh is not None:
                    act.wait_ge(scales_ready, weigh + 1)
                    if weigh:
                        act.wait_ge(summed, weigh)
                        act.wait_ge(y_ready, weigh)
                    for r in range(TPC):
                        nc.scalar.activation(wkv[:, r, 0:D], ps_qk[:, r, D:2 * D], ACT.Exp,
                                             scale=rms[:, 0, 2 * r + 1:2 * r + 2])
                        last = nc.scalar.activation(eq[:, r, :], ps_qk[:, r, 0:D], ACT.Exp,
                                                    scale=rms[:, 1, 2 * r:2 * r + 1])
                    last.then_inc(exps_ready, 1)
                if gate is not None:
                    act.wait_ge(ug_turned, gate + 1)
                    if gate:
                        act.wait_ge(out_ready, gate)
                    nc.scalar.activation(g_t[:, :], turned_in(gate), ACT.Copy).then_inc(ug_copied, 1)


def project_qkv(nc, m, n, first=None, layer=None):
    mixing = layer is None
    src = m.x if mixing or first else m.z
    with ExitStack() as ctx:
        def sb(name, shape, dt=F32):
            return ctx.enter_context(nc.sbuf_tensor(name + n, shape, dt))

        sem = m.phase_semaphores()

        tmp = sb("p_tmp", [P, 3, TILES])
        scale = sb("p_scale", [P, TILES]) if first else m.rstd
        hn = sb("p_hn", [P, 2, TPC, D])
        h_t = sb("p_h_t", [P, 2, CH])
        raw = sb("p_raw", [P, 2, CH])
        rest = sb("p_rest", [P, 2, CH])
        parts = sb("p_parts", [P, 2, 2, 3, CH], BF16)
        ps_turn = ctx.enter_context(nc.psum_tensor("p_ps_turn" + n, [P, CH], F32))
        ps_qk = ctx.enter_context(nc.psum_tensor("p_ps_qk" + n, [P, 2, 2, CH], F32))
        ps_mixed = ctx.enter_context(nc.psum_tensor("p_ps_mixed" + n, [P, 2, CH], F32))
        ps_v = ctx.enter_context(nc.psum_tensor("p_ps_v" + n, [P, TPC, D], F32))
        hn_ready, turned, h_ready = sem("p_hn_ready"), sem("p_turned"), sem("p_h_ready")
        qk_ready, raw_ready, mixed = sem("p_qk_ready"), sem("p_raw_ready"), sem("p_mixed")
        v_ready, high_ready = sem("p_v_ready"), sem("p_high_ready")
        rest_ready, mid_ready, low_ready = sem("p_rest_ready"), sem("p_mid_ready"), sem("p_low_ready")
        v_kept, dve_steps = sem("p_v_kept"), sem("p_dve_steps")
        written = [[sem(f"p_written{k}{slot}") for slot in range(2)] for k in range(2)]
        var_ready, rstd_ready = sem("p_var_ready"), sem("p_rstd_ready")
        block = ctx.enter_context(nc.Block())
        weights = [m.w_b[:, i, :] if mixing else m.w_dh[:, layer, i, :] for i in range(2)]
        weights.append(m.w_b[:, 2, :] if mixing else m.w_att[:, layer, 2, :])
        bias = [(m.vecs if mixing else m.vecs_dh)[:, c:c + 1]
                for c in ((B_BQ, B_BK) if mixing else (BQ + layer, BK + layer))]
        bv = m.bv[:, LAYERS if mixing else layer, :]

        def projected(c, k):
            return ps_mixed[:, k, :] if mixing else ps_qk[:, c % 2, k, :]

        def write_part(sp, c, k, part):
            dram, parts_of = ((m.q_dram, Q_PARTS), (m.k_dram, K_PARTS))[k]
            places = [g for g, of in enumerate(parts_of) if of == part]
            stride = places[1] - places[0] if len(places) > 1 else 1
            dst = dram.rearrange("(g d) h q -> (d h) g q", d=HD)[:, places[0]:places[-1] + 1:stride,
                                                               c * CH:(c + 1) * CH]
            sp.dma_start(dst, parts[:, c % 2, k, part:part + 1, :].broadcast_to([P, len(places), CH]))\
                .then_inc(written[k][c % 2], 16)

        @block.gpsimd
        def _(pool):
            m.clear_previous(pool)
            inverse_root(nc, pool, m, m.rstd[:, :], tmp[:, 0, :], var_ready, rstd_ready, 1)
            if first:
                inverse_root(nc, pool, m, scale[:, :], tmp[:, 0, :], var_ready, rstd_ready, 2)

        @block.sync
        def _(sp):
            for c in range(CHUNKS):
                for part, ready in enumerate((high_ready, mid_ready, low_ready)):
                    for k in range(2):
                        sp.wait_ge(ready, 2 * c + k + 1)
                        write_part(sp, c, k, part)
            for k in range(2):
                for slot in range(2):
                    sp.wait_ge(written[k][slot], 16 * 3 * CHUNKS // 2)

        @block.vector
        def _(dve):
            step = Steps(dve, dve_steps)
            token_stats(nc, step, m, tmp, var_ready, rstd_ready, 1)
            if first:
                step(nc.vector.tensor_tensor(tmp[:, 1, :], tmp[:, 1, :], tmp[:, 2, :], ALU.add))
                step(nc.vector.tensor_tensor(tmp[:, 2, :], m.rstd[:, :], m.rstd[:, :], ALU.mult))
                step(nc.vector.tensor_tensor(tmp[:, 1, :], tmp[:, 1, :], tmp[:, 2, :], ALU.mult))
                nc.vector.tensor_scalar(tmp[:, 0, :], tmp[:, 1, :], LN_EPS, None, ALU.add).then_inc(var_ready, 1)
                normalise(nc, step, m.z, m.x, m)
                dve.wait_ge(rstd_ready, 2)
                step(nc.vector.tensor_tensor(scale[:, :], scale[:, :], m.rstd[:, :], ALU.mult))

            def normalise_chunk(c):
                if c >= 2:
                    dve.wait_ge(turned, c - 1)
                for r in range(TPC):
                    t = c * TPC + r
                    last = nc.vector.tensor_scalar(hn[:, c % 2, r, :], src[:, t, :], m.mean[:, t:t + 1],
                                                   scale[:, t:t + 1], ALU.subtract, ALU.mult)
                last.then_inc(hn_ready, 1)

            normalise_chunk(0)
            normalise_chunk(1)
            for c in range(CHUNKS):
                if mixing:
                    for k in range(2):
                        dve.wait_ge(qk_ready, 2 * c + k + 1)
                        nc.vector.tensor_scalar(raw[:, k, :], ps_qk[:, c % 2, k, :], bias[k], None, ALU.add)\
                            .then_inc(raw_ready, 1)
                dve.wait_ge(v_ready, c + 1)
                nc.vector.tensor_tensor(m.v_all[:, c * TPC:(c + 1) * TPC, :], ps_v[:, :, :],
                                        bv.unsqueeze(1).broadcast_to([P, TPC, D]), ALU.add).then_inc(v_kept, 1)
                if c + 2 < CHUNKS:
                    normalise_chunk(c + 2)
                for k in range(2):
                    dve.wait_ge(high_ready, 2 * c + k + 1)
                    if c:
                        dve.wait_ge(low_ready, 2 * (c - 1) + k + 1)
                    if mixing:
                        nc.vector.tensor_tensor(rest[:, k, :], projected(c, k), parts[:, c % 2, k, 0, :],
                                                ALU.subtract).then_inc(rest_ready, 1)
                    else:
                        nc.vector.scalar_tensor_tensor(rest[:, k, :], projected(c, k), bias[k],
                                                       parts[:, c % 2, k, 0, :], ALU.add, ALU.subtract)\
                            .then_inc(rest_ready, 1)
                for k in range(2):
                    dve.wait_ge(mid_ready, 2 * c + k + 1)
                    nc.vector.tensor_tensor(parts[:, c % 2, k, 2, :], rest[:, k, :], parts[:, c % 2, k, 1, :],
                                            ALU.subtract).then_inc(low_ready, 1)

        @block.tensor
        def _(pe):
            def transpose_chunk(c):
                pe.wait_ge(hn_ready, c + 1)
                if c:
                    pe.wait_ge(h_ready, c)
                for r in range(TPC):
                    last = nc.tensor.transpose(ps_turn[:, r * P:(r + 1) * P], hn[:, c % 2, r, :], m.ident[:, :])
                last.then_inc(turned, 1)

            transpose_chunk(0)
            transpose_chunk(1)
            for c in range(CHUNKS):
                pe.wait_ge(h_ready, c + 1)
                if c >= 2:
                    pe.wait_ge(raw_ready if mixing else rest_ready, 2 * (c - 1))
                for k in range(2):
                    nc.tensor.matmul(ps_qk[:, c % 2, k, :], weights[k],
                                     h_t[:, c % 2, :], start=True, stop=True)\
                        .then_inc(qk_ready, 1)
                if c:
                    pe.wait_ge(v_kept, c)
                for r in range(TPC):
                    last = nc.tensor.matmul(ps_v[:, r, :], h_t[:, c % 2, r * P:(r + 1) * P], weights[2],
                                            start=True, stop=True)
                last.then_inc(v_ready, 1)
                if mixing:
                    for k in range(2):
                        pe.wait_ge(raw_ready, 2 * c + k + 1)
                        if c:
                            pe.wait_ge(rest_ready, 2 * (c - 1) + k + 1)
                        nc.tensor.matmul(ps_mixed[:, k, :], m.mix_dh[:, :], raw[:, k, :], start=True, stop=True)\
                            .then_inc(mixed, 1)
                if c + 2 < CHUNKS:
                    transpose_chunk(c + 2)

        @block.scalar
        def _(act):
            def copy_chunk(c):
                act.wait_ge(turned, c + 1)
                if c >= 2:
                    act.wait_ge(v_ready, c - 1)
                if mixing:
                    nc.scalar.activation(h_t[:, c % 2, :], ps_turn[:, :], ACT.Copy).then_inc(h_ready, 1)
                else:
                    nc.scalar.activation(h_t[:, c % 2, :], ps_turn[:, :], ACT.Identity,
                                         scale=m.vecs[:, LN1_W + layer:LN1_W + layer + 1],
                                         bias=m.vecs[:, LN1_B + layer:LN1_B + layer + 1]).then_inc(h_ready, 1)

            copy_chunk(0)
            copy_chunk(1)
            for c in range(CHUNKS):
                for k in range(2):
                    act.wait_ge(mixed if mixing else qk_ready, 2 * c + k + 1)
                    if c >= 2:
                        act.wait_ge(written[k][c % 2], 16 * 3 * (c // 2))
                    if mixing:
                        nc.scalar.activation(parts[:, c % 2, k, 0, :], projected(c, k), ACT.Copy)\
                            .then_inc(high_ready, 1)
                    else:
                        nc.scalar.activation(parts[:, c % 2, k, 0, :], projected(c, k), ACT.Identity, bias=bias[k])\
                            .then_inc(high_ready, 1)
                if c + 2 < CHUNKS:
                    copy_chunk(c + 2)
                for k in range(2):
                    act.wait_ge(rest_ready, 2 * c + k + 1)
                    nc.scalar.activation(parts[:, c % 2, k, 1, :], rest[:, k, :], ACT.Copy).then_inc(mid_ready, 1)


SCAN_KEYS = 512
RING_A = 4
RING_S, RING_P = 3, 8
PACING = {True: (88, 2500, 600, 0.9), False: (72, 3500, 600, 1.0)}


def attention_schedule(causal, last_quad):
    lead, margin, reload, hurry = PACING[causal]
    blocks = [TPC * (c + 1) if causal else TILES for c in range(CHUNKS)]

    pieces = []
    for c in range(CHUNKS):
        for j in range(QUAD):
            for t in range(TPC):
                keys = (TPC * c + t + 1) * P if causal else S
                for p in range(-(-keys // SCAN_KEYS)):
                    pieces.append((c, j, t, p, min(SCAN_KEYS, keys - SCAN_KEYS * p)))
    units = [(c, kb, j) for c in range(CHUNKS) for kb in range(blocks[c]) for j in range(QUAD)]

    def unit_cost(c, kb):
        return (CH - (max(0, kb - TPC * c) * P if causal else 0)) + 40

    starts, total = [], 0
    for c, kb, j in units:
        starts.append(total)
        total += unit_cost(c, kb)
    begins = [starts[units.index((c, 0, 0))] for c in range(CHUNKS)] + [total]
    own, following = pieces[lead:], ([] if last_quad else pieces[:lead])
    work = [(x, False) for x in own] + [(x, True) for x in following]
    costs = [x[4] + 60 for x, _ in work]
    pace = total / sum(x[4] + 60 for x in pieces)
    even, at = [], 0.0
    for cost in costs:
        even.append(at)
        at += cost * pace
    latest, bound = [0.0] * len(work), float(total)
    for i in range(len(work) - 1, -1, -1):
        (c, *_), nxt = work[i]
        if not nxt:
            bound = min(bound, begins[c] - margin)
        bound -= costs[i] * hurry
        latest[i] = bound
    times = []
    for i, ((c, *_), nxt) in enumerate(work):
        when = min(even[i], latest[i])
        if nxt:
            when = max(when, begins[c + 1] + reload)
        times.append(max(when, times[-1] if times else when))

    order, pending, given = [], None, 0

    def give(upto_time):
        nonlocal given
        while given < len(work) and times[given] <= upto_time:
            (c, j, t, p, width), nxt = work[given]
            order.append(("scan", c, j, t, p, width, nxt))
            given += 1
            if given == len(work) or work[given][0][0] != c:
                if (c, j, t) == (c, QUAD - 1, TPC - 1):
                    order.append(("rows", c, nxt))

    for u, (c, kb, j) in enumerate(units):
        order.append(("scores", c, kb, j))
        give(starts[u])
        if j == QUAD - 1:
            if pending:
                order.append(("values", *pending))
                if pending[1] == blocks[pending[0]] - 1:
                    order.append(("drain", pending[0]))
            pending = (c, kb)
    give(float("inf"))
    order += [("values", *pending), ("drain", pending[0])]
    first = []
    for i, (c, j, t, p, width) in enumerate(pieces[:lead]):
        first.append(("scan", c, j, t, p, width, False))
        if pieces[i + 1][0] != c:
            first.append(("rows", c, False))
    return first, order, blocks


def split_expert_weights(nc, m, pool, raw):
    pieces = [(m.ins["L0_ffn_e_w1"][0, e], m.w1_hi[:, e, :], m.w1_lo[:, e, :]) for e in range(E)]

    def place(k):
        return raw[:, k % 2, :]

    for k in range(2):
        pool.dma_start(place(k), pieces[k][0]).then_inc(m.weights_in[k], 16)
    for k, (_, hi, lo) in enumerate(pieces):
        pool.wait_ge(m.weights_in[k % 2], 16 * (k // 2 + 1))
        nc.gpsimd.tensor_copy(hi, place(k)).then_inc(m.weights_hi, 1)
        pool.wait_ge(m.weights_hi, k + 1)
        nc.gpsimd.tensor_tensor(lo, place(k), hi.bitcast(F32), ALU.subtract).then_inc(m.weights_split, 1)
        if k + 2 < len(pieces):
            pool.wait_ge(m.weights_split, k + 1)
            pool.dma_start(place(k), pieces[k + 2][0]).then_inc(m.weights_in[k % 2], 16)


def attention_heads(nc, m, n, causal, load_experts=False):
    first, order, blocks = attention_schedule(causal, False)
    _, order_last, _ = attention_schedule(causal, True)
    scans_first = sum(x[0] == "scan" for x in first)
    scans = sum(x[0] == "scan" for x in order)
    units = QUAD * sum(blocks)
    before = [QUAD * sum(blocks[:c]) for c in range(CHUNKS)]

    def unit(c, kb, j):
        return before[c] + kb * QUAD + j

    def previous(u, ring):
        return u - ring if u >= ring else u + ring * ((units - 1 - u) // ring) - units

    with ExitStack() as ctx:
        def sb(name, shape, dt=F32):
            return ctx.enter_context(nc.sbuf_tensor(name + n, shape, dt))

        sem = m.phase_semaphores()

        probs = sb("h_probs", [P, RING_P, CH])
        maxima = sb("h_maxima", [P, 2, QUAD * TPC, S // SCAN_KEYS])
        negated = sb("h_negated", [P, 32], BF16)
        neg_rows = sb("h_neg_rows", [P, 2, 32], BF16)
        drained_sb = sb("h_drained", [P, 2, CH])
        raw_weights = sb("h_raw_weights", [P, 2, FF]) if load_experts else None
        ps_scan = ctx.enter_context(nc.psum_tensor("h_ps_scan" + n, [P, RING_A, SCAN_KEYS], F32))
        ps_scores = ctx.enter_context(nc.psum_tensor("h_ps_scores" + n, [P, RING_S, CH], F32))
        ps_values = ctx.enter_context(nc.psum_tensor("h_ps_values" + n, [P, CH], F32))
        scanned, reduced, scored, exped, valued = (sem(s) for s in ("h_scanned", "h_reduced", "h_scored", "h_exped",
                                                                    "h_valued"))
        drained, neg_ready, neg_turned, v_in = (sem(s) for s in ("h_drained_", "h_neg_ready", "h_neg_turned", "h_v_in"))
        q_in = [sem(f"h_q_in{c}") for c in range(CHUNKS)]
        scan_in = [sem(f"h_scan_in{j}") for j in range(QUAD)]
        k_in = [sem(f"h_k_in{c}") for c in range(CHUNKS)]
        rows_in = [sem(f"h_rows_in{c}") for c in range(CHUNKS)]
        out_done = [sem(f"h_out_done{c}") for c in range(2)]
        block = ctx.enter_context(nc.Block())

        def cols(c):
            return slice(c * CH, (c + 1) * CH)

        @block.tensor
        def _(pe):
            def scan(q, a, c, j, t, p, width):
                if (j, t, p) == (0, 0, 0):
                    pe.wait_ge(q_in[c], 16 * (q + 1))
                if (t, p) == (0, 0):
                    pe.wait_ge(scan_in[j], 16 * (q + 1))
                if not (isinstance(a, int) and a < RING_A):
                    pe.wait_ge(reduced, a - RING_A + 1)
                slot = piece[0] % RING_A
                piece[0] += 1
                at = (TPC * c + t) * P
                queries = m.q_stack[:, c, j, t * P:(t + 1) * P]
                for o in range(0, width, CH):
                    w = min(CH, width - o)
                    diag = causal and SCAN_KEYS * p + o + w == at + P
                    last = nc.tensor.matmul(ps_scan[:, slot, o:o + w], queries,
                                            m.k_scan[:, j, SCAN_KEYS * p + o:SCAN_KEYS * p + o + w],
                                            start=True, stop=not diag)
                    if diag:
                        last = nc.tensor.matmul(ps_scan[:, slot, o + w - P:o + w], m.ident_bf[:, :],
                                                m.hide_right[:, :], start=False, stop=True)
                last.then_inc(scanned, 1)

            def scores(q, c, kb, j):
                u = unit(c, kb, j)
                if j == 0 and kb == 0:
                    pe.wait_ge(rows_in[c], 64 * (q + 1))
                if j == 0 and kb % TPC == 0:
                    pe.wait_ge(k_in[kb // TPC], 16 * (q + 1))
                pe.wait_ge(exped, units * (q + 1) + previous(u, RING_S) + 1)
                off = max(0, kb - TPC * c) * P if causal else 0
                diag = causal and kb >= TPC * c
                last = nc.tensor.matmul(ps_scores[:, u % RING_S, off:CH], m.k_stack[:, j, kb * P:(kb + 1) * P],
                                        m.q_stack[:, c, j, off:CH], start=True, stop=not diag)
                if diag:
                    last = nc.tensor.matmul(ps_scores[:, u % RING_S, off:off + P], m.ident_bf[:, :],
                                            m.hide_left[:, :], start=False, stop=True)
                last.then_inc(scored, 1)

            def values(q, c, kb):
                if kb == 0:
                    pe.wait_ge(drained, CHUNKS * q + c)
                if kb % TPC == 0:
                    pe.wait_ge(v_in, CHUNKS * q + kb // TPC + 1)
                pe.wait_ge(exped, units * (q + 1) + unit(c, kb, QUAD - 1) + 1)
                off = max(0, kb - TPC * c) * P if causal else 0
                for j in range(QUAD):
                    nc.tensor.matmul(ps_values[32 * j:32 * j + 32, off:CH], m.v_quad[:, kb, j, :],
                                     probs[:, unit(c, kb, j) % RING_P, off:CH],
                                     start=kb == 0, stop=kb == blocks[c] - 1).then_inc(valued, 1)

            def run(q, steps, a):
                for s in steps:
                    if s[0] == "scan":
                        scan(q + 1 if s[6] else q, a, *s[1:6])
                        a = a + 1
                    elif s[0] == "scores":
                        scores(q, *s[1:])
                    elif s[0] == "values":
                        values(q, *s[1:])

            pe.sem_inc(valued, units)
            piece = [0]
            run(0, first, 0)
            with pe.Fori(0, QUADS - 1) as q:
                run(q, order, q * scans + scans_first)
            run(QUADS - 1, order_last, (QUADS - 1) * scans + scans_first)

        @block.scalar
        def _(act):
            act.sem_inc(exped, units)

            def run(q, steps):
                for s in steps:
                    if s[0] == "scores":
                        c, kb, j = s[1:]
                        u = unit(c, kb, j)
                        off = max(0, kb - TPC * c) * P if causal else 0
                        act.wait_ge(scored, units * q + u + 1)
                        act.wait_ge(valued, units * (q + 1) + previous(u, RING_P) + 1)
                        nc.scalar.activation(probs[:, u % RING_P, off:CH], ps_scores[:, u % RING_S, off:CH], ACT.Exp,
                                             scale=SOFTMAX_SCALE).then_inc(exped, 1)

            with act.Fori(0, QUADS - 1) as q:
                run(q, order)
            run(QUADS - 1, order_last)

        @block.vector
        def _(dve):
            nc.vector.memset(negated[:, :], 0.0).then_inc(neg_ready, 1)
            dve.wait_ge(neg_ready, 1)

            def run(q, steps, a, r):
                for s in steps:
                    if s[0] == "scan":
                        c, j, t, p, width = s[1:6]
                        slot = piece[0] % RING_A
                        piece[0] += 1
                        dve.wait_ge(scanned, a + 1)
                        nc.vector.reduce_max(maxima[:, c % 2, TPC * j + t, p:p + 1], ps_scan[:, slot, 0:width],
                                             AXIS_X).then_inc(reduced, 1)
                        a = a + 1
                    elif s[0] == "rows":
                        c, own = s[1], (q + 1 if s[2] else q)
                        dve.wait_ge(reduced, a)
                        n_pieces = -(-(S if not causal else (c + 1) * CH) // SCAN_KEYS)
                        if n_pieces > 1:
                            nc.vector.tensor_reduce(negated[:, 0:QUAD * TPC], maxima[:, c % 2, :, 0:n_pieces], AXIS_X, ALU.max,
                                                    negate=True).then_inc(neg_ready, 1)
                        else:
                            nc.vector.tensor_scalar(negated[:, 0:QUAD * TPC], maxima[:, c % 2, :, 0], -1.0, None,
                                                    ALU.mult).then_inc(neg_ready, 1)
                        dve.wait_ge(neg_ready, r + 2)
                        if c >= 2:
                            dve.wait_ge(rows_in[c - 2], 64 * (own + 1))
                        elif not (isinstance(own, int) and own == 0):
                            dve.wait_ge(rows_in[c + 2], 64 * own)
                        nc.vector.transpose(neg_rows[:, c % 2, :], negated[:, :]).then_inc(neg_turned, 1)
                        dve.wait_ge(neg_turned, r + 1)
                        r = r + 1
                    elif s[0] == "drain":
                        c = s[1]
                        dve.wait_ge(valued, units * (q + 1) + unit(c, blocks[c] - 1, QUAD - 1) + 1)
                        dve.wait_ge(out_done[c % 2], 16 * (2 * q + c // 2))
                        nc.vector.tensor_copy(drained_sb[:, c % 2, :], ps_values[:, :]).then_inc(drained, 1)

            piece = [0]
            ahead = sum(x[0] == "rows" for x in first)
            run(0, first, 0, 0)
            with dve.Fori(0, QUADS - 1) as q:
                run(q, order, q * scans + scans_first, q * CHUNKS + ahead)
            run(QUADS - 1, order_last, (QUADS - 1) * scans + scans_first, (QUADS - 1) * CHUNKS + ahead)

        @block.gpsimd
        def _(pool):
            m.clear_previous(pool)
            def copy_values(q, i):
                nc.gpsimd.tensor_copy(m.v_quad[:, TPC * i:TPC * (i + 1), :, 0:HD],
                                      m.v_all[:, TPC * i:TPC * (i + 1), bass.ds(q * (QUAD * HD), QUAD * HD)]
                                      .rearrange("p k (j d) -> p k j d", d=HD)).then_inc(v_in, 1)

            for i in range(CHUNKS):
                copy_values(0, i)
            if load_experts:
                split_expert_weights(nc, m, pool, raw_weights)
            with pool.Fori(0, QUADS - 1) as q:
                for i in range(CHUNKS):
                    pool.wait_ge(valued, units * (q + 1) + unit(CHUNKS - 1, TPC * i + TPC - 1, QUAD - 1) + 1)
                    copy_values(q + 1, i)

        @block.sync
        def _(sp):
            def load(dst, dram, q, c, sem_):
                at = dst[0:STACK, c, :, :] if dst is m.q_stack else dst[0:STACK, :, cols(c)]
                sp.dma_start(at, dram[:, bass.ds(q * QUAD, QUAD), cols(c)]).then_inc(sem_, 16)

            def load_search_keys(q, j):
                sp.dma_start(m.k_scan[0:STACK, j:j + 1, :], m.k_dram[:, bass.ds(q * QUAD + j, 1), :])\
                    .then_inc(scan_in[j], 16)

            def run(q, steps, a, r, reload):
                for s in steps:
                    if s[0] == "scan":
                        a = a + 1
                        c, j, t, p = s[1:5]
                        if reload and (c, t, p) == (CHUNKS - 1, TPC - 1, S // SCAN_KEYS - 1):
                            sp.wait_ge(scanned, a)
                            load_search_keys(q + 1, j)
                    elif s[0] == "rows":
                        c = s[1]
                        r = r + 1
                        sp.wait_ge(neg_turned, r)
                        rows = m.q_stack[SHIFT_ROW:SHIFT_ROW + 1, c, :, :]\
                            .rearrange("p j (t b k) -> p (j t) b k", t=TPC, k=32)
                        for b in range(4):
                            sp.dma_start(rows[:, :, b, :], neg_rows[32 * b:32 * b + QUAD * TPC, c % 2, :])\
                                .then_inc(rows_in[c], 16)
                    elif s[0] == "scores" and reload and s[3] == QUAD - 1:
                        c, kb = s[1:3]
                        if kb == blocks[c] - 1:
                            sp.wait_ge(scored, units * q + unit(c, kb, QUAD - 1) + 1)
                            load(m.q_stack, m.q_dram, q + 1, c, q_in[c])
                        if c == CHUNKS - 1 and kb % TPC == TPC - 1:
                            sp.wait_ge(scored, units * q + unit(c, kb, QUAD - 1) + 1)
                            load(m.k_stack, m.k_dram, q + 1, kb // TPC, k_in[kb // TPC])
                    elif s[0] == "drain":
                        c = s[1]
                        sp.wait_ge(drained, CHUNKS * q + c + 1)
                        sp.dma_start(m.o_dram[bass.ds(q * QUAD, QUAD), :, cols(c)], drained_sb[:, c % 2, :])\
                            .then_inc(out_done[c % 2], 16)

            for k in range(CHUNKS):
                load(m.q_stack, m.q_dram, 0, k, q_in[k])
                load_search_keys(0, k)
            for c in range(CHUNKS):
                load(m.k_stack, m.k_dram, 0, c, k_in[c])
            ahead = sum(x[0] == "rows" for x in first)
            run(0, first, 0, 0, False)
            with sp.Fori(0, QUADS - 1) as q:
                run(q, order, q * scans + scans_first, q * CHUNKS + ahead, True)
            run(QUADS - 1, order_last, (QUADS - 1) * scans + scans_first, (QUADS - 1) * CHUNKS + ahead, False)
            for half in range(2):
                sp.wait_ge(out_done[half], 16 * QUADS * CHUNKS // 2)


def finish_attention(nc, m, n, layer=None):
    dst = m.x if layer is None else m.z
    with ExitStack() as ctx:
        def sb(name, shape, dt=F32):
            return ctx.enter_context(nc.sbuf_tensor(name + n, shape, dt))

        sem = m.phase_semaphores()

        y = sb("f_y", [P, CHUNKS, CH])
        inverse = sb("f_inverse", [P, CHUNKS, CH])
        sums = sb("f_sums", [P, HEADS * S // P])
        ps = ctx.enter_context(nc.psum_tensor("f_ps" + n, [P, CHUNKS, TPC, D], F32))
        loaded = [sem(f"f_loaded{c}") for c in range(CHUNKS)]
        sums_in, inverted, inverse_out = sem("f_sums_in"), sem("f_inverted"), sem("f_inverse_out")
        y_ready, projected, dve_steps = sem("f_y_ready"), sem("f_projected"), sem("f_dve_steps")
        block = ctx.enter_context(nc.Block())

        @block.gpsimd
        def _(pool):
            m.clear_previous(pool)

        @block.sync
        def _(sp):
            across = HEADS * S // P
            sp.dma_start(sums[:, :], m.o_dram[:, HD, :].rearrange("h (s q) -> h s q", q=across)).then_inc(sums_in, 16)
            for c in range(CHUNKS):
                sp.dma_start(y[:, c, :], m.o_dram[:, 0:HD, c * CH:(c + 1) * CH]).then_inc(loaded[c], 16)
            sp.wait_ge(inverted, 1)
            sp.dma_start(m.r_dram.rearrange("h (s q) -> (h s) q", q=across), sums[:, :]).then_inc(inverse_out, 16)
            sp.wait_ge(inverse_out, 16)
            for c in range(CHUNKS):
                sp.dma_start(inverse[:, c, :], m.r_dram[:, c * CH:(c + 1) * CH].unsqueeze(1)
                             .broadcast_to([HEADS, HD, CH])).then_inc(loaded[c], 16)

        @block.vector
        def _(dve):
            step = Steps(dve, dve_steps)
            dve.wait_ge(sums_in, 16)
            nc.vector.reciprocal(sums[:, :], sums[:, :]).then_inc(inverted, 1)
            if layer is not None:
                step(nc.vector.tensor_tensor(dst[:, :, :], dst[:, :, :], m.bo[:, layer:layer + 1, :]
                                             .broadcast_to([P, TILES, D]), ALU.add))
            for c in range(CHUNKS):
                dve.wait_ge(loaded[c], 32)
                nc.vector.tensor_tensor(y[:, c, :], y[:, c, :], inverse[:, c, :], ALU.mult).then_inc(y_ready, 1)
            for c in range(CHUNKS):
                tiles = dst[:, c * TPC:(c + 1) * TPC, :]
                dve.wait_ge(projected, c + 1)
                step(nc.vector.tensor_tensor(tiles, tiles, ps[:, c, :, :], ALU.add))
                chunk_stats(nc, m, dst, c)

        @block.tensor
        def _(pe):
            right = m.ident[:, :] if layer is None else m.w_att[:, layer, 3, :]
            for c in range(CHUNKS):
                pe.wait_ge(y_ready, c + 1)
                for r in range(TPC):
                    last = nc.tensor.matmul(ps[:, c, r, :], y[:, c, r * P:(r + 1) * P], right, start=True, stop=True)
                last.then_inc(projected, 1)


def top2(nc, step, t, logits, rank):
    full = list(logits.shape)
    v = nc.vector

    def pick(values, onehot, top):
        step(v.tensor_reduce(t[top], values, AXIS_X, ALU.max))
        step(v.tensor_tensor(t["s"], values, t[top].broadcast_to(full), ALU.is_equal))
        step(v.tensor_tensor(t["s"], t["s"], rank.broadcast_to(full), ALU.mult))
        step(v.tensor_reduce(t["r"], t["s"], AXIS_X, ALU.max))
        step(v.tensor_tensor(t[onehot], t["s"], t["r"].broadcast_to(full), ALU.is_equal))

    pick(logits, "h1", "m1")
    step(v.scalar_tensor_tensor(t["l2"], t["h1"], -3e38, logits, ALU.mult, ALU.add))
    pick(t["l2"], "h2", "m2")
    return v.tensor_tensor(t["d"], t["m2"], t["m1"], ALU.subtract)


def top2_combine(nc, step, t, full):
    v = nc.vector
    step(v.tensor_scalar(t["r"], t["ed"], 1.0, None, ALU.add))
    step(v.reciprocal(t["r"], t["r"]))
    step(v.tensor_tensor(t["h2"], t["h2"], t["ed"].broadcast_to(full), ALU.mult))
    step(v.tensor_tensor(t["s"], t["h1"], t["h2"], ALU.add))
    return v.tensor_tensor(t["cw"], t["s"], t["r"].broadcast_to(full), ALU.mult)


COMBINE_STEPS = 4


def router_tiles(nc, ctx, n, parts, groups):
    t = {}
    for name in ("s", "h1", "h2", "l2", "cw", "lg"):
        t[name] = ctx.enter_context(nc.sbuf_tensor(f"t_{name}{n}", [parts, groups, E], F32))[:, :, :]
    for name in ("m1", "m2", "r", "d", "ed"):
        t[name] = ctx.enter_context(nc.sbuf_tensor(f"t_{name}{n}", [parts, groups, 1], F32))[:, :, :]
    return t


def experts(nc, m, n, layer, last, out=None):
    by_token = layer == 0
    n_exp = E if by_token else TOPK
    blocks = n_exp * FB
    ring_h = 4
    turn_at = 6 if by_token else 0
    lag = 3
    with ExitStack() as ctx:
        def sb(name, shape, dt=F32):
            return ctx.enter_context(nc.sbuf_tensor(name + n, shape, dt))

        sem = m.phase_semaphores()

        tmp = sb("e_tmp", [P, 3, TILES])
        hn = m.v_all
        h_hi = sb("e_h_hi", [P, CHUNKS, CH], F32R)
        h_lo = sb("e_h_lo", [P, CHUNKS, CH], F32R)
        hidden = sb("e_hidden", [P, ring_h, CH])
        cw_t = sb("e_cw_t", [E, CH])
        if by_token:
            t = router_tiles(nc, ctx, n, P, TILES)
            cw_now = sb("e_cw_now", [P, TPC, E])
            sum_now, inverse_now = sb("e_sum_now", [P, TPC, E]), sb("e_inverse_now", [P, TPC, 1])
            w1_hi, w1_lo, w2 = m.w1_hi, m.w1_lo, m.w2
        else:
            t = router_tiles(nc, ctx, n, 1, 1)
            w1_hi, w1_lo = sb("e_w1_hi", [P, TOPK, FF], F32R), sb("e_w1_lo", [P, TOPK, FF], F32R)
            w2 = sb("e_w2", [P, TOPK, FB, D])
            raw_w1 = m.v_all[:, 0:TOPK * FB, :].rearrange("p (k b) d -> p k (b d)", k=TOPK)
            b1 = sb("e_b1", [P, TOPK, FB])
            sums = sb("e_sums", [P, CHUNKS])
            mean_h = sb("e_mean_h", [P, 1])
            ids = sb("e_ids", [1, TOPK])
            pair = sb("e_pair", [1, TOPK])
            pair_rows = sb("e_pair_rows", [P, TOPK])
        ps_turn = ctx.enter_context(nc.psum_tensor("e_ps_turn" + n, [P, 2, CH], F32))
        ps_h = ctx.enter_context(nc.psum_tensor("e_ps_h" + n, [P, FB, CH], F32))
        ps_y = ctx.enter_context(nc.psum_tensor("e_ps_y" + n, [P, 2, TPC, D], F32))
        ps_b2 = ps_turn[:, 1, :].rearrange("p (t d) -> p t d", d=D)
        ps_logits = (ps_turn[:, 0, 0:TILES * E] if by_token else ps_y[:, 0, 0, :]).rearrange("p (t e) -> p t e", e=E)
        hn_ready, turned, h_ready, h_split = (sem(s) for s in ("e_hn_ready", "e_turned", "e_h_ready", "e_h_split"))
        logits_ready, top_ready, exp_ready, cw_ready = (sem(s) for s in ("e_logits", "e_top", "e_exp", "e_cw"))
        cw_turned, cwt_ready, b2_ready, b2_added = (sem(s) for s in ("e_cw_turned", "e_cwt", "e_b2_ready",
                                                                     "e_b2_added"))
        up_ready, gelu_ready, down_ready, added = (sem(s) for s in ("e_up", "e_gelu", "e_down", "e_added"))
        dve_steps, weights_in, weights_split = sem("e_dve"), sem("e_weights_in"), sem("e_weights_split")
        mean_ready, pair_ready, pair_spread = sem("e_mean"), sem("e_pair_ready"), sem("e_pair_spread")
        cw_set, h_ready_hi = sem("e_cw_set"), sem("e_h_ready_hi")
        pair_kept = sem("e_pair_kept")
        var_ready, rstd_ready, x_added = sem("e_var_ready"), sem("e_rstd_ready"), sem("e_x_added")
        written = sem("e_written")
        block = ctx.enter_context(nc.Block())
        ln_w = m.vecs[:, LN2_W + layer:LN2_W + layer + 1]
        ln_b = m.vecs[:, LN2_B + layer:LN2_B + layer + 1]
        full = [P, TILES, E]

        @block.gpsimd
        def _(pool):
            m.clear_previous(pool)
            inverse_root(nc, pool, m, m.rstd[:, :], tmp[:, 0, :], var_ready, rstd_ready, 1)

        @block.vector
        def _(dve):
            step = Steps(dve, dve_steps)
            token_stats(nc, step, m, tmp, var_ready, rstd_ready, 1)
            for c in range(CHUNKS):
                for r in range(TPC):
                    i = c * TPC + r
                    last_ = nc.vector.tensor_scalar(hn[:, i, :], m.z[:, i, :], m.mean[:, i:i + 1],
                                                    m.rstd[:, i:i + 1], ALU.subtract, ALU.mult)
                last_.then_inc(hn_ready, 1)
            for c in range(CHUNKS):
                dve.wait_ge(h_ready, c + 1)
                nc.vector.tensor_tensor(h_lo[:, c, :], ps_turn[:, c % 2, :], h_hi[:, c, :].bitcast(F32),
                                        ALU.subtract).then_inc(h_split, 1)
            if by_token:
                dve.wait_ge(logits_ready, 1)
                step(nc.vector.tensor_tensor(t["lg"], ps_logits, m.gate_b[:, layer:layer + 1, :].broadcast_to(full),
                                             ALU.add))
                top2(nc, step, t, t["lg"], m.rank[:, :].unsqueeze(1)).then_inc(top_ready, 1)
                dve.wait_ge(top_ready, 1)
            else:
                step(nc.vector.tensor_reduce(mean_h[:, :], sums[:, :], AXIS_X, ALU.add))
                nc.vector.tensor_scalar(mean_h[:, :], mean_h[:, :], 1.0 / S, None, ALU.mult).then_inc(mean_ready, 1)
                dve.wait_ge(logits_ready, 1)
                step(nc.vector.tensor_tensor(t["lg"], ps_logits[0:1, 0:1, :], m.gate_b[0:1, layer:layer + 1, :],
                                             ALU.add))
                top2(nc, step, t, t["lg"], m.rank[0:1, :].unsqueeze(1)).then_inc(top_ready, 1)
                for k, onehot in enumerate(("h1", "h2")):
                    step(nc.vector.tensor_tensor(t["s"], t[onehot], m.rank[0:1, :].unsqueeze(1), ALU.mult))
                    step(nc.vector.tensor_reduce(ids[:, k:k + 1], t["s"], AXIS_X, ALU.add))
                step(nc.vector.tensor_scalar(ids[:, :], ids[:, :], -1.0, float(E), ALU.mult, ALU.add))
                nc.vector.tensor_copy(m.ids_int[:, :], ids[:, :]).then_inc(cw_set, 1)
                dve.wait_ge(exp_ready, 1)
                step(top2_combine(nc, step, t, [1, 1, E]))
                step(nc.vector.tensor_copy(pair[:, 0:1], t["r"][:, :, 0]))
                nc.vector.tensor_tensor(pair[:, 1:2], t["ed"][:, :, 0], t["r"][:, :, 0], ALU.mult)\
                    .then_inc(pair_ready, 1)
                dve.wait_ge(pair_spread, 1)
                nc.vector.tensor_copy(pair_rows[:, :], ps_y[:, 0, 0, E:E + TOPK]).then_inc(pair_kept, 1)
                dve.wait_ge(pair_kept, 1)
                dve.wait_ge(weights_in, 16 * 3 * TOPK)
                step(nc.vector.tensor_copy(w1_hi[:, :, :], raw_w1))
                nc.vector.tensor_tensor(w1_lo[:, :, :], raw_w1, w1_hi[:, :, :].bitcast(F32), ALU.subtract)\
                    .then_inc(weights_split, 1)

            before = step.n
            with dve.Fori(0, CHUNKS) as i:
                def add_expert(e):
                    dve.wait_ge(down_ready, blocks * i + FB * (e + 1) + ring_h)
                    if e:
                        dve.wait_ge(added, n_exp * i + e)
                    if e == (1 if by_token else 0):
                        dve.wait_ge(b2_added, i + 1)
                    for r in range(TPC):
                        at = bass.ds(i * TPC + r, 1)
                        weight = cw_now[:, r, e:e + 1] if by_token else pair_rows[:, e:e + 1]
                        last_ = nc.vector.scalar_tensor_tensor(m.z[:, at, :], ps_y[:, e % 2, r:r + 1, :], weight,
                                                               m.z[:, at, :], ALU.mult, ALU.add)
                    last_.then_inc(added, 1)

                if by_token:
                    dve.wait_ge(added, n_exp * i)
                    dve.wait_ge(exp_ready, i + 1)
                    step = Steps(dve, dve_steps, i * COMBINE_STEPS + before)
                    now = {name: t[name][:, token_tiles(i), :] for name in ("h1", "h2", "ed")}
                    now.update(r=inverse_now[:, :, :], s=sum_now[:, :, :], cw=cw_now[:, :, :])
                    top2_combine(nc, step, now, [P, TPC, E]).then_inc(cw_set, 1)
                    assert step.n == COMBINE_STEPS
                if by_token:
                    dve.wait_ge(cw_set, i + 1)
                    add_expert(0)
                    dve.wait_ge(added, n_exp * i + 1)
                dve.wait_ge(b2_ready, i + 1)
                nc.vector.tensor_tensor(m.z[:, token_tiles(i), :], m.z[:, token_tiles(i), :], ps_b2, ALU.add)\
                    .then_inc(b2_added, 1)
                for e in range(1 if by_token else 0, n_exp):
                    add_expert(e)
                dve.wait_ge(added, n_exp * (i + 1))
                if last:
                    nc.vector.tensor_tensor(m.x[:, token_tiles(i), :], m.x[:, token_tiles(i), :],
                                            m.z[:, token_tiles(i), :], ALU.add).then_inc(x_added, 1)
                    dve.wait_ge(x_added, i + 1)
                for r in range(TPC):
                    at = bass.ds(i * TPC + r, 1)
                    nc.vector.bn_stats(m.st[:, at, :], (m.x if last else m.z)[:, at, :])

        @block.tensor
        def _(pe):
            def turn(c):
                pe.wait_ge(hn_ready, c + 1)
                if c >= 2:
                    pe.wait_ge(h_split, c - 1)
                for r in range(TPC):
                    last_ = nc.tensor.transpose(ps_turn[:, c % 2, r * P:(r + 1) * P], hn[:, c * TPC + r, :],
                                                m.ident[:, :])
                last_.then_inc(turned, 1)

            def product(out, left, right, start, stop):
                nc.tensor.matmul(out, left[0], right[0], start=start, stop=False, skip_group_check=True)
                nc.tensor.matmul(out, left[1], right[0], start=False, stop=False, skip_group_check=True)
                return nc.tensor.matmul(out, left[0], right[1], start=False, stop=stop, skip_group_check=True)

            pe.sem_inc(down_ready, ring_h)
            for c in range(CHUNKS):
                turn(c)
            pe.wait_ge(h_split, CHUNKS)
            if by_token:
                for i in range(TILES):
                    c, q = i // TPC, slice(i % TPC * P, (i % TPC + 1) * P)
                    last_ = product(ps_logits[:, i, :], (h_hi[:, c, q], h_lo[:, c, q]),
                                    (m.gate_hi[:, layer, :], m.gate_lo[:, layer, :]), True, True)
                last_.then_inc(logits_ready, 1)
                pe.wait_ge(m.weights_split, E)
                pe.wait_ge(m.w2_in, 16)
            else:
                pe.wait_ge(mean_ready, 1)
                nc.tensor.matmul(ps_logits[0:1, 0, :], mean_h[:, :], m.gate_w[:, layer, :], start=True, stop=True)\
                    .then_inc(logits_ready, 1)
                pe.wait_ge(pair_ready, 1)
                nc.tensor.matmul(ps_y[:, 0, 0, E:E + TOPK], m.ones[0:1, :], pair[:, :], start=True, stop=True)\
                    .then_inc(pair_spread, 1)
                for r in range(TPC):
                    last_ = nc.tensor.matmul(ps_turn[0:E, 0, r * P:(r + 1) * P], t["cw"][:, 0, :], m.ones[0:1, :],
                                             start=True, stop=True)
                last_.then_inc(cw_turned, 1)
                pe.wait_ge(pair_kept, 1)
                pe.wait_ge(weights_split, 1)
            with pe.Fori(0, CHUNKS) as i:
                now = (h_hi[:, bass.ds(i, 1), :], h_lo[:, bass.ds(i, 1), :])

                def up(k):
                    e, b = k // FB, k % FB
                    pe.wait_ge(gelu_ready, blocks * i + k + 1)
                    q = slice(b * P, (b + 1) * P)
                    product(ps_h[:, b, :], (w1_hi[:, e, q], w1_lo[:, e, q]), now, True, True).then_inc(up_ready, 1)

                def down(k):
                    e, b = k // FB, k % FB
                    pe.wait_ge(gelu_ready, blocks * i + k + 1 + FB)
                    if b == 0:
                        pe.wait_ge(added, n_exp * i + (e - 1 if e >= 2 else 0))
                    for r in range(TPC):
                        q = slice(r * P, (r + 1) * P)
                        last_ = nc.tensor.matmul(ps_y[:, e % 2, r, :], hidden[:, k % ring_h, q], w2[:, e, b, :],
                                                 start=b == 0 and r == 0, stop=b == FB - 1, skip_group_check=True)
                    last_.then_inc(down_ready, 1)

                for k in range(blocks):
                    up(k)
                    if k == turn_at:
                        if by_token:
                            pe.wait_ge(cw_set, i + 1)
                            for r in range(TPC):
                                last_ = nc.tensor.transpose(ps_turn[0:E, 0, r * P:(r + 1) * P], cw_now[:, r, :],
                                                            m.ident[:, :])
                            last_.then_inc(cw_turned, 1)
                    if k == turn_at + 1:
                        pe.wait_ge(cwt_ready, i + 1 if by_token else 1)
                        pe.wait_ge(b2_added, i)
                        for r in range(TPC):
                            last_ = nc.tensor.matmul(ps_b2[:, r, :], cw_t[:, r * P:(r + 1) * P], m.b2[:, layer, :],
                                                     start=True, stop=True)
                        last_.then_inc(b2_ready, 1)
                    if k >= lag:
                        down(k - lag)
                for k in range(blocks - lag, blocks):
                    down(k)

        @block.scalar
        def _(act):
            for c in range(CHUNKS):
                act.wait_ge(turned, c + 1)
                nc.scalar.activation(h_hi[:, c, :], ps_turn[:, c % 2, :], ACT.Identity, scale=ln_w, bias=ln_b)\
                    .then_inc(h_ready_hi, 1)
                act.wait_ge(h_ready_hi, c + 1)
                nc.scalar.activation(ps_turn[:, c % 2, :], ps_turn[:, c % 2, :], ACT.Identity, scale=ln_w, bias=ln_b,
                                     accum_out=None if by_token else sums[:, c:c + 1]).then_inc(h_ready, 1)
            act.sem_inc(gelu_ready, FB)
            if not by_token:
                act.wait_ge(top_ready, 1)
                nc.scalar.activation(t["ed"], t["d"], ACT.Exp).then_inc(exp_ready, 1)
                act.wait_ge(cw_turned, 1)
                nc.scalar.activation(cw_t[:, :], ps_turn[0:E, 0, :], ACT.Copy).then_inc(cwt_ready, 1)
            with act.Fori(0, CHUNKS) as i:
                for k in range(blocks):
                    e, b = k // FB, k % FB
                    act.wait_ge(up_ready, blocks * i + k + 1)
                    act.wait_ge(down_ready, blocks * i + k + 1)
                    bias = m.vecs[:, E_B1 + k:E_B1 + k + 1] if by_token else b1[:, e, b:b + 1]
                    nc.scalar.activation(hidden[:, k % ring_h, :], ps_h[:, b, :], ACT.Gelu, bias=bias)\
                        .then_inc(gelu_ready, 1)
                    if k == 3 and by_token:
                        act.wait_ge(top_ready, 1)
                        nc.scalar.activation(t["ed"][:, token_tiles(i), :], t["d"][:, token_tiles(i), :], ACT.Exp)\
                            .then_inc(exp_ready, 1)
                    if k == turn_at and by_token:
                        act.wait_ge(cw_turned, i + 1)
                        nc.scalar.activation(cw_t[:, :], ps_turn[0:E, 0, :], ACT.Copy).then_inc(cwt_ready, 1)

        if not by_token:
            @block.sync
            def _(sp):
                sp.wait_ge(cw_set, 1)
                sp.wait_ge(turned, CHUNKS)
                for k in range(TOPK):
                    one = bass.ds(sp.value_load(m.ids_int[0:1, k:k + 1], min_val=0, max_val=E - 1), 1)
                    sp.dma_start(raw_w1[:, k, :], m.ins["L0_ffn_e_w1"][layer, one].rearrange("e p f -> (e p) f"))\
                        .then_inc(weights_in, 16)
                    sp.dma_start(w2[:, k, :, :], m.ins["L0_ffn_e_w2"][layer, one]
                                 .rearrange("e (i p) d -> p (e i) d", p=P)).then_inc(weights_in, 16)
                    sp.dma_start(b1[:, k, :], m.ins["L0_ffn_e_b1"][layer, one].rearrange("e (i p) -> p (e i)", p=P),
                                 allow_slow_non_contiguous=True).then_inc(weights_in, 16)
                sp.wait_ge(weights_in, 16 * 3 * TOPK)
                if out is not None:
                    for c in range(CHUNKS):
                        sp.wait_ge(x_added, c + 1)
                        tiles = slice(c * TPC, (c + 1) * TPC)
                        sp.dma_start(out[0].rearrange("(t p) d -> p t d", p=P)[:, tiles, :], m.x[:, tiles, :])\
                            .then_inc(written, 16)
                    sp.wait_ge(written, 16 * CHUNKS)


def feed_forward(nc, m, n, load_experts=False, out=None):
    for layer in range(LAYERS):
        tag = f"{n}{layer}"
        project_qkv(nc, m, tag, first=layer == 0, layer=layer)
        attention_heads(nc, m, tag, causal=True, load_experts=load_experts and layer == 0)
        finish_attention(nc, m, tag, layer)
        experts(nc, m, tag, layer, last=layer == LAYERS - 1, out=out if layer == LAYERS - 1 else None)


def build(nc, ins, out):
    with ExitStack() as ctx:
        m = Memory(nc, ctx, ins)
        set_up(nc, m, "s")
        stage_a(nc, m, "a")
        feed_forward(nc, m, "f", load_experts=True)
        project_qkv(nc, m, "b", layer=None)
        attention_heads(nc, m, "b", causal=False)
        finish_attention(nc, m, "b")
        feed_forward(nc, m, "g", out=out)


def kernel(**inputs):
    import concourse.bacc as bacc
    from concourse.bass_utils import run_bass_kernel_spmd

    nc = bacc.Bacc("TRN2", target_bir_lowering=False, num_devices=1)
    arrays, ins = {}, {}
    for name, value in inputs.items():
        a = np.ascontiguousarray(value)
        arrays["in_" + name] = a
        ins[name] = nc.dram_tensor("in_" + name, a.shape, mybir.dt.from_np(a.dtype), kind="ExternalInput").ap()
    out = nc.dram_tensor("out", [1, S, D], F32, kind="ExternalOutput").ap()
    build(nc, ins, out)
    result = run_bass_kernel_spmd(nc, [arrays], core_ids=[0])
    return result.results[0]["out"]
```
